# Optimizing a Trainium2 kernel written in Bass

```python
import numpy as np
import jax
import jax.numpy as jnp

def _softmax(x, axis=-1):
    return jax.nn.softmax(x, axis=axis)

def _gelu(x):
    return jax.nn.gelu(x, approximate=True)

def _silu(x):
    return jax.nn.silu(x)

def _sigmoid(x):
    return jax.nn.sigmoid(x)

def _layernorm(x, axis=-1, eps=1e-05):
    m = jnp.mean(x, axis=axis, keepdims=True)
    v = jnp.var(x, axis=axis, keepdims=True)
    return (x - m) / jnp.sqrt(v + eps)

def _scatter_add(tgt, idx, src, axis=0):
    return tgt.at[idx].add(src)

def _segment_sum(src, seg, n):
    return jax.ops.segment_sum(src, seg, n)
kernel_name = 'mk_rec_standalone_d1_rec_r8_e7584c'

def setup_inputs(seed: int=0):
    np.random.seed(seed)
    _w = jnp.asarray

    def _rec_inputs():
        import jax
        import jax.numpy as jnp
        _rk = jax.random.key(seed)
        r_user_idx = jax.random.randint(jax.random.fold_in(_rk, 1), (2048,), 176, 99964, jnp.int32)
        r_context_idx = jnp.stack([jax.random.randint(jax.random.fold_in(jax.random.fold_in(_rk, 2), 0), (2048,), 69, 99837, jnp.int32), jax.random.randint(jax.random.fold_in(jax.random.fold_in(_rk, 2), 1), (2048,), 134, 99935, jnp.int32), jax.random.randint(jax.random.fold_in(jax.random.fold_in(_rk, 2), 2), (2048,), 67, 99938, jnp.int32)], axis=1)
        return (r_user_idx, r_context_idx)
    r_user_idx, r_context_idx = _rec_inputs()

    def _L0_rec_setup():
        import jax, jax.numpy as jnp
        import numpy as np
        NEG_SLOPE = 0.2

        def gat_conv(x, src, dst, W, att_src, att_dst, bias, heads):
            N = x.shape[0]
            Fout = att_src.shape[-1]
            h = (x @ W).reshape(N, heads, Fout)
            a_s = jnp.einsum('nhc,hc->nh', h, att_src)
            a_d = jnp.einsum('nhc,hc->nh', h, att_dst)
            e = jax.nn.leaky_relu(a_s[src] + a_d[dst], NEG_SLOPE)
            m = jax.lax.stop_gradient(jax.ops.segment_max(e, dst, num_segments=N))
            ex = jnp.exp(e - m[dst])
            denom = jax.ops.segment_sum(ex, dst, num_segments=N)
            alpha = ex / (denom[dst] + 1e-16)
            msg = h[src] * alpha[:, :, None]
            out = jax.ops.segment_sum(msg, dst, num_segments=N)
            return out.reshape(N, heads * Fout) + bias
        key = jax.random.key(seed)
        ks = jax.random.split(key, 16)
        NU, NS, D, H, CTX, B, E = (12500, 12500, 64, 2, 3, 512, 200000)
        inp = {'user_idx': jax.random.randint(ks[0], (B,), 0, NU), 'context_idx': jax.random.randint(ks[1], (B, CTX), 0, NS), 'edge_index': jax.random.randint(ks[2], (2, E), 0, NS), 'user_emb': jax.random.normal(ks[3], (NU, D), jnp.float32), 'service_emb': jax.random.normal(ks[4], (NS, D), jnp.float32), 'W1': jax.random.normal(ks[5], (D, H * D), jnp.float32) / np.sqrt(D), 'att_src1': jax.random.normal(ks[6], (H, D), jnp.float32) / np.sqrt(D), 'att_dst1': jax.random.normal(ks[7], (H, D), jnp.float32) / np.sqrt(D), 'b1': jnp.zeros((H * D,), jnp.float32), 'W2': jax.random.normal(ks[8], (H * D, D), jnp.float32) / np.sqrt(H * D), 'att_src2': jax.random.normal(ks[9], (1, D), jnp.float32) / np.sqrt(D), 'att_dst2': jax.random.normal(ks[10], (1, D), jnp.float32) / np.sqrt(D), 'b2': jnp.zeros((D,), jnp.float32), 'fc_w': jax.random.normal(ks[11], (D * (CTX + 1), NS), jnp.float32) / np.sqrt(D * (CTX + 1)), 'fc_b': jnp.zeros((NS,), jnp.float32)}
        return inp
    _L0_rec_all = _L0_rec_setup()
    _L0_rec_in = {k: v for k, v in _L0_rec_all.items() if k in ('edge_index', 'user_emb', 'service_emb', 'W1', 'att_src1', 'att_dst1', 'b1', 'W2', 'att_src2', 'att_dst2', 'b2', 'fc_w', 'fc_b')}
    del _L0_rec_all
    return {'r_user_idx': r_user_idx, 'r_context_idx': r_context_idx, 'L0_rec_edge_index': _L0_rec_in['edge_index'], 'L0_rec_user_emb': _L0_rec_in['user_emb'], 'L0_rec_service_emb': _L0_rec_in['service_emb'], 'L0_rec_W1': _L0_rec_in['W1'], 'L0_rec_att_src1': _L0_rec_in['att_src1'], 'L0_rec_att_dst1': _L0_rec_in['att_dst1'], 'L0_rec_b1': _L0_rec_in['b1'], 'L0_rec_W2': _L0_rec_in['W2'], 'L0_rec_att_src2': _L0_rec_in['att_src2'], 'L0_rec_att_dst2': _L0_rec_in['att_dst2'], 'L0_rec_b2': _L0_rec_in['b2'], 'L0_rec_fc_w': _L0_rec_in['fc_w'], 'L0_rec_fc_b': _L0_rec_in['fc_b']}

def reference(r_user_idx, r_context_idx, L0_rec_edge_index, L0_rec_user_emb, L0_rec_service_emb, L0_rec_W1, L0_rec_att_src1, L0_rec_att_dst1, L0_rec_b1, L0_rec_W2, L0_rec_att_src2, L0_rec_att_dst2, L0_rec_b2, L0_rec_fc_w, L0_rec_fc_b):
    import jax
    import jax.numpy as jnp

    def _L0_rec_ref(user_idx, context_idx, edge_index, user_emb, service_emb, W1, att_src1, att_dst1, b1, W2, att_src2, att_dst2, b2, fc_w, fc_b):
        import jax, jax.numpy as jnp
        import numpy as np
        NEG_SLOPE = 0.2

        def gat_conv(x, src, dst, W, att_src, att_dst, bias, heads):
            N = x.shape[0]
            Fout = att_src.shape[-1]
            h = (x @ W).reshape(N, heads, Fout)
            a_s = jnp.einsum('nhc,hc->nh', h, att_src)
            a_d = jnp.einsum('nhc,hc->nh', h, att_dst)
            e = jax.nn.leaky_relu(a_s[src] + a_d[dst], NEG_SLOPE)
            m = jax.lax.stop_gradient(jax.ops.segment_max(e, dst, num_segments=N))
            ex = jnp.exp(e - m[dst])
            denom = jax.ops.segment_sum(ex, dst, num_segments=N)
            alpha = ex / (denom[dst] + 1e-16)
            msg = h[src] * alpha[:, :, None]
            out = jax.ops.segment_sum(msg, dst, num_segments=N)
            return out.reshape(N, heads * Fout) + bias
        N = service_emb.shape[0]
        loops = jnp.arange(N)
        src = jnp.concatenate([edge_index[0], loops])
        dst = jnp.concatenate([edge_index[1], loops])
        user_vec = user_emb[user_idx]
        g = gat_conv(service_emb, src, dst, W1, att_src1, att_dst1, b1, heads=2)
        g = jax.nn.elu(g)
        g = gat_conv(g, src, dst, W2, att_src2, att_dst2, b2, heads=1)
        ctx = g[context_idx]
        ctx = ctx.reshape(ctx.shape[0], -1)
        x = jnp.concatenate([user_vec, ctx], axis=1)
        return x @ fc_w + fc_b
    y = _L0_rec_ref(r_user_idx, r_context_idx, L0_rec_edge_index, L0_rec_user_emb, L0_rec_service_emb, L0_rec_W1, L0_rec_att_src1, L0_rec_att_dst1, L0_rec_b1, L0_rec_W2, L0_rec_att_src2, L0_rec_att_dst2, L0_rec_b2, L0_rec_fc_w, L0_rec_fc_b)
    return y

_drawn_inputs = setup_inputs


def setup_inputs(seed=0):
    import zlib

    import numpy as np

    out = dict(_drawn_inputs(seed))
    spreads = {'L0_rec_b1': (0.0, 0.1), 'L0_rec_b2': (0.0, 0.1), 'L0_rec_fc_b': (0.0, 0.1)}
    factors = {'L0_rec_att_src2': 3.345, 'L0_rec_att_dst2': 5.722}
    for name, (base, spread) in spreads.items():
        noise = np.random.default_rng([zlib.crc32(name.encode()), seed]).standard_normal(out[name].shape)
        drawn = base * np.exp(spread * noise) if base else spread * noise
        out[name] = jnp.asarray(drawn.astype(out[name].dtype))
    for name, factor in factors.items():
        out[name] = (out[name] * factor).astype(out[name].dtype)
    return out
```

```python
from contextlib import ExitStack

import numpy as np

import concourse.bass as bass
from concourse import mybir

F32 = mybir.dt.float32
I32 = mybir.dt.int32
BF16 = mybir.dt.bfloat16
ALU = mybir.AluOpType
ACT = mybir.ActivationFunctionType
AX = mybir.AxisListType

P = 128
NODES = 12500
EDGES = 200000
D = 64
HEADS1, HEADS2 = 2, 1
BATCH = 2048
CTX = 3
SLOPE = 0.2
EPS = 1e-16
NEG = -1e30

FIELD_BITS = 14
FIELD = (1 << FIELD_BITS) - 1
TAG = 1 << (2 * FIELD_BITS)
DUMMY = NODES << FIELD_BITS | TAG | 1
COLS = 2048
COL_BITS, PART_BITS = 11, 7
IN_PARTS = 125

ROWS = 64
GROUPS = 2 * (-(-(EDGES + NODES) // (P * ROWS * 2)))
TILES = GROUPS * ROWS
CHUNK = 4
CHUNKS = -(-(NODES + P) // (CHUNK * P))
WIDTH = CHUNKS * CHUNK * P
REG_BATCH = 16
SLOTS = 4

LOADS = D + 1
ROW1 = LOADS + 2 * HEADS1
ROW2 = LOADS + 2 * HEADS2


class Mem:

    def __init__(self, nc, stack, stage):
        self.nc, self.stack, self.stage = nc, stack, stage

    def sbuf(self, name, shape, dtype=F32):
        return self.stack.enter_context(self.nc.sbuf_tensor(f"{self.stage}_{name}", shape, dtype))

    def psum(self, name, shape, dtype=F32):
        return self.stack.enter_context(self.nc.psum_tensor(f"{self.stage}_{name}", shape, dtype))

    def sem(self, name):
        return self.stack.enter_context(self.nc.semaphore(f"{self.stage}_{name}"))


class Steps:

    def __init__(self, eng, sem, base=0):
        self.eng, self.sem, self.base, self.n = eng, sem, base, 0

    def did(self, ins):
        ins.then_inc(self.sem, 1)
        self.n += 1
        return self.n

    def settle(self, n=None):
        self.eng.wait_ge(self.sem, self.base + (self.n if n is None else n))

    def then(self, ins):
        self.did(ins)
        self.settle()


def as_float(bits):
    return float(np.array(bits, np.int32).view(np.float32))


def weights_and_sort(nc, dram, keep):
    with ExitStack() as stack:
        m = Mem(nc, stack, "sort")
        key_a = m.sbuf("key_a", [P, COLS])
        key_b = m.sbuf("key_b", [P, COLS])
        src = m.sbuf("src", [IN_PARTS, EDGES // IN_PARTS], I32)
        dst = m.sbuf("dst", [IN_PARTS, EDGES // IN_PARTS], I32)
        upper = m.sbuf("upper", [P, COLS // 2])
        part = m.sbuf("part", [P, 1], I32)
        bit = m.sbuf("bit", [P, PART_BITS], I32)
        sign = m.sbuf("sign", [P, PART_BITS])
        turn = m.sbuf("turn", [P, PART_BITS + 1])
        per = NODES // IN_PARTS
        table = m.sbuf("table", [IN_PARTS, per, ROW1])
        prod = m.sbuf("prod", [IN_PARTS, per, D])
        w1 = m.sbuf("w1", [D, HEADS1 * D])
        w1t = m.sbuf("w1t", [P, D])
        att1 = m.sbuf("att1", [P, 2 * HEADS1])
        att1_wide = m.sbuf("att1_wide", [P, 2 * HEADS1, P])
        score_w = m.sbuf("score_w", [P, 2 * HEADS1, D])
        w2t = m.sbuf("w2t", [D, P])
        att2 = m.sbuf("att2", [D, 2])
        turned = m.psum("turned", [P, COLS])
        ps_w1t = m.psum("ps_w1t", [P, 512])
        ps_w2t = m.psum("ps_w2t", [P, 512])
        ps_score = m.psum("ps_score", [P, 512])
        ident = keep["ident"]

        edges_in = m.sem("edges_in")
        nodes_in = m.sem("nodes_in")
        weights_in = m.sem("weights_in")
        keys_filled = m.sem("keys_filled")
        consts = m.sem("consts")
        zeroed = m.sem("zeroed")
        step = m.sem("step")
        flipped = m.sem("flipped")
        before_turn = m.sem("before_turn")
        after_turn = m.sem("after_turn")
        upper_ready = m.sem("upper_ready")
        prepared = m.sem("prepared")
        wide = m.sem("wide")
        score_ready = m.sem("score_ready")
        pool_step = m.sem("pool_step")
        table_ready = m.sem("table_ready")
        sorted_keys = m.sem("sorted_keys")
        stored = m.sem("stored")
        block = stack.enter_context(nc.Block())

        @block.sync
        def _(sp):
            sp.dma_start(dst[:, :], dram["edges"][1].rearrange("(p c) -> p c", p=IN_PARTS)).then_inc(edges_in, 16)
            sp.dma_start(src[:, :], dram["edges"][0].rearrange("(p c) -> p c", p=IN_PARTS)).then_inc(edges_in, 16)
            sp.dma_start(w1[:, :], dram["W1"]).then_inc(weights_in, 16)
            sp.dma_start(keep["w2ext"][:, 0:D], dram["W2"]).then_inc(weights_in, 16)
            sp.dma_start(keep["b1"][:, :], dram["b1"].rearrange("(c o) -> c o", o=1)).then_inc(weights_in, 16)
            sp.dma_start(keep["b2"][:, :], dram["b2"].rearrange("(o c) -> o c", o=1).to_broadcast([P, D])
                         ).then_inc(weights_in, 16)
            sp.dma_start(att2[:, 0:1], dram["att_src2"].rearrange("h d -> d h")).then_inc(weights_in, 16)
            sp.dma_start(att2[:, 1:2], dram["att_dst2"].rearrange("h d -> d h")).then_inc(weights_in, 16)
            sp.wait_ge(zeroed, 1)
            for h in range(HEADS1):
                own = slice(h * D, (h + 1) * D)
                sp.dma_start(att1[own, h:h + 1], dram["att_src1"][h:h + 1].rearrange("h d -> d h")
                             ).then_inc(weights_in, 16)
                sp.dma_start(att1[own, HEADS1 + h:HEADS1 + h + 1],
                             dram["att_dst1"][h:h + 1].rearrange("h d -> d h")).then_inc(weights_in, 16)
                sp.dma_start(keep["w1z"][0:D, h, own], dram["W1"][:, own]).then_inc(weights_in, 16)
            sp.dma_start(table[:, :, 0:D], dram["service"].rearrange("(p c) d -> p c d", p=IN_PARTS)
                         ).then_inc(nodes_in, 16)
            sp.wait_ge(table_ready, 1)
            sp.dma_start(dram["table1"].rearrange("(p c) d -> p c d", p=IN_PARTS), table[:, :, :]
                         ).then_inc(stored, 16)
            sp.wait_ge(sorted_keys, 1)
            sp.dma_start(dram["keys"][1:1 + P * COLS].rearrange("(p c) -> p c", p=P), key_a[:, :].bitcast(I32)
                         ).then_inc(stored, 16)
            sp.dma_start(dram["keys"][0:1].rearrange("(p c) -> p c", p=1), key_a[P - 1:P, COLS - 1:COLS].bitcast(I32)
                         ).then_inc(stored, 16)
            sp.wait_ge(stored, 48)

        @block.gpsimd
        def _(pool):
            g = nc.gpsimd
            mine = Steps(pool, pool_step)
            mine.then(g.memset(key_a[:, :], as_float(DUMMY)))
            loops = key_a[0:IN_PARTS, EDGES // IN_PARTS:EDGES // IN_PARTS + per].bitcast(I32)
            g.iota(loops, [[1, per]], base=0, channel_multiplier=per).then_inc(keys_filled, 1)
            g.iota(part[:, :], [[0, 1]], base=0, channel_multiplier=1).then_inc(consts, 1)
            mine.then(g.memset(att1[:, :], 0.0))
            mine.then(g.memset(keep["w2ext"][:, D:D + 1], 0.0))
            mine.then(g.memset(keep["sel"][:, :, :], 0.0))
            mine.then(g.memset(keep["w1z"][:, :, :], 0.0))
            pool.sem_inc(zeroed, 1)
            for h in range(HEADS1):
                mine.then(g.memset(keep["sel"][D:D + 1, h, h * D:(h + 1) * D], 1.0))
            mine.then(g.memset(keep["ones"][:, :], 1.0))
            mine.then(g.memset(ident[:, :], 0.0))
            mine.then(g.affine_select(out=ident[:, :], in_=ident[:, :], compare_op=ALU.not_equal, fill=1.0,
                                      base=0, pattern=[[-1, P]], channel_multiplier=1))
            pool.sem_inc(consts, 1)
            mine.then(g.iota(keep["lane"][:, :], [[1, P]], base=0, channel_multiplier=0,
                             allow_small_or_imprecise_dtypes=True))
            pool.wait_ge(weights_in, 16 * (6 + 3 * HEADS1))
            mine.then(g.tensor_copy(att1_wide[:, :, :],
                                    att1[:, :].unsqueeze(2).to_broadcast([P, 2 * HEADS1, P])))
            pool.sem_inc(wide, 1)
            pool.wait_ge(nodes_in, 16)
            pool.wait_ge(score_ready, 1)
            mine.then(g.memset(table[:, :, D:D + 1], 1.0))
            for c in range(2 * HEADS1):
                w = score_w[0:IN_PARTS, c:c + 1, :].to_broadcast([IN_PARTS, per, D])
                mine.then(g.tensor_tensor(prod[:, :, :], table[:, :, 0:D], w, ALU.mult))
                half = D
                while half > 1:
                    half //= 2
                    to = prod[:, :, 0:half] if half > 1 else table[:, :, LOADS + c:LOADS + c + 1]
                    mine.then(g.tensor_tensor(to, prod[:, :, 0:half], prod[:, :, half:2 * half], ALU.add))
            pool.sem_inc(table_ready, 1)

        @block.scalar
        def _(act):
            act.wait_ge(prepared, 2)
            nc.scalar.copy(w1t[:, :], ps_w1t[:, 0:D]).then_inc(prepared, 1)
            nc.scalar.copy(w2t[:, :], ps_w2t[0:D, 0:P]).then_inc(prepared, 1)
            act.wait_ge(prepared, 5)
            nc.scalar.copy(keep["w2ext"][:, LOADS:ROW2], ps_w2t[:, 256:258])
            nc.scalar.copy(score_w[:, :, :], ps_score[:, 0:2 * HEADS1 * D].rearrange(
                "p (c d) -> p c d", d=D)).then_inc(score_ready, 1)
            for n in range(1, PART_BITS + 1):
                for way, dist in enumerate((1 << (n - 1), COLS // 2)):
                    act.wait_ge(after_turn, 2 * n - 1 + way)
                    nc.scalar.copy(upper[:, :].rearrange("p (m d) -> p m d", d=dist),
                                   turned[:, :].rearrange("p (m t d) -> p m t d", t=2, d=dist)[:, :, 1, :]
                                   ).then_inc(upper_ready, 1)

        @block.tensor
        def _(pe):
            pe.wait_ge(consts, 2)
            pe.wait_ge(weights_in, 16 * (6 + 3 * HEADS1))
            nc.tensor.transpose(ps_w1t[:, 0:D], w1[:, :], ident[0:D, 0:D]).then_inc(prepared, 1)
            nc.tensor.transpose(ps_w2t[0:D, 0:P], keep["w2ext"][:, 0:D], ident[:, :]).then_inc(prepared, 1)
            pe.wait_ge(prepared, 4)
            pe.wait_ge(wide, 1)
            for c in range(2 * HEADS1):
                nc.tensor.matmul(ps_score[:, c * D:(c + 1) * D], att1_wide[:, c, :], w1t[:, :],
                                 start=True, stop=True)
            nc.tensor.matmul(ps_w2t[:, 256:258], w2t[:, :], att2[:, :], start=True, stop=True
                             ).then_inc(prepared, 1)
            chunks = COLS // P
            for n in range(PART_BITS):
                for way in range(2):
                    pe.wait_ge(before_turn, 2 * n + way + 1)
                    for c in range(chunks):
                        if way == 0:
                            out, inp = turned[:, c * P:(c + 1) * P], key_a[:, c * P:(c + 1) * P]
                        else:
                            out, inp = turned[:, c * P:(c + 1) * P], key_b[:, c * P:(c + 1) * P]
                        last = nc.tensor.transpose(out, inp, ident[:, :])
                    last.then_inc(after_turn, 1)

        @block.vector
        def _(dve):
            v = nc.vector
            mine = Steps(dve, step)
            edge_cols = slice(0, EDGES // IN_PARTS)
            loop_cols = slice(EDGES // IN_PARTS, EDGES // IN_PARTS + per)
            bits_a = key_a[0:IN_PARTS, :].bitcast(I32)
            dve.wait_ge(keys_filled, 1)
            dve.wait_ge(consts, 1)
            mine.did(v.tensor_scalar(bits_a[:, loop_cols], bits_a[:, loop_cols], FIELD_BITS, TAG,
                                     ALU.logical_shift_left, ALU.bitwise_or))
            dve.wait_ge(edges_in, 32)
            mine.did(v.tensor_scalar(dst[:, :], dst[:, :], FIELD_BITS, TAG,
                                     ALU.logical_shift_left, ALU.bitwise_or))
            mine.did(v.tensor_scalar(src[:, :], src[:, :], 1.0, None, ALU.add))
            for b in range(PART_BITS):
                mine.did(v.tensor_scalar(bit[:, b:b + 1], part[:, :], b, 1,
                                         ALU.logical_shift_right, ALU.bitwise_and))
            mine.settle()
            mine.did(v.tensor_tensor(bits_a[:, edge_cols], dst[:, :], src[:, :], ALU.bitwise_or))
            mine.then(v.tensor_scalar(sign[:, :], bit[:, :], -2.0, 1.0, ALU.mult, ALU.add))
            mine.did(v.tensor_copy(turn[:, 0:1], sign[:, 0:1]))
            mine.did(v.tensor_tensor(turn[:, 1:PART_BITS], sign[:, 1:PART_BITS], sign[:, 0:PART_BITS - 1],
                                     ALU.mult))
            mine.then(v.tensor_copy(turn[:, PART_BITS:PART_BITS + 1], sign[:, PART_BITS - 1:PART_BITS]))

            def exchange(to, of, dist):
                a, b = (x.rearrange("p (m t d) -> p m t d", t=2, d=dist) for x in (of[:, :], to[:, :]))
                low, high = a[:, :, 0, :], a[:, :, 1, :]
                if of is turned:
                    high = upper[:, :].rearrange("p (m d) -> p m d", d=dist)
                mine.did(v.tensor_tensor(b[:, :, 0, :], low, high, ALU.min))
                mine.did(v.tensor_tensor(b[:, :, 1, :], low, high, ALU.max))
                mine.settle()

            at, other = key_a, key_b
            for k in range(1, COL_BITS):
                for j in reversed(range(k)):
                    views = [x[:, :].rearrange("p (n w m t d) -> p n w m t d", w=2, m=1 << (k - 1 - j),
                                               t=2, d=1 << j) for x in (at, other)]
                    for way in range(2):
                        a, b = (x[:, :, way] for x in views)
                        for t, op in ((0, ALU.min), (1, ALU.max)):
                            mine.did(v.tensor_tensor(b[:, :, :, t ^ way, :], a[:, :, :, 0, :],
                                                     a[:, :, :, 1, :], op))
                    mine.settle()
                    at, other = other, at
            for k in range(COL_BITS, COL_BITS + PART_BITS + 1):
                n = k - COL_BITS
                mine.then(v.tensor_scalar(key_a[:, :], at[:, :], turn[:, n:n + 1], None, ALU.mult))
                at, other = key_a, key_b
                if n:
                    dve.sem_inc(before_turn, 1)
                    dve.wait_ge(upper_ready, 2 * n - 1)
                    of = turned
                    for j in reversed(range(n)):
                        to = key_b if (j % 2 == 0) else key_a
                        exchange(to, of, 1 << j)
                        of = to
                    dve.sem_inc(before_turn, 1)
                    dve.wait_ge(upper_ready, 2 * n)
                    at = turned
                for j in reversed(range(COL_BITS)):
                    to = key_a if (at is not key_a) else key_b
                    exchange(to, at, 1 << j)
                    at = to
            assert at is key_a
            dve.sem_inc(sorted_keys, 1)


def index_tiles(nc, dram, keep):
    with ExitStack() as stack:
        m = Mem(nc, stack, "index")
        keys = m.sbuf("keys", [ROWS, GROUPS, P + 2], I32)
        node = m.sbuf("node", [ROWS, GROUPS, P + 2])
        field = m.sbuf("field", [ROWS, GROUPS, P])
        loop = m.sbuf("loop", [ROWS, GROUPS, P])
        row = m.sbuf("row", [ROWS, GROUPS, P])
        first = m.sbuf("first", [GROUPS, ROWS], I32)
        turned = m.psum("turned", [P, 2, 2, ROWS])
        turned_first = m.psum("turned_first", [P, 512])

        keys_in = m.sem("keys_in")
        step = m.sem("step")
        rows_ready = m.sem("rows_ready")
        turned_row = m.sem("turned_row")
        copied = m.sem("copied")
        nodes_ready = m.sem("nodes_ready")
        turned_nodes = m.sem("turned_nodes")
        first_ready = m.sem("first_ready")
        window_out = m.sem("window_out")
        window_in = m.sem("window_in")
        block = stack.enter_context(nc.Block())
        group = ROWS * P

        @block.sync
        def _(sp):
            t = dram["keys"].tensor
            for half in range(2):
                n = GROUPS // 2
                sp.dma_start(keys[:, half * n:(half + 1) * n, :],
                             bass.AP(tensor=t, offset=half * n * group, ap=[[P, ROWS], [group, n], [1, P + 2]])
                             ).then_inc(keys_in, 16)
            sp.wait_ge(first_ready, 1)
            sp.dma_start(dram["window"].rearrange("(b r) -> b r", r=ROWS), first[:, :]).then_inc(window_out, 16)
            sp.wait_ge(window_out, 16)
            sp.dma_start(keep["window"][:, :], dram["window"].rearrange("(o c) -> o c", o=1)
                         ).then_inc(window_in, 16)
            sp.wait_ge(window_in, 16)

        @block.vector
        def _(dve):
            v = nc.vector
            mine = Steps(dve, step)
            dve.wait_ge(keys_in, 32)
            mine.then(v.tensor_scalar(field[:, :, :].bitcast(I32), keys[:, :, 1:P + 1], FIELD, None,
                                      ALU.bitwise_and))
            mine.then(v.tensor_scalar(keys[:, :, :], keys[:, :, :], FIELD_BITS, FIELD,
                                      ALU.logical_shift_right, ALU.bitwise_and))
            mine.did(v.tensor_copy(node[:, :, :], keys[:, :, :]))
            mine.then(v.tensor_copy(row[:, :, :], field[:, :, :].bitcast(I32)))
            dve.sem_inc(nodes_ready, 1)
            own = node[:, :, 1:P + 1]
            mine.did(v.tensor_tensor(keep["starts"][:, :, :], own, node[:, :, 0:P], ALU.not_equal))
            mine.did(v.tensor_tensor(keep["ends"][:, :, ::-1], own, node[:, :, 2:P + 2], ALU.not_equal))
            mine.then(v.tensor_scalar(loop[:, :, :], row[:, :, :], 0.0, None, ALU.is_equal))
            mine.did(v.tensor_scalar(keep["starts"][:, :, :], keep["starts"][:, :, :], NEG, None, ALU.mult))
            mine.did(v.tensor_scalar(keep["ends"][:, :, :], keep["ends"][:, :, :], NEG, None, ALU.mult))
            mine.did(v.tensor_scalar(keep["others"][:, :, :], loop[:, :, :], -NEG, NEG, ALU.mult, ALU.add))
            mine.did(v.scalar_tensor_tensor(out=field[:, :, :], in0=own, scalar=1.0, in1=loop[:, :, :],
                                            op0=ALU.add, op1=ALU.mult))
            mine.settle()
            mine.did(v.scalar_tensor_tensor(out=row[:, :, :], in0=row[:, :, :], scalar=-1.0,
                                            in1=field[:, :, :], op0=ALU.add, op1=ALU.add))
            mine.then(v.tensor_tensor(loop[:, :, :], own, node[:, :, 1:2].to_broadcast([ROWS, GROUPS, P]),
                                      ALU.subtract))
            dve.sem_inc(rows_ready, 1)
            dve.wait_ge(turned_nodes, 1)
            v.tensor_copy(first[:, :], turned_first[0:GROUPS, 0:ROWS]).then_inc(first_ready, 1)
            for n in range(GROUPS // 2):
                dve.wait_ge(turned_row, n + 1)
                to = slice(2 * n * ROWS, 2 * (n + 1) * ROWS)
                v.tensor_copy(keep["rows"][:, to].rearrange("p (b r) -> p b r", b=2), turned[:, 0])
                v.tensor_copy(keep["places"][:, to].rearrange("p (b r) -> p b r", b=2),
                              turned[:, 1]).then_inc(copied, 1)

        @block.tensor
        def _(pe):
            pe.wait_ge(nodes_ready, 1)
            nc.tensor.transpose(turned_first[0:GROUPS, 0:ROWS], node[:, :, 1], keep["ident"][0:ROWS, 0:ROWS]
                                ).then_inc(turned_nodes, 1)
            pe.wait_ge(rows_ready, 1)
            for n in range(GROUPS // 2):
                if n:
                    pe.wait_ge(copied, n)
                for what, of in enumerate((row, loop)):
                    for b in range(2):
                        last = nc.tensor.transpose(turned[:, what, b], of[:, 2 * n + b, :],
                                                   keep["ident"][0:ROWS, 0:ROWS])
                last.then_inc(turned_row, 1)


def wait_alone(eng, sem, value, passed):
    eng.wait_ge(sem, value)
    eng.sem_inc(passed, 1)


def sum_messages(nc, table, keep, acc, heads, stage):
    with ExitStack() as stack:
        m = Mem(nc, stack, stage)
        both = 2 * heads
        width = LOADS + both
        fetched = m.sbuf("fetched", [P, 2 * ROWS, width])
        rows_now = m.sbuf("rows_now", [P, 2 * ROWS], I32)
        places_now = m.sbuf("places_now", [P, ROWS])
        weights_now = m.sbuf("weights_now", [P, heads, ROWS])
        onehot = m.sbuf("onehot", [P, SLOTS, heads, P])
        own_loop = m.sbuf("own_loop", [ROWS, heads, P])
        first = m.sbuf("first", [ROWS, P])
        last = m.sbuf("last", [ROWS, P])
        forth = m.sbuf("forth", [ROWS, both, P])
        back = m.sbuf("back", [ROWS, heads, P])
        tails = m.sbuf("tails", [ROWS, 6 * heads])
        tails_forth = m.sbuf("tails_forth", [both, 2 * ROWS])
        tails_back = m.sbuf("tails_back", [heads, 2 * ROWS])
        carry = m.sbuf("carry", [both, ROWS + 1])
        carry_back = m.sbuf("carry_back", [heads, ROWS + 1])
        carried = m.sbuf("carried", [ROWS, 3 * heads])
        top = m.sbuf("top", [ROWS, heads, P])
        dst_score = m.sbuf("dst_score", [ROWS, heads, P])
        z = m.sbuf("z", [ROWS, heads, P])
        weight = m.sbuf("weight", [ROWS, heads, P])
        old = m.sbuf("old", [1, heads])
        factor = m.sbuf("factor", [1, heads])
        ps_scores = m.psum("ps_scores", [ROWS, both, P])
        ps_small = m.psum("ps_small", [P, 512])
        ps_weights = m.psum("ps_weights", [P, 512])
        ps_sum = [m.psum(f"ps_sum{s}", [P, 512]) for s in range(SLOTS)]
        turned_weights = ps_weights[:, 0:heads * ROWS].rearrange("p (h r) -> p h r", h=heads)
        turned_tails = [ps_small[0:n, c * ROWS:(c + 1) * ROWS]
                        for c, n in enumerate((both, both, heads, heads))]
        turned_carry = ps_small[0:ROWS, 4 * ROWS:4 * ROWS + 3 * heads]
        ps_factor = ps_small[0:LOADS, 5 * ROWS:5 * ROWS + heads]

        landed = [m.sem("landed_even"), m.sem("landed_odd")]
        rows_copied = m.sem("rows_copied")
        scores_turned = m.sem("scores_turned")
        tails_ready = m.sem("tails_ready")
        tails_turned = m.sem("tails_turned")
        carry_ready = m.sem("carry_ready")
        carry_turned = m.sem("carry_turned")
        exponents_ready = m.sem("exponents_ready")
        weights_ready = m.sem("weights_ready")
        weights_turned = m.sem("weights_turned")
        weights_copied = m.sem("weights_copied")
        step = m.sem("step")
        pe_passed = m.sem("pe_passed")
        pool_passed = m.sem("pool_passed")
        onehot_ready = m.sem("onehot_ready")
        summed = m.sem("summed")
        added = m.sem("added")
        block = stack.enter_context(nc.Block())

        @block.gpsimd
        def _(pool):
            with pool.Fori(0, GROUPS // 2) as i:
                for half in range(2):
                    pool.wait_ge(summed, (2 * i + half + 1) * ROWS)
                    nc.gpsimd.tensor_copy(rows_now[:, half * ROWS:(half + 1) * ROWS],
                                          keep["rows"][:, bass.ds((2 * i + half) * ROWS, ROWS)]
                                          ).then_inc(rows_copied, 1)
                    wait_alone(pool, rows_copied, 2 * i + half + 1, pool_passed)
                    for r in range(half * ROWS, (half + 1) * ROWS):
                        nc.gpsimd.indirect_dma_start(
                            fetched[:, r, :], None, table,
                            bass.IndirectOffsetOnAxis(ap=rows_now[:, r:r + 1], axis=0)).then_inc(landed[half], 16)

        @block.tensor
        def _(pe):
            ident = keep["ident"]
            pe.sem_inc(summed, 2 * ROWS)
            with pe.Fori(0, GROUPS // 2) as i:
                for half in range(2):
                    group = 2 * i + half
                    wait_alone(pe, landed[half], (i + 1) * (16 * ROWS), pe_passed)
                    tiles = slice(half * ROWS, (half + 1) * ROWS)
                    for c in range(both):
                        t = nc.tensor.transpose(ps_scores[:, c, :], fetched[:, tiles, LOADS + c], ident[:, :])
                    t.then_inc(scores_turned, 1)
                    wait_alone(pe, tails_ready, group + 1, pe_passed)
                    c = 0
                    for to, n in zip(turned_tails, (both, both, heads, heads)):
                        t = nc.tensor.transpose(to, tails[:, c:c + n], ident[0:ROWS, 0:ROWS])
                        c += n
                    t.then_inc(tails_turned, 1)
                    wait_alone(pe, carry_ready, group + 1, pe_passed)
                    nc.tensor.transpose(turned_carry[:, 0:both], carry[:, 0:ROWS], ident[0:both, 0:both])
                    nc.tensor.transpose(turned_carry[:, both:3 * heads], carry_back[:, 1:ROWS + 1],
                                        ident[0:heads, 0:heads]).then_inc(carry_turned, 1)
                    wait_alone(pe, weights_ready, group + 1, pe_passed)
                    for h in range(heads):
                        nc.tensor.transpose(turned_weights[:, h, :], weight[:, h, :], ident[0:ROWS, 0:ROWS])
                    nc.tensor.matmul(ps_factor, keep["ones"][0:1, 0:LOADS], factor[:, :], start=True, stop=True
                                     ).then_inc(weights_turned, 1)
                    for r in range(ROWS):
                        pe.wait_ge(onehot_ready, group * ROWS + (r + 1))
                        pe.wait_ge(added, group * ROWS + (r + 1))
                        nc.tensor.matmul(ps_sum[r % SLOTS][0:LOADS, 0:heads * P],
                                         fetched[:, half * ROWS + r, 0:LOADS],
                                         onehot[:, r % SLOTS].rearrange("p h c -> p (h c)"),
                                         start=True, stop=True).then_inc(summed, 1)

        @block.scalar
        def _(act):
            with act.Fori(0, GROUPS) as group:
                act.wait_ge(exponents_ready, group + 1)
                nc.scalar.activation(factor[:, :], old[:, :], ACT.Exp)
                nc.scalar.activation(weight[:, :, :], z[:, :, :], ACT.Exp).then_inc(weights_ready, 1)
                nc.scalar.copy(places_now[:, :], keep["places"][:, bass.ds(group * ROWS, ROWS)])
                act.wait_ge(weights_turned, group + 1)
                nc.scalar.copy(weights_now[:, :, :], turned_weights).then_inc(weights_copied, 1)

        @block.vector
        def _(dve):
            v = nc.vector
            v.memset(carry[:, :], NEG)
            v.memset(carry_back[:, :], NEG)
            v.memset(acc[:, :, :], 0.0).then_inc(added, SLOTS)
            dve.wait_ge(added, SLOTS)
            steps = 24 + 6 * heads
            with dve.Fori(0, GROUPS) as group:
                mine = Steps(dve, step, group * steps)
                starts, ends, others = (keep[x][:, bass.ds(group, 1), :].rearrange("r o e -> r (o e)")
                                        for x in ("starts", "ends", "others"))
                dve.wait_ge(scores_turned, group + 1)
                src_scores = ps_scores[:, 0:heads, :]
                mine.did(v.tensor_tensor(own_loop[:, :, :], ps_scores[:, heads:both, :],
                                         keep["others"][:, bass.ds(group, 1), :].to_broadcast([ROWS, heads, P]),
                                         ALU.add))
                mine.did(v.tensor_tensor_scan(first[:, :], starts, starts, 0.0, ALU.min, ALU.min))
                mine.did(v.tensor_tensor_scan(last[:, ::-1], ends, ends, 0.0, ALU.min, ALU.min))
                for h in range(heads):
                    mine.did(v.tensor_tensor_scan(forth[:, h, :], starts, ps_scores[:, h, :], NEG, ALU.add, ALU.max))
                    mine.did(v.tensor_tensor_scan(back[:, h, ::-1], ends, ps_scores[:, h, ::-1], NEG,
                                                  ALU.add, ALU.max))
                mine.settle()
                for h in range(heads):
                    mine.did(v.tensor_tensor_scan(forth[:, heads + h, :], starts, own_loop[:, h, :], NEG,
                                                  ALU.add, ALU.max))
                mine.settle()
                mine.did(v.tensor_copy(tails[:, 0:both], forth[:, :, P - 1]))
                mine.did(v.tensor_copy(tails[:, both:2 * both], first[:, P - 1:P].to_broadcast([ROWS, both])))
                mine.did(v.tensor_copy(tails[:, 2 * both:2 * both + heads], back[:, :, 0]))
                mine.did(v.tensor_copy(tails[:, 2 * both + heads:3 * both], last[:, 0:1].to_broadcast([ROWS, heads])))
                mine.settle()
                dve.sem_inc(tails_ready, 1)
                dve.wait_ge(tails_turned, group + 1)
                mine.did(v.tensor_copy(tails_forth[:, :], ps_small[0:both, 0:2 * ROWS]))
                mine.did(v.tensor_copy(tails_back[:, :], ps_small[0:heads, 2 * ROWS:4 * ROWS]))
                mine.settle()
                mine.did(v.tensor_tensor_scan(carry[:, 1:ROWS + 1], tails_forth[:, ROWS:2 * ROWS],
                                              tails_forth[:, 0:ROWS], carry[:, 0:1], ALU.add, ALU.max))
                mine.did(v.tensor_tensor_scan(carry_back[:, 0:ROWS][:, ::-1], tails_back[:, ROWS:2 * ROWS][:, ::-1],
                                              tails_back[:, 0:ROWS][:, ::-1], NEG, ALU.add, ALU.max))
                mine.settle()
                dve.sem_inc(carry_ready, 1)
                dve.wait_ge(carry_turned, group + 1)
                mine.did(v.tensor_copy(carry[:, 0:1], carry[:, ROWS:ROWS + 1]))
                mine.did(v.tensor_copy(carried[:, :], turned_carry))
                mine.settle()
                for h in range(heads):
                    for to, gate, col, of in ((top[:, h], first, h, forth[:, h]),
                                              (dst_score[:, h], first, heads + h, forth[:, heads + h]),
                                              (back[:, h], last, both + h, back[:, h])):
                        mine.did(v.scalar_tensor_tensor(out=to, in0=gate[:, :], scalar=carried[:, col:col + 1],
                                                        in1=of, op0=ALU.add, op1=ALU.max))
                mine.settle()
                mine.did(v.tensor_tensor(top[:, :, :], top[:, :, :], back[:, :, :], ALU.max))
                mine.did(v.tensor_tensor(z[:, :, :], src_scores, dst_score[:, :, :], ALU.add))
                mine.did(v.tensor_tensor(old[:, :], carried[0:1, 0:heads], dst_score[0:1, :, 0], ALU.add))
                mine.settle()
                mine.did(v.tensor_tensor(top[:, :, :], top[:, :, :], dst_score[:, :, :], ALU.add))

                def leaky(x):
                    mine.did(v.scalar_tensor_tensor(out=x, in0=x, scalar=SLOPE, in1=x, op0=ALU.mult, op1=ALU.max))

                leaky(z[:, :, :])
                leaky(old[:, :])
                mine.settle()
                leaky(top[:, :, :])
                mine.settle()
                mine.did(v.tensor_tensor(z[:, :, :], z[:, :, :], top[:, :, :], ALU.subtract))
                mine.did(v.tensor_tensor(old[:, :], old[:, :], top[0:1, :, 0], ALU.subtract))
                mine.settle()
                mine.then(v.tensor_scalar(old[:, :], old[:, :], 0.0, None, ALU.min))
                dve.sem_inc(exponents_ready, 1)
                dve.wait_ge(weights_copied, group + 1)
                for r in range(ROWS + 2):
                    if r < ROWS:
                        if r % REG_BATCH == 0:
                            _, batch = nc.values_load_multi_w_load_instructions(
                                keep["window"][0:1, bass.ds(group * ROWS + r, REG_BATCH)],
                                engines=[mybir.EngineType.DVE], min_val=0, max_val=WIDTH - P,
                                skip_runtime_bounds_check_because="nodes are below NODES")
                            at = {} if r == 0 else at
                            at |= {r + n: x for n, x in enumerate(batch)}
                        if r == 0:
                            first_col = acc[:, :, bass.ds(at[0], 1)]
                            mine.then(v.tensor_tensor(first_col, first_col, ps_factor.unsqueeze(2), ALU.mult))
                        for h in range(heads):
                            t = v.tensor_scalar(onehot[:, r % SLOTS, h, :], keep["lane"][:, :],
                                                places_now[:, r:r + 1], weights_now[:, h, r:r + 1],
                                                ALU.is_equal, ALU.mult)
                        t.then_inc(onehot_ready, 1)
                    if r >= 2:
                        q = r - 2
                        dve.wait_ge(summed, group * ROWS + (2 * ROWS + q + 1))
                        dve.wait_ge(added, group * ROWS + (SLOTS + q))
                        to = acc[:, :, bass.ds(at[q], P)]
                        v.tensor_tensor(to, to, ps_sum[q % SLOTS][0:LOADS, 0:heads * P].rearrange(
                            "p (h c) -> p h c", h=heads), ALU.add).then_inc(added, 1)
                assert mine.n == steps, mine.n


def update_nodes(nc, dram, keep, acc):
    with ExitStack() as stack:
        m = Mem(nc, stack, "update")
        spread = m.sbuf("spread", [P, HEADS1 * WIDTH // P])
        weights = m.sbuf("weights", [P, CHUNK * P])
        mean = m.sbuf("mean", [P, CHUNK * P])
        above = m.sbuf("above", [P, CHUNK * P])
        below = m.sbuf("below", [P, CHUNK * P])
        g = m.sbuf("g", [P, CHUNK * P])
        rows = m.sbuf("rows", [P, CHUNK, ROW2])
        ps_sums = m.psum("ps_sums", [P, CHUNK * P])
        ps_weights = m.psum("ps_weights", [P, CHUNK * P])
        ps_rows = m.psum("ps_rows", [P, CHUNK, P])

        spread_in = m.sem("spread_in")
        eps_added = m.sem("eps_added")
        inverted = m.sem("inverted")
        inverses_in = m.sem("inverses_in")
        sums_ready = m.sem("sums_ready")
        weights_copied = m.sem("weights_copied")
        divided = m.sem("divided")
        below_ready = m.sem("below_ready")
        parts_ready = m.sem("parts_ready")
        g_ready = m.sem("g_ready")
        rows_ready = m.sem("rows_ready")
        rows_copied = m.sem("rows_copied")
        rows_free = m.sem("rows_free")
        ones_set = m.sem("ones_set")
        stored = m.sem("stored")
        block = stack.enter_context(nc.Block())

        @block.tensor
        def _(pe):
            def sums(i):
                cols = bass.ds(i * (CHUNK * P), CHUNK * P)
                for h in range(HEADS1):
                    nc.tensor.matmul(ps_sums[:, :], keep["w1z"][:, h, :], acc[:, h, cols],
                                     start=(h == 0), stop=(h == HEADS1 - 1))
                for h in range(HEADS1):
                    t = nc.tensor.matmul(ps_weights[:, :], keep["sel"][:, h, :], acc[:, h, cols],
                                         start=(h == 0), stop=(h == HEADS1 - 1))
                t.then_inc(sums_ready, 1)

            def rows_of(i):
                pe.wait_ge(g_ready, i + 1)
                for b in range(CHUNK):
                    t = nc.tensor.matmul(ps_rows[:, b, 0:ROW2], g[:, b * P:(b + 1) * P], keep["w2ext"][:, :],
                                         start=True, stop=True)
                t.then_inc(rows_ready, 1)

            pe.wait_ge(inverses_in, 16)
            sums(0)
            with pe.Fori(0, CHUNKS - 1) as i:
                pe.wait_ge(divided, i + 1)
                sums(i + 1)
                rows_of(i)
            rows_of(CHUNKS - 1)

        @block.vector
        def _(dve):
            v = nc.vector
            v.memset(rows[:, :, D:D + 1], 1.0).then_inc(ones_set, 1)
            dve.wait_ge(spread_in, 16)
            v.tensor_scalar(spread[:, :], spread[:, :], EPS, None, ALU.add).then_inc(eps_added, 1)
            dve.wait_ge(eps_added, 1)
            v.reciprocal(spread[:, :], spread[:, :]).then_inc(inverted, 1)
            with dve.Fori(0, CHUNKS) as i:
                dve.wait_ge(weights_copied, i + 1)
                v.tensor_tensor(mean[:, :], ps_sums[:, :], weights[:, :], ALU.mult).then_inc(divided, 1)
                dve.wait_ge(divided, i + 1)
                v.tensor_scalar(below[:, :], mean[:, :], keep["b1"][:, 0:1], 0.0, ALU.add, ALU.min
                                ).then_inc(below_ready, 1)
                dve.wait_ge(parts_ready, i + 1)
                v.scalar_tensor_tensor(out=g[:, :], in0=below[:, :], scalar=-1.0, in1=above[:, :],
                                       op0=ALU.add, op1=ALU.add).then_inc(g_ready, 1)

        @block.scalar
        def _(act):
            def copy_rows(i):
                act.wait_ge(rows_ready, i + 1)
                act.wait_ge(rows_free, i + 1)
                nc.scalar.copy(rows[:, :, 0:D], ps_rows[:, :, 0:D])
                nc.scalar.copy(rows[:, :, LOADS:ROW2], ps_rows[:, :, LOADS:ROW2]).then_inc(rows_copied, 1)

            def inverses(i):
                act.wait_ge(sums_ready, i + 1)
                nc.scalar.copy(weights[:, :], ps_weights[:, :]).then_inc(weights_copied, 1)

            def parts(i):
                act.wait_ge(below_ready, i + 1)
                nc.scalar.activation(above[:, :], mean[:, :], ACT.Relu, bias=keep["b1"][:, 0:1])
                nc.scalar.activation(below[:, :], below[:, :], ACT.Exp).then_inc(parts_ready, 1)

            act.wait_ge(ones_set, 1)
            inverses(0)
            parts(0)
            with act.Fori(0, CHUNKS - 1) as i:
                inverses(i + 1)
                copy_rows(i)
                parts(i + 1)
            copy_rows(CHUNKS - 1)

        @block.sync
        def _(sp):
            weights_row = acc[D:D + 1, :, :].rearrange("o h n -> o (h n)").rearrange("o (p c) -> o p c", p=P)
            sp.dma_start(spread[:, :], weights_row).then_inc(spread_in, 16)
            sp.wait_ge(inverted, 1)
            sp.dma_start(weights_row, spread[:, :]).then_inc(inverses_in, 16)
            sp.sem_inc(rows_free, 1)
            table = dram["table2"].rearrange("(n b p) c -> p n b c", b=CHUNK, p=P)
            with sp.Fori(0, CHUNKS) as i:
                sp.wait_ge(rows_copied, i + 1)
                sp.dma_start(table[:, bass.ds(i, 1)].rearrange("p o b c -> p (o b) c"), rows[:, :, :]
                             ).then_inc(stored, 16)
                sp.wait_ge(stored, 16 * (i + 1))
                sp.sem_inc(rows_free, 1)


def finish_nodes(nc, dram, keep, acc):
    with ExitStack() as stack:
        m = Mem(nc, stack, "finish")
        part = m.sbuf("part", [LOADS, CHUNK * P])
        weights = m.sbuf("weights", [P, CHUNK])
        mean = m.sbuf("mean", [P, CHUNK, D])
        rows = m.sbuf("rows", [P, CHUNK, D])
        turned = m.psum("turned", [P, CHUNK, P])

        part_ready = m.sem("part_ready")
        part_turned = m.sem("part_turned")
        step = m.sem("step")
        divided = m.sem("divided")
        rows_ready = m.sem("rows_ready")
        rows_free = m.sem("rows_free")
        pe_passed = m.sem("pe_passed")
        stored = m.sem("stored")
        block = stack.enter_context(nc.Block())

        @block.scalar
        def _(act):
            act.sem_inc(part_turned, 1)
            with act.Fori(0, CHUNKS) as i:
                act.wait_ge(part_turned, i + 1)
                nc.scalar.copy(part[:, :], acc[:, 0, bass.ds(i * (CHUNK * P), CHUNK * P)]).then_inc(part_ready, 1)

        @block.tensor
        def _(pe):
            pe.sem_inc(divided, 1)
            with pe.Fori(0, CHUNKS) as i:
                wait_alone(pe, divided, i + 1, pe_passed)
                wait_alone(pe, part_ready, i + 1, pe_passed)
                for b in range(CHUNK):
                    t = nc.tensor.transpose(turned[:, b, 0:LOADS], part[:, b * P:(b + 1) * P],
                                            keep["ident"][0:LOADS, 0:LOADS])
                t.then_inc(part_turned, 1)

        @block.vector
        def _(dve):
            v = nc.vector
            with dve.Fori(0, CHUNKS) as i:
                dve.wait_ge(part_turned, i + 2)
                v.tensor_scalar(weights[:, :], turned[:, :, D], EPS, None, ALU.add).then_inc(step, 1)
                dve.wait_ge(step, 2 * i + 1)
                v.reciprocal(weights[:, :], weights[:, :]).then_inc(step, 1)
                dve.wait_ge(step, 2 * i + 2)
                v.tensor_tensor(mean[:, :, :], turned[:, :, 0:D],
                                weights[:, :].unsqueeze(2).to_broadcast([P, CHUNK, D]), ALU.mult
                                ).then_inc(divided, 1)
                dve.wait_ge(divided, i + 2)
                dve.wait_ge(rows_free, i + 1)
                v.tensor_tensor(rows[:, :, :], mean[:, :, :],
                                keep["b2"][:, :].unsqueeze(1).to_broadcast([P, CHUNK, D]), ALU.add
                                ).then_inc(rows_ready, 1)

        @block.sync
        def _(sp):
            sp.sem_inc(rows_free, 1)
            nodes = dram["nodes"].rearrange("(n b p) c -> p n b c", b=CHUNK, p=P)
            with sp.Fori(0, CHUNKS) as i:
                sp.wait_ge(rows_ready, i + 1)
                sp.dma_start(nodes[:, bass.ds(i, 1)].rearrange("p o b c -> p (o b) c"), rows[:, :, :]
                             ).then_inc(stored, 16)
                sp.wait_ge(stored, 16 * (i + 1))
                sp.sem_inc(rows_free, 1)


def dense_layer(nc, dram, keep, out):
    with ExitStack() as stack:
        m = Mem(nc, stack, "dense")
        tiles = BATCH // P
        parts = CTX + 1
        deep = parts * D // P
        cols = 500
        ring = 8
        fc_w = m.sbuf("fc_w", [P, deep, NODES])
        fc_b = m.sbuf("fc_b", [P, NODES])
        x = m.sbuf("x", [P, deep, BATCH])
        results = m.sbuf("results", [P, ring, cols])
        idx = m.sbuf("idx", [P, tiles * parts], I32)
        place = m.sbuf("place", [P, tiles * parts])
        below = m.sbuf("below", [P, tiles * parts])
        gathered = m.sbuf("gathered", [P, 2, parts * D])
        turned = m.psum("turned", [P, deep, P])
        ps = [m.psum(f"ps{s}", [P, 512]) for s in range(4)]

        fc_in = m.sem("fc_in")
        idx_in = m.sem("idx_in")
        step = m.sem("step")
        idx_ready = m.sem("idx_ready")
        landed = [m.sem("landed_even"), m.sem("landed_odd")]
        x_turned = m.sem("x_turned")
        x_copied = m.sem("x_copied")
        product = m.sem("product")
        biased = m.sem("biased")
        stored = [m.sem(f"stored{s}") for s in range(ring)]
        block = stack.enter_context(nc.Block())
        steps = NODES // cols
        out_v = out.rearrange("(p t) c -> p t c", t=tiles)

        @block.sync
        def _(sp):
            sp.dma_start(idx[:, 0:tiles], dram["user_idx"].rearrange("(p t) -> p t", p=P)).then_inc(idx_in, 16)
            sp.dma_start(idx[:, tiles:], dram["ctx_idx"].rearrange("(p t) c -> p (t c)", p=P)).then_inc(idx_in, 16)
            sp.dma_start(fc_w[:, :, :], dram["fc_w"].rearrange("(k p) n -> p k n", p=P)).then_inc(fc_in, 16)
            sp.dma_start(fc_b[:, :], dram["fc_b"].rearrange("(o n) -> o n", o=1).to_broadcast([P, NODES])
                         ).then_inc(fc_in, 16)
            with sp.Fori(0, steps) as c:
                for t in range(tiles):
                    sp.wait_ge(biased, c * tiles + (t + 1))
                    sp.dma_start(out_v[:, t, bass.ds(c * cols, cols)], results[:, t % ring, :]
                                 ).then_inc(stored[t % ring], 16)
            for s in range(ring):
                sp.wait_ge(stored[s], 16 * steps * tiles // ring)

        @block.vector
        def _(dve):
            v = nc.vector
            mine = Steps(dve, step)
            dve.wait_ge(idx_in, 32)
            mine.then(v.tensor_copy(place[:, :], idx[:, :]))
            mine.then(v.tensor_scalar(below[:, :], place[:, :], 0.0, float(NODES), ALU.is_lt, ALU.mult))
            mine.then(v.tensor_tensor(place[:, :], place[:, :], below[:, :], ALU.add))
            mine.then(v.tensor_scalar(place[:, :], place[:, :], 0.0, float(NODES - 1), ALU.max, ALU.min))
            v.tensor_copy(idx[:, :], place[:, :]).then_inc(idx_ready, 1)
            for t in range(tiles):
                dve.wait_ge(x_turned, t + 1)
                v.tensor_copy(x[:, :, t * P:(t + 1) * P], turned[:, :, :]).then_inc(x_copied, 1)
            dve.wait_ge(fc_in, 32)

            def add_bias(c, first=False):
                for t in range(tiles):
                    dve.wait_ge(product, c * tiles + (t + 1))
                    if not (first and t < ring):
                        dve.wait_ge(stored[t % ring], 16 * (c * (tiles // ring) + t // ring))
                    v.tensor_tensor(results[:, t % ring, :], ps[t % 4][:, 0:cols],
                                    fc_b[:, bass.ds(c * cols, cols)], ALU.add).then_inc(biased, 1)

            add_bias(0, first=True)
            with dve.Fori(1, steps) as c:
                add_bias(c)

        @block.gpsimd
        def _(pool):
            pool.wait_ge(idx_ready, 1)
            for t in range(tiles):
                if t >= 2:
                    pool.wait_ge(x_turned, t - 1)
                for c in range(parts):
                    col = tiles + t * CTX + c - 1 if c else t
                    nc.gpsimd.indirect_dma_start(
                        gathered[:, t % 2, c * D:(c + 1) * D], None, dram["user"] if c == 0 else dram["nodes"],
                        bass.IndirectOffsetOnAxis(ap=idx[:, col:col + 1], axis=0)).then_inc(landed[t % 2], 16)

        @block.tensor
        def _(pe):
            for t in range(tiles):
                pe.wait_ge(landed[t % 2], 16 * parts * (t // 2 + 1))
                if t:
                    pe.wait_ge(x_copied, t)
                for k in range(deep):
                    q = nc.tensor.transpose(turned[:, k, :], gathered[:, t % 2, k * P:(k + 1) * P],
                                            keep["ident"][:, :])
                q.then_inc(x_turned, 1)
            pe.wait_ge(x_copied, tiles)
            pe.wait_ge(fc_in, 32)

            def products(c, first=False):
                for t in range(tiles):
                    if not (first and t < 4):
                        pe.wait_ge(biased, c * tiles + (t - 3))
                    for k in range(deep):
                        q = nc.tensor.matmul(ps[t % 4][:, 0:cols], x[:, k, t * P:(t + 1) * P],
                                             fc_w[:, k, bass.ds(c * cols, cols)],
                                             start=(k == 0), stop=(k == deep - 1))
                    q.then_inc(product, 1)

            products(0, first=True)
            with pe.Fori(1, steps) as c:
                products(c)


INPUTS = ["r_user_idx", "r_context_idx", "L0_rec_edge_index", "L0_rec_user_emb", "L0_rec_service_emb",
          "L0_rec_W1", "L0_rec_att_src1", "L0_rec_att_dst1", "L0_rec_b1", "L0_rec_W2", "L0_rec_att_src2",
          "L0_rec_att_dst2", "L0_rec_b2", "L0_rec_fc_w", "L0_rec_fc_b"]
SHAPES = {"r_user_idx": ([BATCH], I32), "r_context_idx": ([BATCH, CTX], I32), "L0_rec_edge_index": ([2, EDGES], I32),
          "L0_rec_user_emb": ([NODES, D], F32), "L0_rec_service_emb": ([NODES, D], F32),
          "L0_rec_W1": ([D, 2 * D], F32), "L0_rec_att_src1": ([2, D], F32), "L0_rec_att_dst1": ([2, D], F32),
          "L0_rec_b1": ([2 * D], F32), "L0_rec_W2": ([2 * D, D], F32), "L0_rec_att_src2": ([1, D], F32),
          "L0_rec_att_dst2": ([1, D], F32), "L0_rec_b2": ([D], F32), "L0_rec_fc_w": ([4 * D, NODES], F32),
          "L0_rec_fc_b": ([NODES], F32)}


def declare(nc):
    def inp(n):
        return nc.dram_tensor(f"in_{n}", SHAPES[n][0], SHAPES[n][1], kind="ExternalInput").ap()
    a = {n: inp(n) for n in INPUTS}
    d = {"edges": a["L0_rec_edge_index"], "W1": a["L0_rec_W1"], "W2": a["L0_rec_W2"], "b1": a["L0_rec_b1"],
         "b2": a["L0_rec_b2"], "att_src1": a["L0_rec_att_src1"], "att_dst1": a["L0_rec_att_dst1"],
         "att_src2": a["L0_rec_att_src2"], "att_dst2": a["L0_rec_att_dst2"], "service": a["L0_rec_service_emb"],
         "user": a["L0_rec_user_emb"], "fc_w": a["L0_rec_fc_w"], "fc_b": a["L0_rec_fc_b"],
         "user_idx": a["r_user_idx"], "ctx_idx": a["r_context_idx"]}
    d["out"] = nc.dram_tensor("out", [BATCH, NODES], F32, kind="ExternalOutput").ap()
    for name, shape, dt in (("keys", [1 + P * COLS], I32), ("window", [TILES], I32), ("table1", [NODES, ROW1], F32),
                            ("table2", [WIDTH, ROW2], F32), ("nodes", [WIDTH, D], F32)):
        d[name] = nc.dram_tensor(name, shape, dt, kind="Internal").ap()
    return d


def program(nc, dram, stop=9):
    with ExitStack() as stack:
        m = Mem(nc, stack, "all")
        keep = {
            "ident": m.sbuf("ident", [P, P]), "lane": m.sbuf("lane", [P, P]), "ones": m.sbuf("ones", [P, P]),
            "w1z": m.sbuf("w1z", [LOADS, HEADS1, P]), "sel": m.sbuf("sel", [LOADS, HEADS1, P]),
            "w2ext": m.sbuf("w2ext", [P, ROW2]), "b1": m.sbuf("b1", [P, 1]), "b2": m.sbuf("b2", [P, D]),
        }
        with ExitStack() as graph:
            m = Mem(nc, graph, "graph")
            keep |= {
                "rows": m.sbuf("rows", [P, TILES], I32),
                "places": m.sbuf("places", [P, TILES]),
                "window": m.sbuf("window", [1, TILES], I32),
                "starts": m.sbuf("starts", [ROWS, GROUPS, P], BF16),
                "ends": m.sbuf("ends", [ROWS, GROUPS, P], BF16),
                "others": m.sbuf("others", [ROWS, GROUPS, P], BF16),
            }
            weights_and_sort(nc, dram, keep)
            if stop == 1:
                return
            index_tiles(nc, dram, keep)
            if stop == 2:
                dumps(nc, {"dump_idx": keep["rows"], "dump_loc": keep["places"], "dump_win": keep["window"]})
                return
            with ExitStack() as one:
                acc = Mem(nc, one, "sums1").sbuf("acc", [LOADS, HEADS1, WIDTH])
                sum_messages(nc, dram["table1"], keep, acc, HEADS1, "layer1")
                if stop == 3:
                    return dumps(nc, {"dump_acc": acc})
                update_nodes(nc, dram, keep, acc)
            if stop == 4:
                return
            acc = Mem(nc, graph, "sums2").sbuf("acc", [LOADS, HEADS2, WIDTH])
            sum_messages(nc, dram["table2"], keep, acc, HEADS2, "layer2")
            if stop == 5:
                return dumps(nc, {"dump_acc2": acc})
            finish_nodes(nc, dram, keep, acc)
        if stop == 6:
            return
        dense_layer(nc, dram, keep, dram["out"])


def dumps(nc, what):
    with ExitStack() as st:
        s = st.enter_context(nc.semaphore("dumps"))
        block = st.enter_context(nc.Block())

        @block.sync
        def _(sp):
            for n, t in what.items():
                o = nc.dram_tensor(n, list(t.shape), t.dtype, kind="ExternalOutput").ap()
                sl = tuple(slice(None) for _ in t.shape)
                sp.dma_start(o[sl], t[sl]).then_inc(s, 16)
            sp.wait_ge(s, 16 * len(what))


def kernel(**inputs):
    import concourse.bacc as bacc
    from concourse.bass_utils import run_bass_kernel_spmd

    nc = bacc.Bacc("TRN2", target_bir_lowering=False, num_devices=1)
    program(nc, declare(nc))
    arrays = {f"in_{name}": np.ascontiguousarray(inputs[name]) for name in INPUTS}
    return run_bass_kernel_spmd(nc, [arrays], core_ids=[0]).results[0]["out"]
```

```python
from contextlib import ExitStack, contextmanager

import numpy as np

import concourse.bass as bass
from concourse import mybir

F32 = mybir.dt.float32
F32R = mybir.dt.float32r
I32 = mybir.dt.int32
BF16 = mybir.dt.bfloat16
ALU = mybir.AluOpType
ACT = mybir.ActivationFunctionType
AX = mybir.AxisListType

P = 128
NODES = 12500
EDGES = 200000
D = 64
HEADS1, HEADS2 = 2, 1
BATCH = 2048
CTX = 3
SLOPE = 0.2
EPS = 1e-16
NEG = -1e30

FIELD_BITS = 14
FIELD = (1 << FIELD_BITS) - 1
TAG = 1 << (2 * FIELD_BITS)
DUMMY = NODES << FIELD_BITS | TAG | 1
COLS = 2048
COL_BITS, PART_BITS = 11, 7
IN_PARTS = 125

ROWS = 64
GROUPS = 2 * (-(-(EDGES + NODES) // (P * ROWS * 2)))
TILES = GROUPS * ROWS
CHUNK = 4
CHUNKS = -(-(NODES + P) // (CHUNK * P))
WIDTH = CHUNKS * CHUNK * P
NEED_HIGH = WIDTH // P
REG_BATCH = 16
SLOTS = 4

LOADS = D + 1
ROW1 = LOADS + 2 * HEADS1
ROW2 = LOADS + 2 * HEADS2


class Mem:

    def __init__(self, nc, stack, stage):
        self.nc, self.stack, self.stage = nc, stack, stage

    def sbuf(self, name, shape, dtype=F32):
        return self.stack.enter_context(self.nc.sbuf_tensor(f"{self.stage}_{name}", shape, dtype))

    def psum(self, name, shape, dtype=F32):
        return self.stack.enter_context(self.nc.psum_tensor(f"{self.stage}_{name}", shape, dtype))

    def sem(self, name):
        return self.stack.enter_context(self.nc.semaphore(f"{self.stage}_{name}"))


class Steps:

    def __init__(self, eng, sem, base=0):
        self.eng, self.sem, self.base, self.n = eng, sem, base, 0

    def did(self, ins):
        ins.then_inc(self.sem, 1)
        self.n += 1
        return self.n

    def settle(self, n=None):
        self.eng.wait_ge(self.sem, self.base + (self.n if n is None else n))

    def then(self, ins):
        self.did(ins)
        self.settle()


def as_float(bits):
    return float(np.array(bits, np.int32).view(np.float32))


def weights_and_sort(nc, dram, keep):
    with ExitStack() as stack:
        m = Mem(nc, stack, "sort")
        key_a = m.sbuf("key_a", [P, COLS])
        key_b = m.sbuf("key_b", [P, COLS])
        src = m.sbuf("src", [IN_PARTS, EDGES // IN_PARTS], I32)
        dst = m.sbuf("dst", [IN_PARTS, EDGES // IN_PARTS], I32)
        upper = m.sbuf("upper", [P, COLS // 2])
        part = m.sbuf("part", [P, 1], I32)
        bit = m.sbuf("bit", [P, PART_BITS], I32)
        sign = m.sbuf("sign", [P, PART_BITS])
        turn = m.sbuf("turn", [P, PART_BITS + 1])
        per = NODES // IN_PARTS
        table = m.sbuf("table", [IN_PARTS, per, ROW1])
        prod = m.sbuf("prod", [IN_PARTS, per, D])
        w1 = m.sbuf("w1", [D, HEADS1 * D])
        w1t = m.sbuf("w1t", [P, D])
        att1 = m.sbuf("att1", [P, 2 * HEADS1])
        att1_wide = m.sbuf("att1_wide", [P, 2 * HEADS1, P])
        score_w = m.sbuf("score_w", [P, 2 * HEADS1, D])
        w2t = m.sbuf("w2t", [D, P])
        att2 = m.sbuf("att2", [D, 2])
        turned = m.psum("turned", [P, COLS])
        ps_w1t = m.psum("ps_w1t", [P, 512])
        ps_w2t = m.psum("ps_w2t", [P, 512])
        ps_score = m.psum("ps_score", [P, 512])
        ident = keep["ident"]

        edges_in = m.sem("edges_in")
        nodes_in = m.sem("nodes_in")
        weights_in = m.sem("weights_in")
        keys_filled = m.sem("keys_filled")
        consts = m.sem("consts")
        zeroed = m.sem("zeroed")
        step = m.sem("step")
        flipped = m.sem("flipped")
        before_turn = m.sem("before_turn")
        after_turn = m.sem("after_turn")
        upper_ready = m.sem("upper_ready")
        prepared = m.sem("prepared")
        wide = m.sem("wide")
        score_ready = m.sem("score_ready")
        pool_step = m.sem("pool_step")
        table_ready = m.sem("table_ready")
        sorted_keys = m.sem("sorted_keys")
        stored = m.sem("stored")
        block = stack.enter_context(nc.Block())

        @block.sync
        def _(sp):
            sp.dma_start(dst[:, :], dram["edges"][1].rearrange("(p c) -> p c", p=IN_PARTS)).then_inc(edges_in, 16)
            sp.dma_start(src[:, :], dram["edges"][0].rearrange("(p c) -> p c", p=IN_PARTS)).then_inc(edges_in, 16)
            sp.dma_start(w1[:, :], dram["W1"]).then_inc(weights_in, 16)
            sp.dma_start(keep["w2ext"][:, 0:D], dram["W2"]).then_inc(weights_in, 16)
            sp.dma_start(keep["b1"][:, :], dram["b1"].rearrange("(c o) -> c o", o=1)).then_inc(weights_in, 16)
            sp.dma_start(keep["b2"][:, :], dram["b2"].rearrange("(o c) -> o c", o=1).to_broadcast([P, D])
                         ).then_inc(weights_in, 16)
            sp.dma_start(att2[:, 0:1], dram["att_src2"].rearrange("h d -> d h")).then_inc(weights_in, 16)
            sp.dma_start(att2[:, 1:2], dram["att_dst2"].rearrange("h d -> d h")).then_inc(weights_in, 16)
            sp.wait_ge(zeroed, 1)
            for h in range(HEADS1):
                own = slice(h * D, (h + 1) * D)
                sp.dma_start(att1[own, h:h + 1], dram["att_src1"][h:h + 1].rearrange("h d -> d h")
                             ).then_inc(weights_in, 16)
                sp.dma_start(att1[own, HEADS1 + h:HEADS1 + h + 1],
                             dram["att_dst1"][h:h + 1].rearrange("h d -> d h")).then_inc(weights_in, 16)
                sp.dma_start(keep["w1z"][0:D, h, own], dram["W1"][:, own]).then_inc(weights_in, 16)
            sp.dma_start(table[:, :, 0:D], dram["service"].rearrange("(p c) d -> p c d", p=IN_PARTS)
                         ).then_inc(nodes_in, 16)
            sp.wait_ge(table_ready, 1)
            sp.dma_start(dram["table1"].rearrange("(p c) d -> p c d", p=IN_PARTS), table[:, :, :]
                         ).then_inc(stored, 16)
            sp.wait_ge(sorted_keys, 1)
            sp.dma_start(dram["keys"][1:1 + P * COLS].rearrange("(p c) -> p c", p=P), key_a[:, :].bitcast(I32)
                         ).then_inc(stored, 16)
            sp.dma_start(dram["keys"][0:1].rearrange("(p c) -> p c", p=1), key_a[P - 1:P, COLS - 1:COLS].bitcast(I32)
                         ).then_inc(stored, 16)
            sp.wait_ge(stored, 48)

        @block.gpsimd
        def _(pool):
            g = nc.gpsimd
            mine = Steps(pool, pool_step)
            mine.then(g.memset(key_a[:, :], as_float(DUMMY)))
            loops = key_a[0:IN_PARTS, EDGES // IN_PARTS:EDGES // IN_PARTS + per].bitcast(I32)
            g.iota(loops, [[1, per]], base=0, channel_multiplier=per).then_inc(keys_filled, 1)
            g.iota(part[:, :], [[0, 1]], base=0, channel_multiplier=1).then_inc(consts, 1)
            mine.then(g.memset(att1[:, :], 0.0))
            mine.then(g.memset(keep["w2ext"][:, D:D + 1], 0.0))
            mine.then(g.memset(keep["sel"][:, :, :], 0.0))
            mine.then(g.memset(keep["w1z"][:, :, :], 0.0))
            pool.sem_inc(zeroed, 1)
            for h in range(HEADS1):
                mine.then(g.memset(keep["sel"][D:D + 1, h, h * D:(h + 1) * D], 1.0))
            mine.then(g.memset(keep["ones"][:, :], 1.0))
            mine.then(g.memset(ident[:, :], 0.0))
            mine.then(g.affine_select(out=ident[:, :], in_=ident[:, :], compare_op=ALU.not_equal, fill=1.0,
                                      base=0, pattern=[[-1, P]], channel_multiplier=1))
            pool.sem_inc(consts, 1)
            mine.then(g.iota(keep["lane"][:, :], [[1, P]], base=0, channel_multiplier=0,
                             allow_small_or_imprecise_dtypes=True))
            pool.wait_ge(weights_in, 16 * (6 + 3 * HEADS1))
            mine.then(g.tensor_copy(att1_wide[:, :, :],
                                    att1[:, :].unsqueeze(2).to_broadcast([P, 2 * HEADS1, P])))
            pool.sem_inc(wide, 1)
            pool.wait_ge(nodes_in, 16)
            pool.wait_ge(score_ready, 1)
            mine.then(g.memset(table[:, :, D:D + 1], 1.0))
            for c in range(2 * HEADS1):
                w = score_w[0:IN_PARTS, c:c + 1, :].to_broadcast([IN_PARTS, per, D])
                mine.then(g.tensor_tensor(prod[:, :, :], table[:, :, 0:D], w, ALU.mult))
                half = D
                while half > 1:
                    half //= 2
                    to = prod[:, :, 0:half] if half > 1 else table[:, :, LOADS + c:LOADS + c + 1]
                    mine.then(g.tensor_tensor(to, prod[:, :, 0:half], prod[:, :, half:2 * half], ALU.add))
            pool.sem_inc(table_ready, 1)

        @block.scalar
        def _(act):
            act.wait_ge(prepared, 2)
            nc.scalar.copy(w1t[:, :], ps_w1t[:, 0:D]).then_inc(prepared, 1)
            nc.scalar.copy(w2t[:, :], ps_w2t[0:D, 0:P]).then_inc(prepared, 1)
            act.wait_ge(prepared, 5)
            nc.scalar.copy(keep["w2ext"][:, LOADS:ROW2], ps_w2t[:, 256:258])
            nc.scalar.copy(score_w[:, :, :], ps_score[:, 0:2 * HEADS1 * D].rearrange(
                "p (c d) -> p c d", d=D)).then_inc(score_ready, 1)
            for n in range(1, PART_BITS + 1):
                for way, dist in enumerate((1 << (n - 1), COLS // 2)):
                    act.wait_ge(after_turn, 2 * n - 1 + way)
                    nc.scalar.copy(upper[:, :].rearrange("p (m d) -> p m d", d=dist),
                                   turned[:, :].rearrange("p (m t d) -> p m t d", t=2, d=dist)[:, :, 1, :]
                                   ).then_inc(upper_ready, 1)

        @block.tensor
        def _(pe):
            pe.wait_ge(consts, 2)
            pe.wait_ge(weights_in, 16 * (6 + 3 * HEADS1))
            nc.tensor.transpose(ps_w1t[:, 0:D], w1[:, :], ident[0:D, 0:D]).then_inc(prepared, 1)
            nc.tensor.transpose(ps_w2t[0:D, 0:P], keep["w2ext"][:, 0:D], ident[:, :]).then_inc(prepared, 1)
            pe.wait_ge(prepared, 4)
            pe.wait_ge(wide, 1)
            for c in range(2 * HEADS1):
                nc.tensor.matmul(ps_score[:, c * D:(c + 1) * D], att1_wide[:, c, :], w1t[:, :],
                                 start=True, stop=True)
            nc.tensor.matmul(ps_w2t[:, 256:258], w2t[:, :], att2[:, :], start=True, stop=True
                             ).then_inc(prepared, 1)
            chunks = COLS // P
            for n in range(PART_BITS):
                for way in range(2):
                    pe.wait_ge(before_turn, 2 * n + way + 1)
                    for c in range(chunks):
                        if way == 0:
                            out, inp = turned[:, c * P:(c + 1) * P], key_a[:, c * P:(c + 1) * P]
                        else:
                            out, inp = turned[:, c * P:(c + 1) * P], key_b[:, c * P:(c + 1) * P]
                        last = nc.tensor.transpose(out, inp, ident[:, :])
                    last.then_inc(after_turn, 1)

        @block.vector
        def _(dve):
            v = nc.vector
            mine = Steps(dve, step)
            edge_cols = slice(0, EDGES // IN_PARTS)
            loop_cols = slice(EDGES // IN_PARTS, EDGES // IN_PARTS + per)
            bits_a = key_a[0:IN_PARTS, :].bitcast(I32)
            dve.wait_ge(keys_filled, 1)
            dve.wait_ge(consts, 1)
            mine.did(v.tensor_scalar(bits_a[:, loop_cols], bits_a[:, loop_cols], FIELD_BITS, TAG,
                                     ALU.logical_shift_left, ALU.bitwise_or))
            dve.wait_ge(edges_in, 32)
            mine.did(v.tensor_scalar(dst[:, :], dst[:, :], FIELD_BITS, TAG,
                                     ALU.logical_shift_left, ALU.bitwise_or))
            mine.did(v.tensor_scalar(src[:, :], src[:, :], 1.0, None, ALU.add))
            for b in range(PART_BITS):
                mine.did(v.tensor_scalar(bit[:, b:b + 1], part[:, :], b, 1,
                                         ALU.logical_shift_right, ALU.bitwise_and))
            mine.settle()
            mine.did(v.tensor_tensor(bits_a[:, edge_cols], dst[:, :], src[:, :], ALU.bitwise_or))
            mine.then(v.tensor_scalar(sign[:, :], bit[:, :], -2.0, 1.0, ALU.mult, ALU.add))
            mine.did(v.tensor_copy(turn[:, 0:1], sign[:, 0:1]))
            mine.did(v.tensor_tensor(turn[:, 1:PART_BITS], sign[:, 1:PART_BITS], sign[:, 0:PART_BITS - 1],
                                     ALU.mult))
            mine.then(v.tensor_copy(turn[:, PART_BITS:PART_BITS + 1], sign[:, PART_BITS - 1:PART_BITS]))

            def exchange(to, of, dist):
                a, b = (x.rearrange("p (m t d) -> p m t d", t=2, d=dist) for x in (of[:, :], to[:, :]))
                low, high = a[:, :, 0, :], a[:, :, 1, :]
                if of is turned:
                    high = upper[:, :].rearrange("p (m d) -> p m d", d=dist)
                mine.did(v.tensor_tensor(b[:, :, 0, :], low, high, ALU.min))
                mine.did(v.tensor_tensor(b[:, :, 1, :], low, high, ALU.max))
                mine.settle()

            at, other = key_a, key_b
            for k in range(1, COL_BITS):
                for j in reversed(range(k)):
                    views = [x[:, :].rearrange("p (n w m t d) -> p n w m t d", w=2, m=1 << (k - 1 - j),
                                               t=2, d=1 << j) for x in (at, other)]
                    for way in range(2):
                        a, b = (x[:, :, way] for x in views)
                        for t, op in ((0, ALU.min), (1, ALU.max)):
                            mine.did(v.tensor_tensor(b[:, :, :, t ^ way, :], a[:, :, :, 0, :],
                                                     a[:, :, :, 1, :], op))
                    mine.settle()
                    at, other = other, at
            for k in range(COL_BITS, COL_BITS + PART_BITS + 1):
                n = k - COL_BITS
                mine.then(v.tensor_scalar(key_a[:, :], at[:, :], turn[:, n:n + 1], None, ALU.mult))
                at, other = key_a, key_b
                if n:
                    dve.sem_inc(before_turn, 1)
                    dve.wait_ge(upper_ready, 2 * n - 1)
                    of = turned
                    for j in reversed(range(n)):
                        to = key_b if (j % 2 == 0) else key_a
                        exchange(to, of, 1 << j)
                        of = to
                    dve.sem_inc(before_turn, 1)
                    dve.wait_ge(upper_ready, 2 * n)
                    at = turned
                for j in reversed(range(COL_BITS)):
                    to = key_a if (at is not key_a) else key_b
                    exchange(to, at, 1 << j)
                    at = to
            assert at is key_a
            dve.sem_inc(sorted_keys, 1)


def index_tiles(nc, dram, keep, stage, chosen=None):
    with ExitStack() as stack:
        m = Mem(nc, stack, stage)
        keys = m.sbuf("keys", [ROWS, GROUPS, P + 2], I32)
        node = m.sbuf("node", [ROWS, GROUPS, P + 2])
        field = m.sbuf("field", [ROWS, GROUPS, P])
        loop = m.sbuf("loop", [ROWS, GROUPS, P])
        row = m.sbuf("row", [ROWS, GROUPS, P])
        first = m.sbuf("first", [GROUPS, 2, ROWS], I32)
        turned = m.psum("turned", [P, 2, 2, ROWS])
        turned_first = m.psum("turned_first", [P, 2, ROWS])

        keys_in = m.sem("keys_in")
        step = m.sem("step")
        rows_ready = m.sem("rows_ready")
        turned_row = m.sem("turned_row")
        copied = m.sem("copied")
        copies_out = m.sem("copies_out")
        nodes_ready = m.sem("nodes_ready")
        turned_nodes = m.sem("turned_nodes")
        first_ready = m.sem("first_ready")
        window_out = m.sem("window_out")
        window_in = m.sem("window_in")
        block = stack.enter_context(nc.Block())
        group = ROWS * P

        @block.gpsimd
        def _(pool):
            if chosen is not None:
                for n in range(GROUPS):
                    nc.gpsimd.indirect_dma_start(
                        keys[:, n, :], None, dram["tile_keys"],
                        bass.IndirectOffsetOnAxis(ap=chosen[:, n:n + 1], axis=0)).then_inc(keys_in, 16)

        @block.sync
        def _(sp):
            if chosen is None:
                t = dram["keys"].tensor
                with_neighbours = bass.AP(tensor=t, offset=0, ap=[[P, TILES], [1, P + 2]])
                sp.dma_start(dram["tile_keys"][0:TILES, :], with_neighbours).then_inc(copies_out, 16)
                sp.dma_start(dram["tile_keys"][TILES:TILES + 1, :],
                             bass.AP(tensor=t, offset=P * COLS - P - 2, ap=[[P + 2, 1], [1, P + 2]])
                             ).then_inc(copies_out, 16)
                for half in range(2):
                    n = GROUPS // 2
                    sp.dma_start(keys[:, half * n:(half + 1) * n, :],
                                 bass.AP(tensor=t, offset=half * n * group, ap=[[P, ROWS], [group, n], [1, P + 2]])
                                 ).then_inc(keys_in, 16)
            sp.wait_ge(first_ready, 1)
            sp.dma_start(dram["window"].rearrange("w (b r) -> b w r", r=ROWS), first[:, :, :]
                         ).then_inc(window_out, 16)
            sp.wait_ge(window_out, 16)
            sp.dma_start(keep["window"][:, :], dram["window"][0:1, :]).then_inc(window_in, 16)
            sp.wait_ge(window_in, 16)
            if chosen is None:
                sp.wait_ge(copies_out, 32)

        @block.vector
        def _(dve):
            v = nc.vector
            mine = Steps(dve, step)
            dve.wait_ge(keys_in, 32 if chosen is None else 16 * GROUPS)
            mine.then(v.tensor_scalar(field[:, :, :].bitcast(I32), keys[:, :, 1:P + 1], FIELD, None,
                                      ALU.bitwise_and))
            mine.then(v.tensor_scalar(keys[:, :, :], keys[:, :, :], FIELD_BITS, FIELD,
                                      ALU.logical_shift_right, ALU.bitwise_and))
            mine.did(v.tensor_copy(node[:, :, :], keys[:, :, :]))
            mine.then(v.tensor_copy(row[:, :, :], field[:, :, :].bitcast(I32)))
            dve.sem_inc(nodes_ready, 1)
            own = node[:, :, 1:P + 1]
            mine.did(v.tensor_tensor(keep["starts"][:, :, :], own, node[:, :, 0:P], ALU.not_equal))
            mine.did(v.tensor_tensor(keep["ends"][:, :, ::-1], own, node[:, :, 2:P + 2], ALU.not_equal))
            mine.then(v.tensor_scalar(loop[:, :, :], row[:, :, :], 0.0, None, ALU.is_equal))
            mine.did(v.tensor_scalar(keep["starts"][:, :, :], keep["starts"][:, :, :], NEG, None, ALU.mult))
            mine.did(v.tensor_scalar(keep["ends"][:, :, :], keep["ends"][:, :, :], NEG, None, ALU.mult))
            mine.did(v.tensor_scalar(keep["others"][:, :, :], loop[:, :, :], -NEG, NEG, ALU.mult, ALU.add))
            mine.did(v.scalar_tensor_tensor(out=field[:, :, :], in0=own, scalar=1.0, in1=loop[:, :, :],
                                            op0=ALU.add, op1=ALU.mult))
            mine.settle()
            mine.did(v.scalar_tensor_tensor(out=row[:, :, :], in0=row[:, :, :], scalar=-1.0,
                                            in1=field[:, :, :], op0=ALU.add, op1=ALU.add))
            mine.then(v.tensor_tensor(loop[:, :, :], own, node[:, :, 1:2].to_broadcast([ROWS, GROUPS, P]),
                                      ALU.subtract))
            dve.sem_inc(rows_ready, 1)
            dve.wait_ge(turned_nodes, 1)
            v.tensor_copy(first[:, :, :], turned_first[0:GROUPS, :, :]).then_inc(first_ready, 1)
            for n in range(GROUPS // 2):
                dve.wait_ge(turned_row, n + 1)
                to = slice(2 * n * ROWS, 2 * (n + 1) * ROWS)
                v.tensor_copy(keep["rows"][:, to].rearrange("p (b r) -> p b r", b=2), turned[:, 0])
                v.tensor_copy(keep["places"][:, to].rearrange("p (b r) -> p b r", b=2),
                              turned[:, 1]).then_inc(copied, 1)

        @block.tensor
        def _(pe):
            pe.wait_ge(nodes_ready, 1)
            for w, col in enumerate((1, P)):
                t = nc.tensor.transpose(turned_first[0:GROUPS, w, :], node[:, :, col], keep["ident"][0:ROWS, 0:ROWS])
            t.then_inc(turned_nodes, 1)
            pe.wait_ge(rows_ready, 1)
            for n in range(GROUPS // 2):
                if n:
                    pe.wait_ge(copied, n)
                for what, of in enumerate((row, loop)):
                    for b in range(2):
                        last = nc.tensor.transpose(turned[:, what, b], of[:, 2 * n + b, :],
                                                   keep["ident"][0:ROWS, 0:ROWS])
                last.then_inc(turned_row, 1)


def clamp_indices(v, mine, idx, place, below):
    mine.then(v.tensor_copy(place[:, :], idx[:, :]))
    mine.then(v.tensor_scalar(below[:, :], place[:, :], 0.0, float(NODES), ALU.is_lt, ALU.mult))
    mine.then(v.tensor_tensor(place[:, :], place[:, :], below[:, :], ALU.add))
    mine.then(v.tensor_scalar(place[:, :], place[:, :], 0.0, float(NODES - 1), ALU.max, ALU.min))


def choose_tiles(nc, dram, keep):
    with ExitStack() as stack:
        m = Mem(nc, stack, "choose")
        looks = BATCH * CTX // P
        per = TILES // P
        idx = m.sbuf("idx", [P, looks], I32)
        place = m.sbuf("place", [P, looks])
        below = m.sbuf("below", [P, looks])
        low_bits = m.sbuf("low_bits", [P, looks], I32)
        high_bits = m.sbuf("high_bits", [P, looks], I32)
        low = m.sbuf("low", [P, looks])
        high = m.sbuf("high", [P, looks])
        onehot_low = m.sbuf("onehot_low", [P, looks, P], BF16)
        onehot_high = m.sbuf("onehot_high", [P, looks, P], BF16)
        part = m.sbuf("part", [P, 1])
        tile_id = m.sbuf("tile_id", [P, per])
        before = m.sbuf("before", [P, P])
        until = m.sbuf("until", [P, P])
        ends_idx = m.sbuf("ends_idx", [P, 2, per], I32)
        found = m.sbuf("found", [P, 2, per])
        flag = m.sbuf("flag", [P, per])
        position = m.sbuf("position", [P, per])
        position_bits = m.sbuf("position_bits", [P, 3, per], I32)
        row_group = m.sbuf("row_group", [P, 2, per])
        value = m.sbuf("value", [P, per])
        in_row = m.sbuf("in_row", [P, per, ROWS])
        in_group = m.sbuf("in_group", [P, per, GROUPS])
        ps_need = m.psum("ps_need", [P, 512])
        ps_before = m.psum("ps_before", [P, 512])
        ps_list = m.psum("ps_list", [P, 512])

        idx_in = m.sem("idx_in")
        step = m.sem("step")
        consts = m.sem("consts")
        onehots_ready = m.sem("onehots_ready")
        counted = m.sem("counted")
        totals_ready = m.sem("totals_ready")
        offsets_ready = m.sem("offsets_ready")
        until_ready = m.sem("until_ready")
        until_out = m.sem("until_out")
        found_in = m.sem("found_in")
        ends_ready = m.sem("ends_ready")
        flags_ready = m.sem("flags_ready")
        flags_counted = m.sem("flags_counted")
        list_ready = m.sem("list_ready")
        listed = m.sem("listed")
        block = stack.enter_context(nc.Block())

        @block.sync
        def _(sp):
            sp.dma_start(idx[:, :], dram["ctx_idx"].rearrange("(p t) c -> p (t c)", p=P)).then_inc(idx_in, 16)
            sp.dma_start(ends_idx[:, :, :], dram["window"].rearrange("w (p j) -> p w j", p=P)).then_inc(idx_in, 16)
            sp.wait_ge(until_ready, 1)
            sp.dma_start(dram["needed"][1:1 + NEED_HIGH * P, :].rearrange("(p c) o -> p (c o)", p=NEED_HIGH),
                         until[0:NEED_HIGH, :]).then_inc(until_out, 16)
            sp.dma_start(dram["needed"][0:1, :], part[0:1, :]).then_inc(until_out, 16)

        @block.gpsimd
        def _(pool):
            g = nc.gpsimd
            g.iota(part[:, :], [[0, 1]], base=0, channel_multiplier=1, allow_small_or_imprecise_dtypes=True)
            g.iota(tile_id[:, :], [[1, per]], base=0, channel_multiplier=per, allow_small_or_imprecise_dtypes=True
                   ).then_inc(consts, 1)
            pool.wait_ge(ends_ready, 1)
            pool.wait_ge(until_out, 32)
            for w in range(2):
                for j in range(per):
                    g.indirect_dma_start(found[:, w, j:j + 1], None, dram["needed"],
                                         bass.IndirectOffsetOnAxis(ap=ends_idx[:, w, j:j + 1], axis=0)
                                         ).then_inc(found_in, 16)

        @block.tensor
        def _(pe):
            pe.wait_ge(onehots_ready, looks)
            for c in range(looks):
                t = nc.tensor.matmul(ps_need[:, 0:P], onehot_high[:, c, :], onehot_low[:, c, :],
                                     start=(c == 0), stop=(c == looks - 1))
            t.then_inc(counted, 1)
            pe.wait_ge(totals_ready, 1)
            nc.tensor.matmul(ps_before[:, 0:1], before[:, :], until[:, P - 1:P], start=True, stop=True
                             ).then_inc(offsets_ready, 1)
            pe.wait_ge(flags_ready, 1)
            nc.tensor.matmul(ps_before[:, 1:2], before[:, :], position[:, per - 1:per], start=True, stop=True)
            nc.tensor.matmul(ps_before[:, 2:3], keep["ones"][:, :], position[:, per - 1:per], start=True, stop=True
                             ).then_inc(flags_counted, 1)
            pe.wait_ge(list_ready, 1)
            for j in range(per):
                t = nc.tensor.matmul(ps_list[0:ROWS, 0:GROUPS], in_row[:, j, :], in_group[:, j, :],
                                     start=(j == 0), stop=(j == per - 1))
            t.then_inc(listed, 1)

        @block.vector
        def _(dve):
            v = nc.vector
            mine = Steps(dve, step)
            dve.wait_ge(idx_in, 32)
            v.tensor_scalar(ends_idx[:, 1, :], ends_idx[:, 1, :], 1.0, None, ALU.add).then_inc(ends_ready, 1)
            clamp_indices(v, mine, idx, place, below)
            mine.then(v.tensor_copy(idx[:, :], place[:, :]))
            mine.did(v.tensor_scalar(low_bits[:, :], idx[:, :], P - 1, None, ALU.bitwise_and))
            mine.then(v.tensor_scalar(high_bits[:, :], idx[:, :], P.bit_length() - 1, None,
                                      ALU.logical_shift_right))
            mine.did(v.tensor_copy(low[:, :], low_bits[:, :]))
            mine.then(v.tensor_copy(high[:, :], high_bits[:, :]))
            for c in range(looks):
                v.tensor_scalar(onehot_low[:, c, :], keep["lane"][:, :], low[:, c:c + 1], None, ALU.is_equal)
                v.tensor_scalar(onehot_high[:, c, :], keep["lane"][:, :], high[:, c:c + 1], None, ALU.is_equal
                                ).then_inc(onehots_ready, 1)
            dve.wait_ge(consts, 1)
            mine.did(v.tensor_scalar(before[:, :], keep["lane"][:, :], part[:, 0:1], None, ALU.is_gt))
            dve.wait_ge(counted, 1)
            mine.then(v.tensor_tensor_scan(until[:, :], keep["ones"][:, :], ps_need[:, 0:P], 0.0,
                                           ALU.mult, ALU.add))
            dve.sem_inc(totals_ready, 1)
            dve.wait_ge(offsets_ready, 1)
            v.tensor_scalar(until[:, :], until[:, :], ps_before[:, 0:1], None, ALU.add).then_inc(until_ready, 1)
            dve.wait_ge(found_in, 16 * 2 * per)
            mine.then(v.tensor_tensor(flag[:, :], found[:, 1, :], found[:, 0, :], ALU.is_gt))
            mine.then(v.tensor_tensor_scan(position[:, :], keep["ones"][:, 0:per], flag[:, :], 0.0,
                                           ALU.mult, ALU.add))
            dve.sem_inc(flags_ready, 1)
            dve.wait_ge(flags_counted, 1)
            mine.did(v.tensor_scalar(place[:, 0:1], ps_before[:, 2:3], float(ROWS - 1), None, ALU.add))
            mine.then(v.tensor_scalar(position[:, :], position[:, :], ps_before[:, 1:2], -1.0, ALU.add, ALU.add))
            mine.did(v.tensor_copy(position_bits[:, 2, 0:1], place[:, 0:1]))
            mine.then(v.tensor_copy(position_bits[:, 0, :], position[:, :]))
            shift = ROWS.bit_length() - 1
            mine.did(v.tensor_scalar(keep["chosen_groups"][:, :], position_bits[0:1, 2, 0:1], shift, None,
                                     ALU.arith_shift_right))
            mine.did(v.tensor_scalar(position_bits[:, 1, :], position_bits[:, 0, :], shift, None,
                                     ALU.arith_shift_right))
            mine.settle()
            mine.then(v.tensor_scalar(position_bits[:, 0, :], position_bits[:, 0, :], ROWS - 1, None,
                                      ALU.bitwise_and))
            mine.did(v.tensor_copy(row_group[:, :, :], position_bits[:, 0:2, :]))
            mine.then(v.tensor_scalar(value[:, :], tile_id[:, :], -float(TILES), None, ALU.add))
            mine.then(v.tensor_tensor(value[:, :], value[:, :], flag[:, :], ALU.mult))
            for j in range(per):
                mine.did(v.tensor_scalar(in_row[:, j, :], keep["lane"][:, 0:ROWS], row_group[:, 0, j:j + 1], None,
                                         ALU.is_equal))
                mine.did(v.tensor_scalar(in_group[:, j, :], keep["lane"][:, 0:GROUPS], row_group[:, 1, j:j + 1],
                                         value[:, j:j + 1], ALU.is_equal, ALU.mult))
            mine.settle()
            dve.sem_inc(list_ready, 1)
            dve.wait_ge(listed, 1)
            mine.then(v.tensor_scalar(keep["chosen"][:, :], ps_list[0:ROWS, 0:GROUPS], float(TILES), None, ALU.add))


def wait_alone(eng, sem, value, passed):
    eng.wait_ge(sem, value)
    eng.sem_inc(passed, 1)


@contextmanager
def only_if(eng, group, count):
    if count is None:
        yield
        return
    with eng.If(group < count):
        yield
    with eng.Else():
        eng.nop()


def sum_messages(nc, table, keep, acc, heads, stage, count=None):
    with ExitStack() as stack:
        m = Mem(nc, stack, stage)
        both = 2 * heads
        width = LOADS + both
        fetched = m.sbuf("fetched", [P, 2 * ROWS, width])
        rows_now = m.sbuf("rows_now", [P, 2 * ROWS], I32)
        places_now = m.sbuf("places_now", [P, ROWS])
        weights_now = m.sbuf("weights_now", [P, heads, ROWS])
        onehot = m.sbuf("onehot", [P, SLOTS, heads, P])
        own_loop = m.sbuf("own_loop", [ROWS, heads, P])
        first = m.sbuf("first", [ROWS, P])
        last = m.sbuf("last", [ROWS, P])
        forth = m.sbuf("forth", [ROWS, both, P])
        back = m.sbuf("back", [ROWS, heads, P])
        tails = m.sbuf("tails", [ROWS, 6 * heads])
        tails_forth = m.sbuf("tails_forth", [both, 2 * ROWS])
        tails_back = m.sbuf("tails_back", [heads, 2 * ROWS])
        carry = m.sbuf("carry", [both, ROWS + 1])
        carry_back = m.sbuf("carry_back", [heads, ROWS + 1])
        carried = m.sbuf("carried", [ROWS, 3 * heads])
        top = m.sbuf("top", [ROWS, heads, P])
        dst_score = m.sbuf("dst_score", [ROWS, heads, P])
        z = m.sbuf("z", [ROWS, heads, P])
        weight = m.sbuf("weight", [ROWS, heads, P])
        old = m.sbuf("old", [1, heads])
        factor = m.sbuf("factor", [1, heads])
        ps_scores = m.psum("ps_scores", [ROWS, both, P])
        ps_small = m.psum("ps_small", [P, 512])
        ps_weights = m.psum("ps_weights", [P, 512])
        ps_sum = [m.psum(f"ps_sum{s}", [P, 512]) for s in range(SLOTS)]
        turned_weights = ps_weights[:, 0:heads * ROWS].rearrange("p (h r) -> p h r", h=heads)
        turned_tails = [ps_small[0:n, c * ROWS:(c + 1) * ROWS]
                        for c, n in enumerate((both, both, heads, heads))]
        turned_carry = ps_small[0:ROWS, 4 * ROWS:4 * ROWS + 3 * heads]
        ps_factor = ps_small[0:LOADS, 5 * ROWS:5 * ROWS + heads]

        landed = [m.sem("landed_even"), m.sem("landed_odd")]
        rows_copied = m.sem("rows_copied")
        scores_turned = m.sem("scores_turned")
        tails_ready = m.sem("tails_ready")
        tails_turned = m.sem("tails_turned")
        carry_ready = m.sem("carry_ready")
        carry_turned = m.sem("carry_turned")
        exponents_ready = m.sem("exponents_ready")
        weights_ready = m.sem("weights_ready")
        weights_turned = m.sem("weights_turned")
        weights_copied = m.sem("weights_copied")
        step = m.sem("step")
        pe_passed = m.sem("pe_passed")
        pool_passed = m.sem("pool_passed")
        onehot_ready = m.sem("onehot_ready")
        summed = m.sem("summed")
        added = m.sem("added")
        block = stack.enter_context(nc.Block())

        @block.gpsimd
        def _(pool):
            groups = None if count is None else pool.value_load(count, min_val=1, max_val=GROUPS)
            with pool.Fori(0, GROUPS // 2) as i:
                for half in range(2):
                    with only_if(pool, 2 * i + half, groups):
                        pool.wait_ge(summed, (2 * i + half + 1) * ROWS)
                        nc.gpsimd.tensor_copy(rows_now[:, half * ROWS:(half + 1) * ROWS],
                                              keep["rows"][:, bass.ds((2 * i + half) * ROWS, ROWS)]
                                              ).then_inc(rows_copied, 1)
                        wait_alone(pool, rows_copied, 2 * i + half + 1, pool_passed)
                        for r in range(half * ROWS, (half + 1) * ROWS):
                            nc.gpsimd.indirect_dma_start(
                                fetched[:, r, :], None, table,
                                bass.IndirectOffsetOnAxis(ap=rows_now[:, r:r + 1], axis=0)).then_inc(landed[half], 16)

        @block.tensor
        def _(pe):
            ident = keep["ident"]
            pe.sem_inc(summed, 2 * ROWS)
            groups = None if count is None else pe.value_load(count, min_val=1, max_val=GROUPS)
            with pe.Fori(0, GROUPS // 2) as i:
                for half in range(2):
                    group = 2 * i + half
                    with only_if(pe, group, groups):
                        wait_alone(pe, landed[half], (i + 1) * (16 * ROWS), pe_passed)
                        tiles = slice(half * ROWS, (half + 1) * ROWS)
                        for c in range(both):
                            t = nc.tensor.transpose(ps_scores[:, c, :], fetched[:, tiles, LOADS + c], ident[:, :])
                        t.then_inc(scores_turned, 1)
                        wait_alone(pe, tails_ready, group + 1, pe_passed)
                        c = 0
                        for to, n in zip(turned_tails, (both, both, heads, heads)):
                            t = nc.tensor.transpose(to, tails[:, c:c + n], ident[0:ROWS, 0:ROWS])
                            c += n
                        t.then_inc(tails_turned, 1)
                        wait_alone(pe, carry_ready, group + 1, pe_passed)
                        nc.tensor.transpose(turned_carry[:, 0:both], carry[:, 0:ROWS], ident[0:both, 0:both])
                        nc.tensor.transpose(turned_carry[:, both:3 * heads], carry_back[:, 1:ROWS + 1],
                                            ident[0:heads, 0:heads]).then_inc(carry_turned, 1)
                        wait_alone(pe, weights_ready, group + 1, pe_passed)
                        for h in range(heads):
                            nc.tensor.transpose(turned_weights[:, h, :], weight[:, h, :], ident[0:ROWS, 0:ROWS])
                        nc.tensor.matmul(ps_factor, keep["ones"][0:1, 0:LOADS], factor[:, :], start=True, stop=True
                                         ).then_inc(weights_turned, 1)
                        for r in range(ROWS):
                            pe.wait_ge(onehot_ready, group * ROWS + (r + 1))
                            pe.wait_ge(added, group * ROWS + (r + 1))
                            nc.tensor.matmul(ps_sum[r % SLOTS][0:LOADS, 0:heads * P],
                                             fetched[:, half * ROWS + r, 0:LOADS],
                                             onehot[:, r % SLOTS].rearrange("p h c -> p (h c)"),
                                             start=True, stop=True).then_inc(summed, 1)

        @block.scalar
        def _(act):
            groups = None if count is None else act.value_load(count, min_val=1, max_val=GROUPS)
            with act.Fori(0, GROUPS) as group:
                with only_if(act, group, groups):
                    act.wait_ge(exponents_ready, group + 1)
                    nc.scalar.activation(factor[:, :], old[:, :], ACT.Exp)
                    nc.scalar.activation(weight[:, :, :], z[:, :, :], ACT.Exp).then_inc(weights_ready, 1)
                    nc.scalar.copy(places_now[:, :], keep["places"][:, bass.ds(group * ROWS, ROWS)])
                    act.wait_ge(weights_turned, group + 1)
                    nc.scalar.copy(weights_now[:, :, :], turned_weights).then_inc(weights_copied, 1)

        @block.vector
        def _(dve):
            v = nc.vector
            v.memset(carry[:, :], NEG)
            v.memset(carry_back[:, :], NEG)
            v.memset(acc[:, :, :], 0.0).then_inc(added, SLOTS)
            dve.wait_ge(added, SLOTS)
            steps = 24 + 6 * heads
            groups = None if count is None else dve.value_load(count, min_val=1, max_val=GROUPS)
            with dve.Fori(0, GROUPS) as group:
                with only_if(dve, group, groups):
                    mine = Steps(dve, step, group * steps)
                    starts, ends, others = (keep[x][:, bass.ds(group, 1), :].rearrange("r o e -> r (o e)")
                                            for x in ("starts", "ends", "others"))
                    dve.wait_ge(scores_turned, group + 1)
                    src_scores = ps_scores[:, 0:heads, :]
                    mine.did(v.tensor_tensor(own_loop[:, :, :], ps_scores[:, heads:both, :],
                                             keep["others"][:, bass.ds(group, 1), :].to_broadcast([ROWS, heads, P]),
                                             ALU.add))
                    mine.did(v.tensor_tensor_scan(first[:, :], starts, starts, 0.0, ALU.min, ALU.min))
                    mine.did(v.tensor_tensor_scan(last[:, ::-1], ends, ends, 0.0, ALU.min, ALU.min))
                    for h in range(heads):
                        mine.did(v.tensor_tensor_scan(forth[:, h, :], starts, ps_scores[:, h, :], NEG, ALU.add, ALU.max))
                        mine.did(v.tensor_tensor_scan(back[:, h, ::-1], ends, ps_scores[:, h, ::-1], NEG,
                                                      ALU.add, ALU.max))
                    mine.settle()
                    for h in range(heads):
                        mine.did(v.tensor_tensor_scan(forth[:, heads + h, :], starts, own_loop[:, h, :], NEG,
                                                      ALU.add, ALU.max))
                    mine.settle()
                    mine.did(v.tensor_copy(tails[:, 0:both], forth[:, :, P - 1]))
                    mine.did(v.tensor_copy(tails[:, both:2 * both], first[:, P - 1:P].to_broadcast([ROWS, both])))
                    mine.did(v.tensor_copy(tails[:, 2 * both:2 * both + heads], back[:, :, 0]))
                    mine.did(v.tensor_copy(tails[:, 2 * both + heads:3 * both], last[:, 0:1].to_broadcast([ROWS, heads])))
                    mine.settle()
                    dve.sem_inc(tails_ready, 1)
                    dve.wait_ge(tails_turned, group + 1)
                    mine.did(v.tensor_copy(tails_forth[:, :], ps_small[0:both, 0:2 * ROWS]))
                    mine.did(v.tensor_copy(tails_back[:, :], ps_small[0:heads, 2 * ROWS:4 * ROWS]))
                    mine.settle()
                    mine.did(v.tensor_tensor_scan(carry[:, 1:ROWS + 1], tails_forth[:, ROWS:2 * ROWS],
                                                  tails_forth[:, 0:ROWS], carry[:, 0:1], ALU.add, ALU.max))
                    mine.did(v.tensor_tensor_scan(carry_back[:, 0:ROWS][:, ::-1], tails_back[:, ROWS:2 * ROWS][:, ::-1],
                                                  tails_back[:, 0:ROWS][:, ::-1], NEG, ALU.add, ALU.max))
                    mine.settle()
                    dve.sem_inc(carry_ready, 1)
                    dve.wait_ge(carry_turned, group + 1)
                    mine.did(v.tensor_copy(carry[:, 0:1], carry[:, ROWS:ROWS + 1]))
                    mine.did(v.tensor_copy(carried[:, :], turned_carry))
                    mine.settle()
                    for h in range(heads):
                        for to, gate, col, of in ((top[:, h], first, h, forth[:, h]),
                                                  (dst_score[:, h], first, heads + h, forth[:, heads + h]),
                                                  (back[:, h], last, both + h, back[:, h])):
                            mine.did(v.scalar_tensor_tensor(out=to, in0=gate[:, :], scalar=carried[:, col:col + 1],
                                                            in1=of, op0=ALU.add, op1=ALU.max))
                    mine.settle()
                    mine.did(v.tensor_tensor(top[:, :, :], top[:, :, :], back[:, :, :], ALU.max))
                    mine.did(v.tensor_tensor(z[:, :, :], src_scores, dst_score[:, :, :], ALU.add))
                    mine.did(v.tensor_tensor(old[:, :], carried[0:1, 0:heads], dst_score[0:1, :, 0], ALU.add))
                    mine.settle()
                    mine.did(v.tensor_tensor(top[:, :, :], top[:, :, :], dst_score[:, :, :], ALU.add))

                    def leaky(x):
                        mine.did(v.scalar_tensor_tensor(out=x, in0=x, scalar=SLOPE, in1=x, op0=ALU.mult, op1=ALU.max))

                    leaky(z[:, :, :])
                    leaky(old[:, :])
                    mine.settle()
                    leaky(top[:, :, :])
                    mine.settle()
                    mine.did(v.tensor_tensor(z[:, :, :], z[:, :, :], top[:, :, :], ALU.subtract))
                    mine.did(v.tensor_tensor(old[:, :], old[:, :], top[0:1, :, 0], ALU.subtract))
                    mine.settle()
                    mine.then(v.tensor_scalar(old[:, :], old[:, :], 0.0, None, ALU.min))
                    dve.sem_inc(exponents_ready, 1)
                    dve.wait_ge(weights_copied, group + 1)
                    for r in range(ROWS + 2):
                        if r < ROWS:
                            if r % REG_BATCH == 0:
                                _, batch = nc.values_load_multi_w_load_instructions(
                                    keep["window"][0:1, bass.ds(group * ROWS + r, REG_BATCH)],
                                    engines=[mybir.EngineType.DVE], min_val=0, max_val=WIDTH - P,
                                    skip_runtime_bounds_check_because="nodes are below NODES")
                                at = {} if r == 0 else at
                                at |= {r + n: x for n, x in enumerate(batch)}
                            if r == 0:
                                first_col = acc[:, :, bass.ds(at[0], 1)]
                                mine.then(v.tensor_tensor(first_col, first_col, ps_factor.unsqueeze(2), ALU.mult))
                            for h in range(heads):
                                t = v.tensor_scalar(onehot[:, r % SLOTS, h, :], keep["lane"][:, :],
                                                    places_now[:, r:r + 1], weights_now[:, h, r:r + 1],
                                                    ALU.is_equal, ALU.mult)
                            t.then_inc(onehot_ready, 1)
                        if r >= 2:
                            q = r - 2
                            dve.wait_ge(summed, group * ROWS + (2 * ROWS + q + 1))
                            dve.wait_ge(added, group * ROWS + (SLOTS + q))
                            to = acc[:, :, bass.ds(at[q], P)]
                            v.tensor_tensor(to, to, ps_sum[q % SLOTS][0:LOADS, 0:heads * P].rearrange(
                                "p (h c) -> p h c", h=heads), ALU.add).then_inc(added, 1)
                    assert mine.n == steps, mine.n


def update_nodes(nc, dram, keep, acc):
    with ExitStack() as stack:
        m = Mem(nc, stack, "update")
        spread = m.sbuf("spread", [P, HEADS1 * WIDTH // P])
        weights = m.sbuf("weights", [P, CHUNK * P])
        mean = m.sbuf("mean", [P, CHUNK * P])
        above = m.sbuf("above", [P, CHUNK * P])
        below = m.sbuf("below", [P, CHUNK * P])
        g = m.sbuf("g", [P, CHUNK * P])
        rows = m.sbuf("rows", [P, CHUNK, ROW2])
        ps_sums = m.psum("ps_sums", [P, CHUNK * P])
        ps_weights = m.psum("ps_weights", [P, CHUNK * P])
        ps_rows = m.psum("ps_rows", [P, CHUNK, P])

        spread_in = m.sem("spread_in")
        eps_added = m.sem("eps_added")
        inverted = m.sem("inverted")
        inverses_in = m.sem("inverses_in")
        sums_ready = m.sem("sums_ready")
        weights_copied = m.sem("weights_copied")
        divided = m.sem("divided")
        below_ready = m.sem("below_ready")
        parts_ready = m.sem("parts_ready")
        g_ready = m.sem("g_ready")
        rows_ready = m.sem("rows_ready")
        rows_copied = m.sem("rows_copied")
        rows_free = m.sem("rows_free")
        ones_set = m.sem("ones_set")
        stored = m.sem("stored")
        block = stack.enter_context(nc.Block())

        @block.tensor
        def _(pe):
            def sums(i):
                cols = bass.ds(i * (CHUNK * P), CHUNK * P)
                for h in range(HEADS1):
                    nc.tensor.matmul(ps_sums[:, :], keep["w1z"][:, h, :], acc[:, h, cols],
                                     start=(h == 0), stop=(h == HEADS1 - 1))
                for h in range(HEADS1):
                    t = nc.tensor.matmul(ps_weights[:, :], keep["sel"][:, h, :], acc[:, h, cols],
                                         start=(h == 0), stop=(h == HEADS1 - 1))
                t.then_inc(sums_ready, 1)

            def rows_of(i):
                pe.wait_ge(g_ready, i + 1)
                for b in range(CHUNK):
                    t = nc.tensor.matmul(ps_rows[:, b, 0:ROW2], g[:, b * P:(b + 1) * P], keep["w2ext"][:, :],
                                         start=True, stop=True)
                t.then_inc(rows_ready, 1)

            pe.wait_ge(inverses_in, 16)
            sums(0)
            with pe.Fori(0, CHUNKS - 1) as i:
                pe.wait_ge(divided, i + 1)
                sums(i + 1)
                rows_of(i)
            rows_of(CHUNKS - 1)

        @block.vector
        def _(dve):
            v = nc.vector
            v.memset(rows[:, :, D:D + 1], 1.0).then_inc(ones_set, 1)
            dve.wait_ge(spread_in, 16)
            v.tensor_scalar(spread[:, :], spread[:, :], EPS, None, ALU.add).then_inc(eps_added, 1)
            dve.wait_ge(eps_added, 1)
            v.reciprocal(spread[:, :], spread[:, :]).then_inc(inverted, 1)
            with dve.Fori(0, CHUNKS) as i:
                dve.wait_ge(weights_copied, i + 1)
                v.tensor_tensor(mean[:, :], ps_sums[:, :], weights[:, :], ALU.mult).then_inc(divided, 1)
                dve.wait_ge(divided, i + 1)
                v.tensor_scalar(below[:, :], mean[:, :], keep["b1"][:, 0:1], 0.0, ALU.add, ALU.min
                                ).then_inc(below_ready, 1)
                dve.wait_ge(parts_ready, i + 1)
                v.scalar_tensor_tensor(out=g[:, :], in0=below[:, :], scalar=-1.0, in1=above[:, :],
                                       op0=ALU.add, op1=ALU.add).then_inc(g_ready, 1)

        @block.scalar
        def _(act):
            def copy_rows(i):
                act.wait_ge(rows_ready, i + 1)
                act.wait_ge(rows_free, i + 1)
                nc.scalar.copy(rows[:, :, 0:D], ps_rows[:, :, 0:D])
                nc.scalar.copy(rows[:, :, LOADS:ROW2], ps_rows[:, :, LOADS:ROW2]).then_inc(rows_copied, 1)

            def inverses(i):
                act.wait_ge(sums_ready, i + 1)
                nc.scalar.copy(weights[:, :], ps_weights[:, :]).then_inc(weights_copied, 1)

            def parts(i):
                act.wait_ge(below_ready, i + 1)
                nc.scalar.activation(above[:, :], mean[:, :], ACT.Relu, bias=keep["b1"][:, 0:1])
                nc.scalar.activation(below[:, :], below[:, :], ACT.Exp).then_inc(parts_ready, 1)

            act.wait_ge(ones_set, 1)
            inverses(0)
            parts(0)
            with act.Fori(0, CHUNKS - 1) as i:
                inverses(i + 1)
                copy_rows(i)
                parts(i + 1)
            copy_rows(CHUNKS - 1)

        @block.sync
        def _(sp):
            weights_row = acc[D:D + 1, :, :].rearrange("o h n -> o (h n)").rearrange("o (p c) -> o p c", p=P)
            sp.dma_start(spread[:, :], weights_row).then_inc(spread_in, 16)
            sp.wait_ge(inverted, 1)
            sp.dma_start(weights_row, spread[:, :]).then_inc(inverses_in, 16)
            sp.sem_inc(rows_free, 1)
            table = dram["table2"].rearrange("(n b p) c -> p n b c", b=CHUNK, p=P)
            with sp.Fori(0, CHUNKS) as i:
                sp.wait_ge(rows_copied, i + 1)
                sp.dma_start(table[:, bass.ds(i, 1)].rearrange("p o b c -> p (o b) c"), rows[:, :, :]
                             ).then_inc(stored, 16)
                sp.wait_ge(stored, 16 * (i + 1))
                sp.sem_inc(rows_free, 1)


def finish_nodes(nc, dram, keep, acc):
    with ExitStack() as stack:
        m = Mem(nc, stack, "finish")
        part = m.sbuf("part", [LOADS, CHUNK * P])
        weights = m.sbuf("weights", [P, CHUNK])
        mean = m.sbuf("mean", [P, CHUNK, D])
        rows = m.sbuf("rows", [P, CHUNK, D])
        turned = m.psum("turned", [P, CHUNK, P])

        part_ready = m.sem("part_ready")
        part_turned = m.sem("part_turned")
        step = m.sem("step")
        divided = m.sem("divided")
        rows_ready = m.sem("rows_ready")
        rows_free = m.sem("rows_free")
        pe_passed = m.sem("pe_passed")
        stored = m.sem("stored")
        block = stack.enter_context(nc.Block())

        @block.scalar
        def _(act):
            act.sem_inc(part_turned, 1)
            with act.Fori(0, CHUNKS) as i:
                act.wait_ge(part_turned, i + 1)
                nc.scalar.copy(part[:, :], acc[:, 0, bass.ds(i * (CHUNK * P), CHUNK * P)]).then_inc(part_ready, 1)

        @block.tensor
        def _(pe):
            pe.sem_inc(divided, 1)
            with pe.Fori(0, CHUNKS) as i:
                wait_alone(pe, divided, i + 1, pe_passed)
                wait_alone(pe, part_ready, i + 1, pe_passed)
                for b in range(CHUNK):
                    t = nc.tensor.transpose(turned[:, b, 0:LOADS], part[:, b * P:(b + 1) * P],
                                            keep["ident"][0:LOADS, 0:LOADS])
                t.then_inc(part_turned, 1)

        @block.vector
        def _(dve):
            v = nc.vector
            with dve.Fori(0, CHUNKS) as i:
                dve.wait_ge(part_turned, i + 2)
                v.tensor_scalar(weights[:, :], turned[:, :, D], EPS, None, ALU.add).then_inc(step, 1)
                dve.wait_ge(step, 2 * i + 1)
                v.reciprocal(weights[:, :], weights[:, :]).then_inc(step, 1)
                dve.wait_ge(step, 2 * i + 2)
                v.tensor_tensor(mean[:, :, :], turned[:, :, 0:D],
                                weights[:, :].unsqueeze(2).to_broadcast([P, CHUNK, D]), ALU.mult
                                ).then_inc(divided, 1)
                dve.wait_ge(divided, i + 2)
                dve.wait_ge(rows_free, i + 1)
                v.tensor_tensor(rows[:, :, :], mean[:, :, :],
                                keep["b2"][:, :].unsqueeze(1).to_broadcast([P, CHUNK, D]), ALU.add
                                ).then_inc(rows_ready, 1)

        @block.sync
        def _(sp):
            sp.sem_inc(rows_free, 1)
            nodes = dram["nodes"].rearrange("(n b p) c -> p n b c", b=CHUNK, p=P)
            with sp.Fori(0, CHUNKS) as i:
                sp.wait_ge(rows_ready, i + 1)
                sp.dma_start(nodes[:, bass.ds(i, 1)].rearrange("p o b c -> p (o b) c"), rows[:, :, :]
                             ).then_inc(stored, 16)
                sp.wait_ge(stored, 16 * (i + 1))
                sp.sem_inc(rows_free, 1)


def dense_layer(nc, dram, keep, out):
    with ExitStack() as stack:
        m = Mem(nc, stack, "dense")
        tiles = BATCH // P
        parts = CTX + 1
        deep = parts * D // P
        cols = 500
        pieces = 5
        span = cols * pieces
        spans = NODES // span
        per_span = tiles * pieces
        ring = 4
        raw = m.sbuf("raw", [P, deep, span])
        w_high = m.sbuf("w_high", [P, 2, deep, span], F32R)
        w_low = m.sbuf("w_low", [P, 2, deep, span], F32R)
        fc_b = m.sbuf("fc_b", [P, 2, span])
        x_high = m.sbuf("x_high", [P, deep, BATCH], F32R)
        x_low = m.sbuf("x_low", [P, deep, BATCH], F32R)
        results = m.sbuf("results", [P, ring, span])
        idx = m.sbuf("idx", [P, tiles * parts], I32)
        place = m.sbuf("place", [P, tiles * parts])
        below = m.sbuf("below", [P, tiles * parts])
        gathered = m.sbuf("gathered", [P, 2, parts * D])
        turned = [m.psum(f"turned{s}", [P, 2 * deep, P]) for s in range(2)]
        ps = [m.psum(f"ps{s}", [P, 512]) for s in range(pieces)]

        piece_in = [m.sem(f"piece_in{s}") for s in range(pieces)]
        span_in = m.sem("span_in")
        bias_in = [m.sem("bias_in_even"), m.sem("bias_in_odd")]
        idx_in = m.sem("idx_in")
        step = m.sem("step")
        idx_ready = m.sem("idx_ready")
        landed = [m.sem("landed_even"), m.sem("landed_odd")]
        x_turned = m.sem("x_turned")
        x_high_ready = m.sem("x_high_ready")
        x_split = m.sem("x_split")
        w_high_ready = m.sem("w_high_ready")
        w_split = m.sem("w_split")
        product = m.sem("product")
        biased = m.sem("biased")
        stored = [m.sem(f"stored{s}") for s in range(ring)]
        block = stack.enter_context(nc.Block())
        out_v = out.rearrange("(p t) c -> p t c", t=tiles)
        w_v = dram["fc_w"].rearrange("(k p) n -> p k n", p=P)

        def piece(s):
            return slice(s * cols, (s + 1) * cols)

        @block.sync
        def _(sp):
            sp.dma_start(idx[:, 0:tiles], dram["user_idx"].rearrange("(p t) -> p t", p=P)).then_inc(idx_in, 16)
            sp.dma_start(idx[:, tiles:], dram["ctx_idx"].rearrange("(p t) c -> p (t c)", p=P)).then_inc(idx_in, 16)
            for s in range(pieces):
                sp.dma_start(raw[:, :, piece(s)], w_v[:, :, piece(s)]).then_inc(piece_in[s], 16)
            with sp.Fori(0, spans) as c:
                for t in range(tiles):
                    sp.wait_ge(biased, c * per_span + (t + 1) * pieces)
                    sp.dma_start(out_v[:, t, bass.ds(c * span, span)], results[:, t % ring, :]
                                 ).then_inc(stored[t % ring], 16)
            for s in range(ring):
                sp.wait_ge(stored[s], 16 * spans * tiles // ring)

        @block.scalar
        def _(act):
            def load_bias(c, slot):
                act.dma_start(fc_b[:, slot, :], dram["fc_b"].rearrange("(o n) -> o n", o=1)[:, bass.ds(c * span, span)]
                              .to_broadcast([P, span])).then_inc(bias_in[slot], 16)

            def load_span(c):
                act.wait_ge(w_split, c * pieces)
                act.dma_start(raw[:, :, :], w_v[:, :, bass.ds(c * span, span)]).then_inc(span_in, 16)

            def high_parts(slot, pieces_now=range(pieces)):
                for s in pieces_now:
                    nc.scalar.copy(w_high[:, slot, :, piece(s)], raw[:, :, piece(s)]).then_inc(w_high_ready, 1)

            def next_span(c, slot, last=False):
                act.wait_ge(biased, (c - 1) * per_span)
                load_bias(c, slot)
                act.wait_ge(span_in, 16 * c)
                high_parts(slot)
                if not last:
                    load_span(c + 1)

            load_bias(0, 0)
            for s in range(pieces):
                act.wait_ge(piece_in[s], 16)
                high_parts(0, [s])
            load_span(1)
            load_bias(1, 1)
            for t in range(tiles):
                if t == tiles // 2:
                    act.wait_ge(span_in, 16)
                    high_parts(1)
                act.wait_ge(x_turned, t + 1)
                nc.scalar.copy(x_high[:, :, t * P:(t + 1) * P], turned[t % 2][:, 0:deep]).then_inc(x_high_ready, 1)
            load_span(2)
            with act.Fori(0, (spans - 3) // 2) as i:
                next_span(2 * i + 2, 0)
                next_span(2 * i + 3, 1)
            next_span(spans - 1, 0, last=True)

        @block.vector
        def _(dve):
            v = nc.vector
            mine = Steps(dve, step)
            dve.wait_ge(idx_in, 32)
            clamp_indices(v, mine, idx, place, below)
            v.tensor_copy(idx[:, :], place[:, :]).then_inc(idx_ready, 1)

            def low_part(c, slot, s):
                dve.wait_ge(w_high_ready, c * pieces + (s + 1))
                v.tensor_tensor(w_low[:, slot, :, piece(s)], raw[:, :, piece(s)],
                                w_high[:, slot, :, piece(s)].bitcast(F32), ALU.subtract).then_inc(w_split, 1)

            def split_x(t):
                dve.wait_ge(x_high_ready, t + 1)
                v.tensor_tensor(x_low[:, :, t * P:(t + 1) * P], turned[t % 2][:, 0:deep],
                                x_high[:, :, t * P:(t + 1) * P].bitcast(F32), ALU.subtract).then_inc(x_split, 1)

            def add_bias(c, slot, first=False, last=False):
                dve.wait_ge(bias_in[slot], 8 * (c - slot) + 16)
                for t in range(tiles):
                    if first and t + 1 < tiles:
                        split_x(t + 1)
                    for s in range(pieces):
                        dve.wait_ge(product, c * per_span + (t * pieces + s + 1))
                        if s == 0 and not (first and t < ring):
                            dve.wait_ge(stored[t % ring], 16 * (c * (tiles // ring) + t // ring))
                        v.tensor_tensor(results[:, t % ring, piece(s)], ps[s][:, 0:cols], fc_b[:, slot, piece(s)],
                                        ALU.add).then_inc(biased, 1)
                    if not last and t >= tiles - pieces - 1 and t < tiles - 1:
                        low_part(c + 1, 1 - slot, t - (tiles - pieces - 1))

            for s in range(pieces):
                low_part(0, 0, s)
            split_x(0)
            add_bias(0, 0, first=True)
            with dve.Fori(0, (spans - 3) // 2) as i:
                add_bias(2 * i + 1, 1)
                add_bias(2 * i + 2, 0)
            add_bias(spans - 2, 1)
            add_bias(spans - 1, 0, last=True)

        @block.gpsimd
        def _(pool):
            pool.wait_ge(idx_ready, 1)
            for t in range(tiles):
                if t >= 2:
                    pool.wait_ge(x_turned, t - 1)
                for c in range(parts):
                    col = tiles + t * CTX + c - 1 if c else t
                    nc.gpsimd.indirect_dma_start(
                        gathered[:, t % 2, c * D:(c + 1) * D], None, dram["user"] if c == 0 else dram["nodes"],
                        bass.IndirectOffsetOnAxis(ap=idx[:, col:col + 1], axis=0)).then_inc(landed[t % 2], 16)

        @block.tensor
        def _(pe):
            def turn_x(t):
                pe.wait_ge(landed[t % 2], 16 * parts * (t // 2 + 1))
                if t >= 2:
                    pe.wait_ge(x_split, t - 1)
                for k in range(deep):
                    q = nc.tensor.transpose(turned[t % 2][:, k, :], gathered[:, t % 2, k * P:(k + 1) * P],
                                            keep["ident"][:, :])
                q.then_inc(x_turned, 1)

            def products(c, slot, first=False):
                if not first:
                    pe.wait_ge(w_split, (c + 1) * pieces)
                for t in range(tiles):
                    if first:
                        if t + 1 < tiles:
                            turn_x(t + 1)
                        pe.wait_ge(x_split, t + 1)
                    for s in range(pieces):
                        if first and t == 0:
                            pe.wait_ge(w_split, s + 1)
                        if not (first and t == 0):
                            pe.wait_ge(biased, c * per_span + ((t - 1) * pieces + s + 1))
                        own = slice(t * P, (t + 1) * P)
                        terms = [(a, b, k) for k in range(deep)
                                 for a, b in ((x_low, w_high), (x_high, w_low), (x_high, w_high))]
                        for n, (a, b, k) in enumerate(terms):
                            q = nc.tensor.matmul(ps[s][:, 0:cols], a[:, k, own], b[:, slot, k, piece(s)],
                                                 start=(n == 0), stop=(n == len(terms) - 1))
                        q.then_inc(product, 1)

            turn_x(0)
            products(0, 0, first=True)
            with pe.Fori(0, (spans - 3) // 2) as i:
                products(2 * i + 1, 1)
                products(2 * i + 2, 0)
            products(spans - 2, 1)
            products(spans - 1, 0)


INPUTS = ["r_user_idx", "r_context_idx", "L0_rec_edge_index", "L0_rec_user_emb", "L0_rec_service_emb",
          "L0_rec_W1", "L0_rec_att_src1", "L0_rec_att_dst1", "L0_rec_b1", "L0_rec_W2", "L0_rec_att_src2",
          "L0_rec_att_dst2", "L0_rec_b2", "L0_rec_fc_w", "L0_rec_fc_b"]
SHAPES = {"r_user_idx": ([BATCH], I32), "r_context_idx": ([BATCH, CTX], I32), "L0_rec_edge_index": ([2, EDGES], I32),
          "L0_rec_user_emb": ([NODES, D], F32), "L0_rec_service_emb": ([NODES, D], F32),
          "L0_rec_W1": ([D, 2 * D], F32), "L0_rec_att_src1": ([2, D], F32), "L0_rec_att_dst1": ([2, D], F32),
          "L0_rec_b1": ([2 * D], F32), "L0_rec_W2": ([2 * D, D], F32), "L0_rec_att_src2": ([1, D], F32),
          "L0_rec_att_dst2": ([1, D], F32), "L0_rec_b2": ([D], F32), "L0_rec_fc_w": ([4 * D, NODES], F32),
          "L0_rec_fc_b": ([NODES], F32)}


def declare(nc):
    def inp(n):
        return nc.dram_tensor(f"in_{n}", SHAPES[n][0], SHAPES[n][1], kind="ExternalInput").ap()
    a = {n: inp(n) for n in INPUTS}
    d = {"edges": a["L0_rec_edge_index"], "W1": a["L0_rec_W1"], "W2": a["L0_rec_W2"], "b1": a["L0_rec_b1"],
         "b2": a["L0_rec_b2"], "att_src1": a["L0_rec_att_src1"], "att_dst1": a["L0_rec_att_dst1"],
         "att_src2": a["L0_rec_att_src2"], "att_dst2": a["L0_rec_att_dst2"], "service": a["L0_rec_service_emb"],
         "user": a["L0_rec_user_emb"], "fc_w": a["L0_rec_fc_w"], "fc_b": a["L0_rec_fc_b"],
         "user_idx": a["r_user_idx"], "ctx_idx": a["r_context_idx"]}
    d["out"] = nc.dram_tensor("out", [BATCH, NODES], F32, kind="ExternalOutput").ap()
    for name, shape, dt in (("keys", [1 + P * COLS], I32), ("window", [2, TILES], I32),
                            ("tile_keys", [TILES + 1, P + 2], I32), ("needed", [1 + NEED_HIGH * P, 1], F32),
                            ("table1", [NODES, ROW1], F32),
                            ("table2", [WIDTH, ROW2], F32), ("nodes", [WIDTH, D], F32)):
        d[name] = nc.dram_tensor(name, shape, dt, kind="Internal").ap()
    return d


def program(nc, dram, stop=9):
    with ExitStack() as stack:
        m = Mem(nc, stack, "all")
        keep = {
            "ident": m.sbuf("ident", [P, P]), "lane": m.sbuf("lane", [P, P]), "ones": m.sbuf("ones", [P, P]),
            "w1z": m.sbuf("w1z", [LOADS, HEADS1, P]), "sel": m.sbuf("sel", [LOADS, HEADS1, P]),
            "w2ext": m.sbuf("w2ext", [P, ROW2]), "b1": m.sbuf("b1", [P, 1]), "b2": m.sbuf("b2", [P, D]),
        }
        with ExitStack() as graph:
            m = Mem(nc, graph, "graph")
            keep |= {
                "rows": m.sbuf("rows", [P, TILES], I32),
                "places": m.sbuf("places", [P, TILES]),
                "window": m.sbuf("window", [1, TILES], I32),
                "chosen": m.sbuf("chosen", [ROWS, GROUPS], I32),
                "chosen_groups": m.sbuf("chosen_groups", [1, 1], I32),
                "starts": m.sbuf("starts", [ROWS, GROUPS, P], BF16),
                "ends": m.sbuf("ends", [ROWS, GROUPS, P], BF16),
                "others": m.sbuf("others", [ROWS, GROUPS, P], BF16),
            }
            weights_and_sort(nc, dram, keep)
            if stop == 1:
                return
            index_tiles(nc, dram, keep, "index1")
            choose_tiles(nc, dram, keep)
            if stop == 2:
                dumps(nc, {"dump_chosen": keep["chosen"], "dump_n": keep["chosen_groups"], "dump_idx": keep["rows"], "dump_loc": keep["places"], "dump_win": keep["window"]})
                return
            with ExitStack() as one:
                acc = Mem(nc, one, "sums1").sbuf("acc", [LOADS, HEADS1, WIDTH])
                sum_messages(nc, dram["table1"], keep, acc, HEADS1, "layer1")
                if stop == 3:
                    return dumps(nc, {"dump_acc": acc})
                update_nodes(nc, dram, keep, acc)
            if stop == 4:
                return
            index_tiles(nc, dram, keep, "index2", keep["chosen"])
            acc = Mem(nc, graph, "sums2").sbuf("acc", [LOADS, HEADS2, WIDTH])
            sum_messages(nc, dram["table2"], keep, acc, HEADS2, "layer2", keep["chosen_groups"][0:1, 0:1])
            if stop == 5:
                return dumps(nc, {"dump_acc2": acc})
            finish_nodes(nc, dram, keep, acc)
        if stop == 6:
            return
        dense_layer(nc, dram, keep, dram["out"])


def dumps(nc, what):
    with ExitStack() as st:
        s = st.enter_context(nc.semaphore("dumps"))
        block = st.enter_context(nc.Block())

        @block.sync
        def _(sp):
            for n, t in what.items():
                o = nc.dram_tensor(n, list(t.shape), t.dtype, kind="ExternalOutput").ap()
                sl = tuple(slice(None) for _ in t.shape)
                sp.dma_start(o[sl], t[sl]).then_inc(s, 16)
            sp.wait_ge(s, 16 * len(what))


def kernel(**inputs):
    import concourse.bacc as bacc
    from concourse.bass_utils import run_bass_kernel_spmd

    nc = bacc.Bacc("TRN2", target_bir_lowering=False, num_devices=1)
    program(nc, declare(nc))
    arrays = {f"in_{name}": np.ascontiguousarray(inputs[name]) for name in INPUTS}
    return run_bass_kernel_spmd(nc, [arrays], core_ids=[0]).results[0]["out"]
```

```python
from contextlib import ExitStack, contextmanager

import numpy as np

import concourse.bass as bass
from concourse import mybir

F32 = mybir.dt.float32
F32R = mybir.dt.float32r
I32 = mybir.dt.int32
BF16 = mybir.dt.bfloat16
ALU = mybir.AluOpType
ACT = mybir.ActivationFunctionType
AX = mybir.AxisListType

P = 128
NODES = 12500
EDGES = 200000
D = 64
HEADS1, HEADS2 = 2, 1
BATCH = 2048
CTX = 3
SLOPE = 0.2
EPS = 1e-16
NEG = -1e30

FIELD_BITS = 14
FIELD = (1 << FIELD_BITS) - 1
TAG = 1 << (2 * FIELD_BITS)
DUMMY = NODES << FIELD_BITS | TAG | 1
COLS = 2048
COL_BITS, PART_BITS = 11, 7
BANK = 512
IN_PARTS = 125

ROWS = 64
GROUPS = 2 * (-(-(EDGES + NODES) // (P * ROWS * 2)))
TILES = GROUPS * ROWS
CHUNK = 4
CHUNKS = -(-(NODES + P) // (CHUNK * P))
WIDTH = CHUNKS * CHUNK * P
SUBS = 4
QUARTER = P // SUBS
QUARTERS = TILES * SUBS
FIRST_GROUPS = 6
NEED_HIGH = WIDTH // P
REG_BATCH = 32
SLOTS = 4

LOADS = D + 1
ROW1 = LOADS + 2 * HEADS1
ROW2 = LOADS + 2 * HEADS2


class Mem:

    def __init__(self, nc, stack, stage):
        self.nc, self.stack, self.stage = nc, stack, stage

    def sbuf(self, name, shape, dtype=F32):
        return self.stack.enter_context(self.nc.sbuf_tensor(f"{self.stage}_{name}", shape, dtype))

    def psum(self, name, shape, dtype=F32):
        return self.stack.enter_context(self.nc.psum_tensor(f"{self.stage}_{name}", shape, dtype))

    def sem(self, name):
        return self.stack.enter_context(self.nc.semaphore(f"{self.stage}_{name}"))


class Steps:

    def __init__(self, eng, sem, base=0):
        self.eng, self.sem, self.base, self.n = eng, sem, base, 0

    def did(self, ins):
        ins.then_inc(self.sem, 1)
        self.n += 1
        return self.n

    def settle(self, n=None):
        self.eng.wait_ge(self.sem, self.base + (self.n if n is None else n))

    def then(self, ins):
        self.did(ins)
        self.settle()


def as_float(bits):
    return float(np.array(bits, np.int32).view(np.float32))


def weights_and_sort(nc, dram, keep):
    with ExitStack() as stack:
        m = Mem(nc, stack, "sort")
        key_a = m.sbuf("key_a", [P, COLS])
        key_b = m.sbuf("key_b", [P, COLS])
        src = m.sbuf("src", [IN_PARTS, EDGES // IN_PARTS], I32)
        dst = m.sbuf("dst", [IN_PARTS, EDGES // IN_PARTS], I32)
        upper = m.sbuf("upper", [P, COLS // 2])
        part = m.sbuf("part", [P, 1], I32)
        bit = m.sbuf("bit", [P, PART_BITS], I32)
        sign = m.sbuf("sign", [P, PART_BITS])
        turn = m.sbuf("turn", [P, PART_BITS + 1])
        per = NODES // IN_PARTS
        table = m.sbuf("table", [IN_PARTS, per, ROW1])
        prod = m.sbuf("prod", [IN_PARTS, per, D])
        w1 = m.sbuf("w1", [D, HEADS1 * D])
        w1t = m.sbuf("w1t", [P, D])
        att1 = m.sbuf("att1", [P, 2 * HEADS1])
        att1_wide = m.sbuf("att1_wide", [P, 2 * HEADS1, P])
        score_w = m.sbuf("score_w", [P, 2 * HEADS1, D])
        w2t = m.sbuf("w2t", [D, P])
        att2 = m.sbuf("att2", [D, 2])
        turned = m.psum("turned", [P, COLS])
        ps_w1t = m.psum("ps_w1t", [P, 512])
        ps_w2t = m.psum("ps_w2t", [P, 512])
        ps_score = m.psum("ps_score", [P, 512])
        ps_count = m.psum("ps_count", [P, 4, P])
        looks = BATCH * CTX // P
        idx = m.sbuf("idx", [P, looks], I32)
        place = m.sbuf("place", [P, looks])
        below = m.sbuf("below", [P, looks])
        low_bits = m.sbuf("low_bits", [P, looks], I32)
        high_bits = m.sbuf("high_bits", [P, looks], I32)
        low = m.sbuf("low", [P, looks])
        high = m.sbuf("high", [P, looks])
        onehot_low = m.sbuf("onehot_low", [P, looks, P], BF16)
        onehot_high = m.sbuf("onehot_high", [P, looks, P], BF16)
        part_float = m.sbuf("part_float", [P, 1])
        until = m.sbuf("until", [P, P])
        counts = m.sbuf("counts", [P, P])
        totals = m.sbuf("totals", [P, P])
        lookups = m.sbuf("lookups", [P, P, 2])
        ident = keep["ident"]

        edges_in = m.sem("edges_in")
        nodes_in = m.sem("nodes_in")
        weights_in = m.sem("weights_in")
        keys_filled = m.sem("keys_filled")
        consts = m.sem("consts")
        zeroed = m.sem("zeroed")
        step = m.sem("step")
        flipped = m.sem("flipped")
        before_turn = m.sem("before_turn")
        after_turn = m.sem("after_turn")
        upper_ready = m.sem("upper_ready")
        prepared = m.sem("prepared")
        wide = m.sem("wide")
        score_ready = m.sem("score_ready")
        pool_step = m.sem("pool_step")
        table_ready = m.sem("table_ready")
        sorted_keys = m.sem("sorted_keys")
        stored = m.sem("stored")
        idx_in = m.sem("idx_in")
        look_step = m.sem("look_step")
        onehots_ready = m.sem("onehots_ready")
        counted = m.sem("counted")
        count_copied = m.sem("count_copied")
        block = stack.enter_context(nc.Block())
        banks = COLS // BANK
        back_order = [b for h in range(banks // 2) for b in (banks // 2 + h, h)]

        def bank(b, size=BANK):
            return slice(b * size, (b + 1) * size)

        @block.sync
        def _(sp):
            sp.dma_start(dst[:, :], dram["edges"][1].rearrange("(p c) -> p c", p=IN_PARTS)).then_inc(edges_in, 16)
            sp.dma_start(src[:, :], dram["edges"][0].rearrange("(p c) -> p c", p=IN_PARTS)).then_inc(edges_in, 16)
            sp.dma_start(w1[:, :], dram["W1"]).then_inc(weights_in, 16)
            sp.dma_start(keep["w2ext"][:, 0:D], dram["W2"]).then_inc(weights_in, 16)
            sp.dma_start(keep["b1"][:, :], dram["b1"].rearrange("(c o) -> c o", o=1)).then_inc(weights_in, 16)
            sp.dma_start(keep["b2"][:, :], dram["b2"].rearrange("(o c) -> o c", o=1).to_broadcast([P, D])
                         ).then_inc(weights_in, 16)
            sp.dma_start(att2[:, 0:1], dram["att_src2"].rearrange("h d -> d h")).then_inc(weights_in, 16)
            sp.dma_start(att2[:, 1:2], dram["att_dst2"].rearrange("h d -> d h")).then_inc(weights_in, 16)
            sp.dma_start(idx[:, :], dram["ctx_idx"].rearrange("(p t) c -> p (t c)", p=P)).then_inc(idx_in, 16)
            sp.wait_ge(zeroed, 1)
            for h in range(HEADS1):
                own = slice(h * D, (h + 1) * D)
                sp.dma_start(att1[own, h:h + 1], dram["att_src1"][h:h + 1].rearrange("h d -> d h")
                             ).then_inc(weights_in, 16)
                sp.dma_start(att1[own, HEADS1 + h:HEADS1 + h + 1],
                             dram["att_dst1"][h:h + 1].rearrange("h d -> d h")).then_inc(weights_in, 16)
                sp.dma_start(keep["w1z"][0:D, h, own], dram["W1"][:, own]).then_inc(weights_in, 16)
            sp.dma_start(table[:, :, 0:D], dram["service"].rearrange("(p c) d -> p c d", p=IN_PARTS)
                         ).then_inc(nodes_in, 16)
            sp.wait_ge(table_ready, 1)
            sp.dma_start(dram["table1"].rearrange("(p c) d -> p c d", p=IN_PARTS), table[:, :, :]
                         ).then_inc(stored, 16)
            sp.wait_ge(count_copied, 3)
            sp.dma_start(dram["needed"].rearrange("(p c) o -> p (c o)", p=NEED_HIGH),
                         lookups[0:NEED_HIGH, :, :].rearrange("p c o -> p (c o)")).then_inc(stored, 16)
            sp.wait_ge(sorted_keys, 1)
            sp.dma_start(dram["keys"][1:1 + P * COLS].rearrange("(p c) -> p c", p=P), key_a[:, :].bitcast(I32)
                         ).then_inc(stored, 16)
            sp.dma_start(dram["keys"][0:1].rearrange("(p c) -> p c", p=1), key_a[P - 1:P, COLS - 1:COLS].bitcast(I32)
                         ).then_inc(stored, 16)
            sp.wait_ge(stored, 64)

        @block.gpsimd
        def _(pool):
            g = nc.gpsimd
            mine = Steps(pool, pool_step)
            mine.then(g.memset(key_a[:, :], as_float(DUMMY)))
            loops = key_a[0:IN_PARTS, EDGES // IN_PARTS:EDGES // IN_PARTS + per].bitcast(I32)
            g.iota(loops, [[1, per]], base=0, channel_multiplier=per).then_inc(keys_filled, 1)
            g.iota(part[:, :], [[0, 1]], base=0, channel_multiplier=1).then_inc(consts, 1)
            mine.then(g.memset(att1[:, :], 0.0))
            mine.then(g.memset(keep["w2ext"][:, D:D + 1], 0.0))
            mine.then(g.memset(keep["w1z"][:, :, :], 0.0))
            pool.sem_inc(zeroed, 1)
            mine.then(g.memset(keep["ones"][:, :], 1.0))
            mine.then(g.memset(ident[:, :], 0.0))
            mine.then(g.affine_select(out=ident[:, :], in_=ident[:, :], compare_op=ALU.not_equal, fill=1.0,
                                      base=0, pattern=[[-1, P]], channel_multiplier=1))
            mine.then(g.iota(keep["lane"][:, :], [[1, P]], base=0, channel_multiplier=0,
                             allow_small_or_imprecise_dtypes=True))
            pool.sem_inc(consts, 1)
            pool.wait_ge(weights_in, 16 * (6 + 3 * HEADS1))
            mine.then(g.tensor_copy(att1_wide[:, :, :],
                                    att1[:, :].unsqueeze(2).to_broadcast([P, 2 * HEADS1, P])))
            pool.sem_inc(wide, 1)
            pool.wait_ge(nodes_in, 16)
            pool.wait_ge(score_ready, 1)
            mine.then(g.memset(table[:, :, D:D + 1], 1.0))
            for c in range(2 * HEADS1):
                w = score_w[0:IN_PARTS, c:c + 1, :].to_broadcast([IN_PARTS, per, D])
                mine.then(g.tensor_tensor(prod[:, :, :], table[:, :, 0:D], w, ALU.mult))
                half = D
                while half > 1:
                    half //= 2
                    to = prod[:, :, 0:half] if half > 1 else table[:, :, LOADS + c:LOADS + c + 1]
                    mine.then(g.tensor_tensor(to, prod[:, :, 0:half], prod[:, :, half:2 * half], ALU.add))
            pool.sem_inc(table_ready, 1)

        @block.scalar
        def _(act):
            act.wait_ge(prepared, 2)
            nc.scalar.copy(w1t[:, :], ps_w1t[:, 0:D]).then_inc(prepared, 1)
            nc.scalar.copy(w2t[:, :], ps_w2t[0:D, 0:P]).then_inc(prepared, 1)
            act.wait_ge(prepared, 5)
            nc.scalar.copy(keep["w2ext"][:, LOADS:ROW2], ps_w2t[:, 256:258])
            nc.scalar.copy(score_w[:, :, :], ps_score[:, 0:2 * HEADS1 * D].rearrange(
                "p (c d) -> p c d", d=D)).then_inc(score_ready, 1)
            for n in range(1, PART_BITS + 1):
                turned_before = 2 * (n - 1) * banks
                for b in range(banks):
                    dist = 1 << (n - 1)
                    act.wait_ge(after_turn, turned_before + b + 1)
                    nc.scalar.copy(upper[:, bank(b, BANK // 2)].rearrange("p (m d) -> p m d", d=dist),
                                   turned[:, bank(b)].rearrange("p (m t d) -> p m t d", t=2, d=dist)[:, :, 1, :]
                                   ).then_inc(upper_ready, 1)
                for h in range(banks // 2):
                    act.wait_ge(after_turn, turned_before + banks + back_order.index(banks // 2 + h) + 1)
                    nc.scalar.copy(upper[:, bank(h)], turned[:, bank(banks // 2 + h)]).then_inc(upper_ready, 1)
            act.wait_ge(counted, 1)
            nc.scalar.copy(counts[:, :], ps_count[:, 0, :]).then_inc(count_copied, 1)
            act.wait_ge(counted, 2)
            nc.scalar.copy(totals[:, :], ps_count[:, 1, :]).then_inc(count_copied, 1)
            act.wait_ge(counted, 3)
            nc.scalar.copy(lookups[:, :, :].rearrange("p c o -> p o c"), ps_count[:, 2:4, :]
                           ).then_inc(count_copied, 1)

        @block.tensor
        def _(pe):
            pe.wait_ge(consts, 2)
            pe.wait_ge(weights_in, 16 * (6 + 3 * HEADS1))
            nc.tensor.transpose(ps_w1t[:, 0:D], w1[:, :], ident[0:D, 0:D]).then_inc(prepared, 1)
            nc.tensor.transpose(ps_w2t[0:D, 0:P], keep["w2ext"][:, 0:D], ident[:, :]).then_inc(prepared, 1)
            pe.wait_ge(prepared, 4)
            pe.wait_ge(wide, 1)
            for c in range(2 * HEADS1):
                nc.tensor.matmul(ps_score[:, c * D:(c + 1) * D], att1_wide[:, c, :], w1t[:, :],
                                 start=True, stop=True)
            nc.tensor.matmul(ps_w2t[:, 256:258], w2t[:, :], att2[:, :], start=True, stop=True
                             ).then_inc(prepared, 1)
            for n in range(PART_BITS):
                for way, order in enumerate((range(banks), back_order)):
                    for i, b in enumerate(order):
                        pe.wait_ge(before_turn, (2 * n + way) * banks + i + 1)
                        for c in range(b * BANK // P, (b + 1) * BANK // P):
                            if way == 0:
                                out, inp = turned[:, c * P:(c + 1) * P], key_a[:, c * P:(c + 1) * P]
                            else:
                                out, inp = turned[:, c * P:(c + 1) * P], key_b[:, c * P:(c + 1) * P]
                            last = nc.tensor.transpose(out, inp, ident[:, :])
                        last.then_inc(after_turn, 1)
            pe.wait_ge(onehots_ready, looks)
            for c in range(looks):
                t = nc.tensor.matmul(ps_count[:, 0, :], onehot_low[:, c, :], onehot_high[:, c, :],
                                     start=(c == 0), stop=(c == looks - 1))
            t.then_inc(counted, 1)
            pe.wait_ge(count_copied, 1)
            nc.tensor.matmul(ps_count[:, 1, :], counts[:, :], keep["ones"][:, :], start=True, stop=True
                             ).then_inc(counted, 1)
            pe.wait_ge(count_copied, 2)
            for to, within in ((2, keep["before"]), (3, until)):
                nc.tensor.matmul(ps_count[:, to, :], counts[:, :], within[:, :], start=True, stop=False)
                t = nc.tensor.matmul(ps_count[:, to, :], keep["before"][:, :], totals[:, :], start=False, stop=True)
            t.then_inc(counted, 1)

        @block.vector
        def _(dve):
            v = nc.vector
            mine = Steps(dve, step)
            edge_cols = slice(0, EDGES // IN_PARTS)
            loop_cols = slice(EDGES // IN_PARTS, EDGES // IN_PARTS + per)
            bits_a = key_a[0:IN_PARTS, :].bitcast(I32)
            dve.wait_ge(keys_filled, 1)
            dve.wait_ge(consts, 1)
            mine.did(v.tensor_scalar(bits_a[:, loop_cols], bits_a[:, loop_cols], FIELD_BITS, TAG,
                                     ALU.logical_shift_left, ALU.bitwise_or))
            dve.wait_ge(edges_in, 32)
            mine.did(v.tensor_scalar(dst[:, :], dst[:, :], FIELD_BITS, TAG,
                                     ALU.logical_shift_left, ALU.bitwise_or))
            mine.did(v.tensor_scalar(src[:, :], src[:, :], 1.0, None, ALU.add))
            for b in range(PART_BITS):
                mine.did(v.tensor_scalar(bit[:, b:b + 1], part[:, :], b, 1,
                                         ALU.logical_shift_right, ALU.bitwise_and))
            mine.settle()
            mine.did(v.tensor_tensor(bits_a[:, edge_cols], dst[:, :], src[:, :], ALU.bitwise_or))
            mine.then(v.tensor_scalar(sign[:, :], bit[:, :], -2.0, 1.0, ALU.mult, ALU.add))
            mine.did(v.tensor_copy(turn[:, 0:1], sign[:, 0:1]))
            mine.did(v.tensor_tensor(turn[:, 1:PART_BITS], sign[:, 1:PART_BITS], sign[:, 0:PART_BITS - 1],
                                     ALU.mult))
            mine.then(v.tensor_copy(turn[:, PART_BITS:PART_BITS + 1], sign[:, PART_BITS - 1:PART_BITS]))

            def split_lookups():
                look = Steps(dve, look_step)
                dve.wait_ge(consts, 2)
                dve.wait_ge(idx_in, 16)
                clamp_indices(v, look, idx, place, below)
                look.did(v.tensor_copy(part_float[:, :], part[:, :]))
                look.then(v.tensor_copy(idx[:, :], place[:, :]))
                look.did(v.tensor_scalar(low_bits[:, :], idx[:, :], P - 1, None, ALU.bitwise_and))
                look.then(v.tensor_scalar(high_bits[:, :], idx[:, :], P.bit_length() - 1, None,
                                          ALU.logical_shift_right))
                look.did(v.tensor_copy(low[:, :], low_bits[:, :]))
                look.did(v.tensor_copy(high[:, :], high_bits[:, :]))
                look.did(v.tensor_scalar(keep["before"][:, :], keep["lane"][:, :], part_float[:, 0:1], None,
                                         ALU.is_gt))
                look.then(v.tensor_scalar(until[:, :], keep["lane"][:, :], part_float[:, 0:1], None, ALU.is_ge))

            def onehot_lookups(part_of):
                for c in part_of:
                    v.tensor_scalar(onehot_low[:, c, :], keep["lane"][:, :], low[:, c:c + 1], None, ALU.is_equal)
                    v.tensor_scalar(onehot_high[:, c, :], keep["lane"][:, :], high[:, c:c + 1], None, ALU.is_equal
                                    ).then_inc(onehots_ready, 1)

            def compare(to, low, high, lower, upper_part):
                mine.did(v.tensor_tensor(to[lower], low, high, ALU.min))
                return v.tensor_tensor(to[upper_part], low, high, ALU.max)

            def pairs(x, dist):
                return x.rearrange("p (m t d) -> p m t d", t=2, d=dist)

            LOW, HIGH = (slice(None), slice(None), 0, slice(None)), (slice(None), slice(None), 1, slice(None))

            def exchange(to, of, dist):
                a = pairs(of[:, :], dist)
                mine.did(compare(pairs(to[:, :], dist), a[LOW], a[HIGH], LOW, HIGH))
                mine.settle()

            def exchange_then_turn(to, of, dist):
                for b in back_order:
                    a = pairs(of[:, bank(b)], dist)
                    compare(pairs(to[:, bank(b)], dist), a[LOW], a[HIGH], LOW, HIGH).then_inc(before_turn, 1)

            def exchange_turned(to, n, dist):
                for b in range(banks):
                    dve.wait_ge(upper_ready, (n - 1) * (banks + banks // 2) + b + 1)
                    high = upper[:, bank(b, BANK // 2)].rearrange("p (m d) -> p m d", d=dist)
                    mine.did(compare(pairs(to[:, bank(b)], dist), pairs(turned[:, bank(b)], dist)[LOW], high,
                                     LOW, HIGH))
                mine.settle()

            def exchange_turned_back(to, n):
                for h in range(banks // 2):
                    dve.wait_ge(upper_ready, (n - 1) * (banks + banks // 2) + banks + h + 1)
                    dve.wait_ge(after_turn, (2 * n - 1) * banks + back_order.index(h) + 1)
                    mine.did(compare(to, turned[:, bank(h)], upper[:, bank(h)],
                                     (slice(None), bank(h)), (slice(None), bank(banks // 2 + h))))
                mine.settle()

            share = looks // (2 * PART_BITS - 2)
            assert share * (2 * PART_BITS - 2) == looks
            at, other = key_a, key_b
            for k in range(1, COL_BITS):
                for j in reversed(range(k)):
                    views = [x[:, :].rearrange("p (n w m t d) -> p n w m t d", w=2, m=1 << (k - 1 - j),
                                               t=2, d=1 << j) for x in (at, other)]
                    for way in range(2):
                        a, b = (x[:, :, way] for x in views)
                        for t, op in ((0, ALU.min), (1, ALU.max)):
                            mine.did(v.tensor_tensor(b[:, :, :, t ^ way, :], a[:, :, :, 0, :],
                                                     a[:, :, :, 1, :], op))
                    mine.settle()
                    at, other = other, at
            for k in range(COL_BITS, COL_BITS + PART_BITS + 1):
                n = k - COL_BITS
                if n == 0:
                    mine.then(v.tensor_scalar(key_a[:, :], at[:, :], turn[:, 0:1], None, ALU.mult))
                    at = key_a
                else:
                    for b in range(banks):
                        v.tensor_scalar(key_a[:, bank(b)], at[:, bank(b)], turn[:, n:n + 1], None, ALU.mult
                                        ).then_inc(before_turn, 1)
                    if n == 1:
                        split_lookups()
                    else:
                        onehot_lookups(range((2 * n - 3) * share, (2 * n - 2) * share))
                    of = turned
                    for j in reversed(range(n)):
                        to = key_b if (j % 2 == 0) else key_a
                        if of is turned:
                            exchange_turned(to, n, 1 << j)
                        elif j:
                            exchange(to, of, 1 << j)
                        else:
                            exchange_then_turn(to, of, 1 << j)
                        of = to
                    if n == 1:
                        dve.sem_inc(before_turn, banks)
                    if n < PART_BITS:
                        onehot_lookups(range((2 * n - 2) * share, (2 * n - 1) * share))
                    at = turned
                for j in reversed(range(COL_BITS)):
                    to = key_a if (at is not key_a) else key_b
                    if at is turned:
                        exchange_turned_back(to, n)
                    else:
                        exchange(to, at, 1 << j)
                    at = to
            assert at is key_a
            dve.sem_inc(sorted_keys, 1)


def index_tiles(nc, dram, keep, stage, chosen=None, count=None):
    with ExitStack() as stack:
        m = Mem(nc, stack, stage)
        subs = 1 if chosen is None else SUBS
        run = P // subs
        batches = [(0, GROUPS)] if chosen is None else [(0, FIRST_GROUPS), (FIRST_GROUPS, 12), (12, 18), (18, GROUPS)]
        keys = m.sbuf("keys", [ROWS, GROUPS, subs, run + 2], I32)
        node = m.sbuf("node", [ROWS, GROUPS, subs, run + 2])
        field = m.sbuf("field", [ROWS, GROUPS, P])
        loop = m.sbuf("loop", [ROWS, GROUPS, P])
        row = m.sbuf("row", [ROWS, GROUPS, P])
        first = m.sbuf("first", [GROUPS, ROWS, subs], I32)
        turned = m.psum("turned", [P, 2, 2, ROWS])
        turned_first = m.psum("turned_first", [GROUPS, subs, ROWS])

        keys_in = [m.sem(f"keys_in{n}") for n in range(len(batches))]
        step = m.sem("step")
        rows_ready = m.sem("rows_ready")
        turned_row = m.sem("turned_row")
        copied = m.sem("copied")
        copies_out = m.sem("copies_out")
        nodes_ready = m.sem("nodes_ready")
        turned_nodes = m.sem("turned_nodes")
        first_ready = m.sem("first_ready")
        window_out = m.sem("window_out")
        window_in = m.sem("window_in")
        firsts_in = m.sem("firsts_in")
        firsts_ready = m.sem("firsts_ready")
        found_in = m.sem("found_in")
        block = stack.enter_context(nc.Block())
        group = ROWS * P
        per = QUARTERS // P
        if chosen is None:
            firsts = m.sbuf("firsts", [P, per + 1, 2], I32)

        def each_batch(eng):
            groups = None if count is None else eng.value_load(count, min_val=1, max_val=GROUPS)
            for n, (lo, hi) in enumerate(batches):
                with only_if(eng, lo, groups):
                    yield n, lo, hi

        @block.gpsimd
        def _(pool):
            if chosen is None:
                pool.wait_ge(firsts_ready, 1)
                for j in range(per + 1):
                    nc.gpsimd.indirect_dma_start(
                        keep["found"][:, j, :], None, dram["needed"],
                        bass.IndirectOffsetOnAxis(ap=firsts[:, j, 0:1], axis=0)).then_inc(found_in, 16)
                pool.wait_ge(found_in, 16 * (per + 1))
            else:
                for n, lo, hi in each_batch(pool):
                    for g in range(max(lo, FIRST_GROUPS), hi):
                        for s in range(subs):
                            nc.gpsimd.indirect_dma_start(
                                keys[:, g, s, :], None, dram["quarter_keys"],
                                bass.IndirectOffsetOnAxis(ap=chosen[:, g * subs + s:g * subs + s + 1], axis=0)
                                ).then_inc(keys_in[n], 16)

        @block.sync
        def _(sp):
            if chosen is None:
                t = dram["keys"].tensor
                sp.dma_start(firsts[:, :, :], bass.AP(tensor=t, offset=1,
                                                      ap=[[per * QUARTER, P], [QUARTER, per + 1], [1, 2]])
                             ).then_inc(firsts_in, 16)
                for half in range(2):
                    n = GROUPS // 2
                    sp.dma_start(keys[:, half * n:(half + 1) * n].rearrange("r g o e -> r g (o e)"),
                                 bass.AP(tensor=t, offset=half * n * group, ap=[[P, ROWS], [group, n], [1, P + 2]])
                                 ).then_inc(keys_in[0], 16)
                sp.dma_start(dram["quarter_keys"][0:QUARTERS, :],
                             bass.AP(tensor=t, offset=0, ap=[[QUARTER, QUARTERS], [1, QUARTER + 2]])
                             ).then_inc(copies_out, 16)
                sp.dma_start(dram["quarter_keys"][QUARTERS:QUARTERS + 1, :],
                             bass.AP(tensor=t, offset=P * COLS - QUARTER - 2, ap=[[QUARTER + 2, 1], [1, QUARTER + 2]])
                             ).then_inc(copies_out, 16)
            for n, lo, hi in each_batch(sp):
                sp.wait_ge(first_ready, n + 1)
                part = dram["window"][0:1, lo * ROWS * subs:hi * ROWS * subs]
                sp.dma_start(part.rearrange("o (g c) -> (o g) c", g=hi - lo),
                             first[0:hi - lo, :, :].rearrange("g r s -> g (r s)")).then_inc(window_out, 16)
                sp.wait_ge(window_out, 16 * (n + 1))
                sp.dma_start(keep["window"][:, lo * ROWS * subs:hi * ROWS * subs], part).then_inc(window_in, 16)
                sp.wait_ge(window_in, 16 * (n + 1))
            if chosen is None:
                sp.wait_ge(copies_out, 32)

        @block.vector
        def _(dve):
            v = nc.vector
            mine = Steps(dve, step)

            def runs(x, lo, hi):
                return x[:, lo:hi, :].rearrange("r g (s e) -> r g s e", s=subs)

            if chosen is None:
                dve.wait_ge(firsts_in, 16)
                v.tensor_scalar(firsts[:, :, :], firsts[:, :, :], FIELD_BITS, FIELD, ALU.logical_shift_right,
                                ALU.bitwise_and).then_inc(firsts_ready, 1)
            for n, lo, hi in each_batch(dve):
                if chosen is None:
                    dve.wait_ge(keys_in[n], 32)
                elif n:
                    dve.wait_ge(keys_in[n], 16 * (hi - lo) * subs)
                keys_now = keep["first_keys"] if chosen is not None and n == 0 else keys[:, lo:hi]
                keys_now, node_now = keys_now[:, :, :, :], node[:, lo:hi]
                field_now, loop_now, row_now = field[:, lo:hi, :], loop[:, lo:hi, :], row[:, lo:hi, :]
                mine.then(v.tensor_scalar(runs(field, lo, hi).bitcast(I32), keys_now[:, :, :, 1:run + 1], FIELD, None,
                                          ALU.bitwise_and))
                mine.then(v.tensor_scalar(keys_now, keys_now, FIELD_BITS, FIELD,
                                          ALU.logical_shift_right, ALU.bitwise_and))
                mine.did(v.tensor_copy(node_now, keys_now))
                mine.then(v.tensor_copy(row_now, field_now.bitcast(I32)))
                dve.sem_inc(nodes_ready, 1)
                own = node_now[:, :, :, 1:run + 1]
                starts, ends, others = (keep[x][:, lo:hi, :] for x in ("starts", "ends", "others"))
                mine.did(v.tensor_tensor(runs(keep["starts"], lo, hi), own, node_now[:, :, :, 0:run], ALU.not_equal))
                mine.did(v.tensor_tensor(runs(keep["ends"], lo, hi)[:, :, ::-1, ::-1], own,
                                         node_now[:, :, :, 2:run + 2], ALU.not_equal))
                mine.then(v.tensor_scalar(loop_now, row_now, 0.0, None, ALU.is_equal))
                mine.did(v.tensor_scalar(starts, starts, NEG, None, ALU.mult))
                mine.did(v.tensor_scalar(ends, ends, NEG, None, ALU.mult))
                mine.did(v.tensor_scalar(others, loop_now, -NEG, NEG, ALU.mult, ALU.add))
                mine.did(v.scalar_tensor_tensor(out=runs(field, lo, hi), in0=own, scalar=1.0,
                                                in1=runs(loop, lo, hi), op0=ALU.add, op1=ALU.mult))
                mine.settle()
                mine.did(v.scalar_tensor_tensor(out=row_now, in0=row_now, scalar=-1.0, in1=field_now,
                                                op0=ALU.add, op1=ALU.add))
                for s in range(subs):
                    mine.did(v.scalar_tensor_tensor(
                        out=loop_now[:, :, s * run:(s + 1) * run], in0=own[:, :, s, :], scalar=float(s * run),
                        in1=own[:, :, s, 0:1].to_broadcast([ROWS, hi - lo, run]), op0=ALU.add, op1=ALU.subtract))
                mine.settle()
                dve.sem_inc(rows_ready, 1)
                dve.wait_ge(turned_nodes, n + 1)
                if n:
                    dve.wait_ge(window_in, 16 * n)
                v.tensor_copy(first[0:hi - lo, :, :].rearrange("g r s -> g s r"), turned_first[0:hi - lo, :, :]
                              ).then_inc(first_ready, 1)
                for pair in range(lo // 2, hi // 2):
                    dve.wait_ge(turned_row, pair + 1)
                    to = slice(2 * pair * ROWS, 2 * (pair + 1) * ROWS)
                    v.tensor_copy(keep["rows"][:, to].rearrange("p (b r) -> p b r", b=2), turned[:, 0])
                    v.tensor_copy(keep["places"][:, to].rearrange("p (b r) -> p b r", b=2),
                                  turned[:, 1]).then_inc(copied, 1)

        @block.tensor
        def _(pe):
            for n, lo, hi in each_batch(pe):
                pe.wait_ge(nodes_ready, n + 1)
                if n:
                    pe.wait_ge(first_ready, n)
                for s in range(subs):
                    t = nc.tensor.transpose(turned_first[0:hi - lo, s, :], node[:, lo:hi, s, 1],
                                            keep["ident"][0:ROWS, 0:ROWS])
                t.then_inc(turned_nodes, 1)
                pe.wait_ge(rows_ready, n + 1)
                for pair in range(lo // 2, hi // 2):
                    if pair:
                        pe.wait_ge(copied, pair)
                    for what, of in enumerate((row, loop)):
                        for b in range(2):
                            last = nc.tensor.transpose(turned[:, what, b], of[:, 2 * pair + b, :],
                                                       keep["ident"][0:ROWS, 0:ROWS])
                    last.then_inc(turned_row, 1)


def clamp_indices(v, mine, idx, place, below):
    mine.then(v.tensor_copy(place[:, :], idx[:, :]))
    mine.then(v.tensor_scalar(below[:, :], place[:, :], 0.0, float(NODES), ALU.is_lt, ALU.mult))
    mine.then(v.tensor_tensor(place[:, :], place[:, :], below[:, :], ALU.add))
    mine.then(v.tensor_scalar(place[:, :], place[:, :], 0.0, float(NODES - 1), ALU.max, ALU.min))


def choose_tiles(nc, keep, m, scratch):
    per = QUARTERS // P
    list_cols = GROUPS * SUBS
    rounded = m.sbuf("rounded", [P, 1])
    tile_id = m.sbuf("tile_id", [P, per])
    flag = m.sbuf("flag", [P, per])
    position = m.sbuf("position", [P, per])
    position_bits = m.sbuf("position_bits", [P, 3, per], I32)
    quarter_bits = m.sbuf("quarter_bits", [P, per], I32)
    row_group = m.sbuf("row_group", [P, 2, per])
    value = m.sbuf("value", [P, per])
    share = per // SUBS
    in_row = scratch[:, 0:share * ROWS].rearrange("p (j r) -> p j r", j=share)
    in_group = m.sbuf("in_group", [P, share, list_cols])
    ps_choose = m.psum("ps_choose", [P, 512])
    ps_before, ps_list = ps_choose[:, 0:4], ps_choose[:, 128:128 + list_cols]

    step = m.sem("choose_step")
    consts = m.sem("consts")
    flags_ready = m.sem("flags_ready")
    flags_counted = m.sem("flags_counted")
    list_ready = m.sem("list_ready")
    listed = m.sem("listed")

    def gpsimd(pool):
        g = nc.gpsimd
        g.iota(tile_id[:, :], [[1, per]], base=0, channel_multiplier=per, allow_small_or_imprecise_dtypes=True
               ).then_inc(consts, 1)

    def tensor(pe):
        pe.wait_ge(flags_ready, 1)
        nc.tensor.matmul(ps_before[:, 1:2], keep["before"][:, :], position[:, per - 1:per], start=True, stop=True)
        nc.tensor.matmul(ps_before[:, 2:3], keep["ones"][:, :], position[:, per - 1:per], start=True, stop=True
                         ).then_inc(flags_counted, 1)
        for part in range(SUBS):
            pe.wait_ge(list_ready, part + 1)
            for j in range(share):
                t = nc.tensor.matmul(ps_list[0:ROWS, :], in_row[:, j, :], in_group[:, j, :],
                                     start=(part == 0 and j == 0), stop=(part == SUBS - 1 and j == share - 1))
            t.then_inc(listed, 1)

    def vector(dve):
        v = nc.vector
        mine = Steps(dve, step)
        mine.then(v.tensor_tensor(flag[:, :], keep["found"][:, 1:, 1], keep["found"][:, 0:per, 0], ALU.is_gt))
        mine.then(v.tensor_tensor_scan(position[:, :], keep["ones"][:, 0:per], flag[:, :], 0.0,
                                       ALU.mult, ALU.add))
        dve.sem_inc(flags_ready, 1)
        dve.wait_ge(flags_counted, 1)
        mine.did(v.tensor_scalar(rounded[:, :], ps_before[:, 2:3], float(ROWS * SUBS - 1), None, ALU.add))
        mine.then(v.tensor_scalar(position[:, :], position[:, :], ps_before[:, 1:2], -1.0, ALU.add, ALU.add))
        mine.did(v.tensor_copy(position_bits[:, 2, 0:1], rounded[:, :]))
        mine.then(v.tensor_copy(position_bits[:, 0, :], position[:, :]))
        sub_bits = SUBS.bit_length() - 1
        group_bits = sub_bits + ROWS.bit_length() - 1
        mine.did(v.tensor_scalar(keep["chosen_groups"][:, :], position_bits[0:1, 2, 0:1], group_bits, None,
                                 ALU.arith_shift_right))
        mine.did(v.tensor_scalar(position_bits[:, 1, :], position_bits[:, 0, :], group_bits, sub_bits,
                                 ALU.arith_shift_right, ALU.logical_shift_left))
        mine.did(v.tensor_scalar(quarter_bits[:, :], position_bits[:, 0, :], SUBS - 1, None, ALU.bitwise_and))
        mine.settle()
        mine.did(v.tensor_scalar(position_bits[:, 0, :], position_bits[:, 0, :], sub_bits, ROWS - 1,
                                 ALU.arith_shift_right, ALU.bitwise_and))
        mine.then(v.tensor_tensor(position_bits[:, 1, :], position_bits[:, 1, :], quarter_bits[:, :], ALU.add))
        mine.did(v.tensor_copy(row_group[:, :, :], position_bits[:, 0:2, :]))
        dve.wait_ge(consts, 1)
        mine.then(v.tensor_scalar(value[:, :], tile_id[:, :], -float(QUARTERS), None, ALU.add))
        mine.then(v.tensor_tensor(value[:, :], value[:, :], flag[:, :], ALU.mult))
        for part in range(SUBS):
            cols = slice(part * share, (part + 1) * share)
            if part:
                dve.wait_ge(listed, part)
            for to, n, what in ((in_row, ROWS, 0), (in_group, list_cols, 1)):
                mine.did(v.tensor_tensor(
                    to[:, :, :], keep["lane"][:, 0:n].unsqueeze(1).to_broadcast([P, share, n]),
                    row_group[:, what, cols].unsqueeze(2).to_broadcast([P, share, n]), ALU.is_equal))
            mine.settle()
            v.tensor_tensor(in_group[:, :, :], in_group[:, :, :],
                            value[:, cols].unsqueeze(2).to_broadcast([P, share, list_cols]), ALU.mult
                            ).then_inc(list_ready, 1)
        dve.wait_ge(listed, SUBS)
        mine.then(v.tensor_scalar(keep["chosen"][:, :], ps_list[0:ROWS, :], float(QUARTERS), None, ALU.add))

    return {"gpsimd": gpsimd, "tensor": tensor, "vector": vector}


def wait_alone(eng, sem, value, passed):
    eng.wait_ge(sem, value)
    eng.sem_inc(passed, 1)


@contextmanager
def only_if(eng, group, count):
    if count is None:
        yield
        return
    with eng.If(count > group if isinstance(group, int) else group < count):
        yield
    with eng.Else():
        eng.nop()


def sum_messages(nc, table, keep, acc, heads, stage, subs=1, count=None, meanwhile=None):
    with ExitStack() as stack:
        m = Mem(nc, stack, stage)
        both = 2 * heads
        width = LOADS + both
        run = P // subs
        lanes = acc.shape[1] // heads
        fetched = m.sbuf("fetched", [P, 2 * ROWS, width])
        rows_now = m.sbuf("rows_now", [P, 2 * ROWS], I32)
        places_now = m.sbuf("places_now", [P, ROWS])
        weights_now = m.sbuf("weights_now", [P, heads, ROWS])
        onehot = m.sbuf("onehot", [P, SLOTS, heads, P])
        own_loop = m.sbuf("own_loop", [ROWS, heads, P])
        first = m.sbuf("first", [ROWS, P])
        last = m.sbuf("last", [ROWS, P])
        forth = m.sbuf("forth", [ROWS, both, P])
        back = m.sbuf("back", [ROWS, heads, P])
        tails = m.sbuf("tails", [ROWS, 6 * heads])
        tails_forth = m.sbuf("tails_forth", [both, 2 * ROWS])
        tails_back = m.sbuf("tails_back", [heads, 2 * ROWS])
        carry = m.sbuf("carry", [both, ROWS + 1])
        carry_back = m.sbuf("carry_back", [heads, ROWS + 1])
        carried = m.sbuf("carried", [ROWS, 3 * heads])
        top = m.sbuf("top", [ROWS, heads, P])
        dst_score = m.sbuf("dst_score", [ROWS, heads, P])
        z = m.sbuf("z", [ROWS, heads, P])
        weight = m.sbuf("weight", [ROWS, heads, P])
        old = m.sbuf("old", [1, heads])
        factor = m.sbuf("factor", [1, heads])
        ps_scores = m.psum("ps_scores", [ROWS, both, P])
        ps_small = m.psum("ps_small", [P, 512])
        ps_weights = m.psum("ps_weights", [P, 512])
        ps_sum = [m.psum(f"ps_sum{s}", [P, 512]) for s in range(SLOTS)]
        turned_weights = ps_weights[:, 0:heads * ROWS].rearrange("p (h r) -> p h r", h=heads)
        turned_tails = [ps_small[0:n, c * ROWS:(c + 1) * ROWS]
                        for c, n in enumerate((both, both, heads, heads))]
        turned_carry = ps_small[0:ROWS, 4 * ROWS:4 * ROWS + 3 * heads]
        ps_factor = ps_small[0:LOADS, 5 * ROWS:5 * ROWS + heads]

        landed = [m.sem("landed_even"), m.sem("landed_odd")]
        rows_copied = m.sem("rows_copied")
        scores_turned = m.sem("scores_turned")
        tails_ready = m.sem("tails_ready")
        tails_turned = m.sem("tails_turned")
        carry_ready = m.sem("carry_ready")
        carry_turned = m.sem("carry_turned")
        exponents_ready = m.sem("exponents_ready")
        weights_ready = m.sem("weights_ready")
        weights_turned = m.sem("weights_turned")
        weights_copied = m.sem("weights_copied")
        step = m.sem("step")
        pe_passed = m.sem("pe_passed")
        pool_passed = m.sem("pool_passed")
        onehot_ready = m.sem("onehot_ready")
        summed = m.sem("summed")
        added = m.sem("added")
        meanwhile = meanwhile(nc, keep, m, onehot[:, :, :, :].rearrange("p s h c -> p (s h c)")) if meanwhile else {}
        block = stack.enter_context(nc.Block())

        @block.gpsimd
        def _(pool):
            if meanwhile:
                meanwhile["gpsimd"](pool)
            groups = None if count is None else pool.value_load(count, min_val=1, max_val=GROUPS)
            with pool.Fori(0, GROUPS // 2) as i:
                for half in range(2):
                    with only_if(pool, 2 * i + half, groups):
                        pool.wait_ge(summed, (2 * i + half + 1) * ROWS)
                        nc.gpsimd.tensor_copy(rows_now[:, half * ROWS:(half + 1) * ROWS],
                                              keep["rows"][:, bass.ds((2 * i + half) * ROWS, ROWS)]
                                              ).then_inc(rows_copied, 1)
                        wait_alone(pool, rows_copied, 2 * i + half + 1, pool_passed)
                        for r in range(half * ROWS, (half + 1) * ROWS):
                            nc.gpsimd.indirect_dma_start(
                                fetched[:, r, :], None, table,
                                bass.IndirectOffsetOnAxis(ap=rows_now[:, r:r + 1], axis=0)).then_inc(landed[half], 16)

        @block.tensor
        def _(pe):
            ident = keep["ident"]
            pe.sem_inc(summed, 2 * ROWS)
            if meanwhile:
                meanwhile["tensor"](pe)
            groups = None if count is None else pe.value_load(count, min_val=1, max_val=GROUPS)
            with pe.Fori(0, GROUPS // 2) as i:
                for half in range(2):
                    group = 2 * i + half
                    with only_if(pe, group, groups):
                        wait_alone(pe, landed[half], (i + 1) * (16 * ROWS), pe_passed)
                        tiles = slice(half * ROWS, (half + 1) * ROWS)
                        for c in range(both):
                            t = nc.tensor.transpose(ps_scores[:, c, :], fetched[:, tiles, LOADS + c], ident[:, :])
                        t.then_inc(scores_turned, 1)
                        wait_alone(pe, tails_ready, group + 1, pe_passed)
                        c = 0
                        for to, n in zip(turned_tails, (both, both, heads, heads)):
                            t = nc.tensor.transpose(to, tails[:, c:c + n], ident[0:ROWS, 0:ROWS])
                            c += n
                        t.then_inc(tails_turned, 1)
                        wait_alone(pe, carry_ready, group + 1, pe_passed)
                        nc.tensor.transpose(turned_carry[:, 0:both], carry[:, 0:ROWS], ident[0:both, 0:both])
                        nc.tensor.transpose(turned_carry[:, both:3 * heads], carry_back[:, 1:ROWS + 1],
                                            ident[0:heads, 0:heads]).then_inc(carry_turned, 1)
                        wait_alone(pe, weights_ready, group + 1, pe_passed)
                        for h in range(heads):
                            nc.tensor.transpose(turned_weights[:, h, :], weight[:, h, :], ident[0:ROWS, 0:ROWS])
                        nc.tensor.matmul(ps_factor, keep["ones"][0:1, 0:LOADS], factor[:, :], start=True, stop=True
                                         ).then_inc(weights_turned, 1)
                        for r in range(ROWS):
                            pe.wait_ge(onehot_ready, group * ROWS + (r + 1))
                            pe.wait_ge(added, (group * ROWS + (r + 1)) * subs)
                            nc.tensor.matmul(ps_sum[r % SLOTS][0:LOADS, 0:heads * P],
                                             fetched[:, half * ROWS + r, 0:LOADS],
                                             onehot[:, r % SLOTS].rearrange("p h c -> p (h c)"),
                                             start=True, stop=True).then_inc(summed, 1)

        @block.scalar
        def _(act):
            groups = None if count is None else act.value_load(count, min_val=1, max_val=GROUPS)
            with act.Fori(0, GROUPS) as group:
                with only_if(act, group, groups):
                    act.wait_ge(exponents_ready, group + 1)
                    nc.scalar.activation(factor[:, :], old[:, :], ACT.Exp)
                    nc.scalar.activation(weight[:, :, :], z[:, :, :], ACT.Exp).then_inc(weights_ready, 1)
                    nc.scalar.copy(places_now[:, :], keep["places"][:, bass.ds(group * ROWS, ROWS)])
                    act.wait_ge(weights_turned, group + 1)
                    nc.scalar.copy(weights_now[:, :, :], turned_weights).then_inc(weights_copied, 1)

        @block.vector
        def _(dve):
            v = nc.vector
            if meanwhile:
                meanwhile["vector"](dve)
            v.memset(carry[:, :], NEG)
            v.memset(carry_back[:, :], NEG)
            v.memset(acc[:, :, :], 0.0).then_inc(added, SLOTS * subs)
            dve.wait_ge(added, SLOTS * subs)
            steps = 24 + 6 * heads
            groups = None if count is None else dve.value_load(count, min_val=1, max_val=GROUPS)
            with dve.Fori(0, GROUPS) as group:
                with only_if(dve, group, groups):
                    mine = Steps(dve, step, group * steps)
                    starts, ends, others = (keep[x][:, bass.ds(group, 1), :].rearrange("r o e -> r (o e)")
                                            for x in ("starts", "ends", "others"))
                    mine.did(v.tensor_tensor_scan(first[:, :], starts, starts, 0.0, ALU.min, ALU.min))
                    mine.did(v.tensor_tensor_scan(last[:, ::-1], ends, ends, 0.0, ALU.min, ALU.min))
                    dve.wait_ge(scores_turned, group + 1)
                    src_scores = ps_scores[:, 0:heads, :]
                    mine.did(v.tensor_tensor(own_loop[:, :, :], ps_scores[:, heads:both, :],
                                             keep["others"][:, bass.ds(group, 1), :].to_broadcast([ROWS, heads, P]),
                                             ALU.add))
                    for h in range(heads):
                        mine.did(v.tensor_tensor_scan(forth[:, h, :], starts, ps_scores[:, h, :], NEG,
                                                      ALU.add, ALU.max))
                        mine.did(v.tensor_tensor_scan(back[:, h, ::-1], ends, ps_scores[:, h, ::-1], NEG,
                                                      ALU.add, ALU.max))
                    mine.settle()
                    for h in range(heads):
                        mine.did(v.tensor_tensor_scan(forth[:, heads + h, :], starts, own_loop[:, h, :], NEG,
                                                      ALU.add, ALU.max))
                    mine.settle()
                    mine.did(v.tensor_copy(tails[:, 0:both], forth[:, :, P - 1]))
                    mine.did(v.tensor_copy(tails[:, both:2 * both], first[:, P - 1:P].to_broadcast([ROWS, both])))
                    mine.did(v.tensor_copy(tails[:, 2 * both:2 * both + heads], back[:, :, 0]))
                    mine.did(v.tensor_copy(tails[:, 2 * both + heads:3 * both], last[:, 0:1].to_broadcast([ROWS, heads])
                                           ))
                    mine.settle()
                    dve.sem_inc(tails_ready, 1)
                    dve.wait_ge(tails_turned, group + 1)
                    mine.did(v.tensor_copy(tails_forth[:, :], ps_small[0:both, 0:2 * ROWS]))
                    mine.did(v.tensor_copy(tails_back[:, :], ps_small[0:heads, 2 * ROWS:4 * ROWS]))
                    mine.settle()
                    mine.did(v.tensor_tensor_scan(carry[:, 1:ROWS + 1], tails_forth[:, ROWS:2 * ROWS],
                                                  tails_forth[:, 0:ROWS], carry[:, 0:1], ALU.add, ALU.max))
                    mine.did(v.tensor_tensor_scan(carry_back[:, 0:ROWS][:, ::-1], tails_back[:, ROWS:2 * ROWS][:, ::-1],
                                                  tails_back[:, 0:ROWS][:, ::-1], NEG, ALU.add, ALU.max))
                    mine.settle()
                    dve.sem_inc(carry_ready, 1)
                    dve.wait_ge(carry_turned, group + 1)
                    mine.did(v.tensor_copy(carry[:, 0:1], carry[:, ROWS:ROWS + 1]))
                    mine.did(v.tensor_copy(carried[:, :], turned_carry))
                    mine.settle()
                    for h in range(heads):
                        for to, gate, col, of in ((top[:, h], first, h, forth[:, h]),
                                                  (dst_score[:, h], first, heads + h, forth[:, heads + h]),
                                                  (back[:, h], last, both + h, back[:, h])):
                            mine.did(v.scalar_tensor_tensor(out=to, in0=gate[:, :], scalar=carried[:, col:col + 1],
                                                            in1=of, op0=ALU.add, op1=ALU.max))
                    mine.settle()
                    mine.did(v.tensor_tensor(top[:, :, :], top[:, :, :], back[:, :, :], ALU.max))
                    mine.did(v.tensor_tensor(z[:, :, :], src_scores, dst_score[:, :, :], ALU.add))
                    mine.did(v.tensor_tensor(old[:, :], carried[0:1, 0:heads], dst_score[0:1, :, 0], ALU.add))
                    mine.settle()
                    mine.did(v.tensor_tensor(top[:, :, :], top[:, :, :], dst_score[:, :, :], ALU.add))

                    def leaky(x):
                        mine.did(v.scalar_tensor_tensor(out=x, in0=x, scalar=SLOPE, in1=x, op0=ALU.mult, op1=ALU.max))

                    leaky(z[:, :, :])
                    leaky(old[:, :])
                    mine.settle()
                    leaky(top[:, :, :])
                    mine.settle()
                    mine.did(v.tensor_tensor(z[:, :, :], z[:, :, :], top[:, :, :], ALU.subtract))
                    mine.did(v.tensor_tensor(old[:, :], old[:, :], top[0:1, :, 0], ALU.subtract))
                    mine.settle()
                    mine.then(v.tensor_scalar(old[:, :], old[:, :], 0.0, None, ALU.min))
                    dve.sem_inc(exponents_ready, 1)
                    dve.wait_ge(weights_copied, group + 1)

                    def add_runs(q, runs):
                        for n in runs:
                            if n == 0:
                                dve.wait_ge(summed, group * ROWS + (2 * ROWS + q + 1))
                            dve.wait_ge(added, (group * ROWS + (SLOTS + q)) * subs + (n + 1 - lanes))
                            lane = slice(n % lanes * heads, (n % lanes + 1) * heads)
                            to = acc[:, lane, bass.ds(at[q * subs + n], run)]
                            v.tensor_tensor(to, to, ps_sum[q % SLOTS][0:LOADS, 0:heads * P].rearrange(
                                "p (h c) -> p h c", h=heads)[:, :, n * run:(n + 1) * run], ALU.add
                                ).then_inc(added, 1)

                    for r in range(ROWS + 2):
                        if r < ROWS:
                            if r * subs % REG_BATCH == 0:
                                _, batch = nc.values_load_multi_w_load_instructions(
                                    keep["window"][0:1, bass.ds((group * ROWS + r) * subs, REG_BATCH)],
                                    engines=[mybir.EngineType.DVE], min_val=0, max_val=WIDTH - P,
                                    skip_runtime_bounds_check_because="nodes are below NODES")
                                at = {} if r == 0 else at
                                at |= {r * subs + n: x for n, x in enumerate(batch)}
                            if r == 0:
                                first_col = acc[:, :, bass.ds(at[0], 1)]
                                factors = ps_factor.unsqueeze(2)
                                if lanes > 1:
                                    factors = factors.to_broadcast([LOADS, lanes, 1])
                                mine.then(v.tensor_tensor(first_col, first_col, factors, ALU.mult))
                        if r >= 2:
                            add_runs(r - 2, range(subs // 2))
                        if r < ROWS:
                            for h in range(heads):
                                t = v.tensor_scalar(onehot[:, r % SLOTS, h, :], keep["lane"][:, :],
                                                    places_now[:, r:r + 1], weights_now[:, h, r:r + 1],
                                                    ALU.is_equal, ALU.mult)
                            t.then_inc(onehot_ready, 1)
                        if r >= 2:
                            add_runs(r - 2, range(subs // 2, subs))
                    assert mine.n == steps, mine.n


TURN = 5
SLOT_OF = (0, 1, 2, 0, 1)
assert CHUNKS % TURN == 0


def wait_past(eng, sem, value):
    if not isinstance(value, int) or value > 0:
        eng.wait_ge(sem, value)


def each_turn(eng, step):
    for j in range(TURN):
        step(j, 0, j)
    with eng.Fori(1, CHUNKS // TURN) as k:
        for j in range(TURN):
            step(k * TURN + j, k, j)


def chunks_in_slot_before(k, j):
    return SLOT_OF.count(SLOT_OF[j]) * k + SLOT_OF[:j].count(SLOT_OF[j])


def update_nodes(nc, dram, keep, acc):
    with ExitStack() as stack:
        m = Mem(nc, stack, "update")
        turn, slot_of, slots, turns = TURN, SLOT_OF, max(SLOT_OF) + 1, CHUNKS // TURN
        size = CHUNK * P
        spread = m.sbuf("spread", [P, HEADS1 * WIDTH // P])
        inverse = m.sbuf("inverse", [P, turn, size])
        mean = m.sbuf("mean", [P, slots, size])
        above = m.sbuf("above", [P, slots, size])
        below = m.sbuf("below", [P, slots, size])
        g = m.sbuf("g", [P, slots, size])
        rows = m.sbuf("rows", [P, slots, CHUNK, ROW2])
        ps_sums = [m.psum(f"ps_sums{s}", [P, size]) for s in range(slots)]
        ps_rows = [m.psum(f"ps_rows{s}", [P, CHUNK, P]) for s in range(slots)]

        spread_in = m.sem("spread_in")
        first_keys_in = m.sem("first_keys_in")
        eps_added = m.sem("eps_added")
        inverted = m.sem("inverted")
        spread_out = m.sem("spread_out")
        pool_passed = m.sem("pool_passed")
        inverses_in = [m.sem(f"inverses_in{j}") for j in range(turn)]
        sums_ready = m.sem("sums_ready")
        divided = m.sem("divided")
        below_ready = m.sem("below_ready")
        parts_ready = m.sem("parts_ready")
        g_ready = m.sem("g_ready")
        rows_ready = m.sem("rows_ready")
        rows_copied = m.sem("rows_copied")
        ones_set = m.sem("ones_set")
        stored = [m.sem(f"stored{s}") for s in range(slots)]
        block = stack.enter_context(nc.Block())

        @block.gpsimd
        def _(pool):
            def step(i, k, j):
                if not (isinstance(i, int) and i < turn):
                    wait_alone(pool, divided, i - (turn - 1), pool_passed)
                for h in range(HEADS1):
                    pool.dma_start(inverse[h * D:(h + 1) * D, j, :],
                                   dram["inverses"][h:h + 1, bass.ds(i * size, size)].to_broadcast([D, size])
                                   ).then_inc(inverses_in[j], 16)

            pool.wait_ge(spread_out, 16)
            each_turn(pool, step)
            for g in range(FIRST_GROUPS):
                for n in range(SUBS):
                    nc.gpsimd.indirect_dma_start(
                        keep["first_keys"][:, g, n, :], None, dram["quarter_keys"],
                        bass.IndirectOffsetOnAxis(ap=keep["chosen"][:, g * SUBS + n:g * SUBS + n + 1], axis=0)
                        ).then_inc(first_keys_in, 16)
            pool.wait_ge(first_keys_in, 16 * FIRST_GROUPS * SUBS)

        @block.tensor
        def _(pe):
            def rows_of(i, j):
                slot = slot_of[j]
                pe.wait_ge(g_ready, i + 1)
                wait_past(pe, rows_copied, i - 1)
                for b in range(CHUNK):
                    t = nc.tensor.matmul(ps_rows[slot][:, b, 0:ROW2], g[:, slot, b * P:(b + 1) * P],
                                         keep["w2ext"][:, :], start=True, stop=True)
                t.then_inc(rows_ready, 1)

            def step(i, k, j):
                wait_past(pe, divided, i - 1)
                for h in range(HEADS1):
                    t = nc.tensor.matmul(ps_sums[slot_of[j]][:, :], keep["w1z"][:, h, :],
                                         acc[:, h, bass.ds(i * size, size)],
                                         start=(h == 0), stop=(h == HEADS1 - 1))
                t.then_inc(sums_ready, 1)
                if not (isinstance(i, int) and i < 2):
                    rows_of(i - 2, (j - 2) % turn)

            each_turn(pe, step)
            rows_of(CHUNKS - 2, turn - 2)
            rows_of(CHUNKS - 1, turn - 1)

        @block.vector
        def _(dve):
            v = nc.vector
            v.memset(rows[:, :, :, D:D + 1], 1.0).then_inc(ones_set, 1)
            dve.wait_ge(spread_in, 16)
            v.tensor_scalar(spread[:, :], spread[:, :], EPS, None, ALU.add).then_inc(eps_added, 1)
            dve.wait_ge(eps_added, 1)
            v.reciprocal(spread[:, :], spread[:, :]).then_inc(inverted, 1)

            def elu(i, j):
                slot = slot_of[j]
                dve.wait_ge(parts_ready, i + 1)
                wait_past(dve, rows_ready, i - 1)
                v.scalar_tensor_tensor(out=g[:, slot, :], in0=below[:, slot, :], scalar=-1.0, in1=above[:, slot, :],
                                       op0=ALU.add, op1=ALU.add).then_inc(g_ready, 1)

            def step(i, k, j):
                slot = slot_of[j]
                dve.wait_ge(inverses_in[j], k * (16 * HEADS1) + 16 * HEADS1)
                dve.wait_ge(sums_ready, i + 1)
                v.tensor_tensor(mean[:, slot, :], ps_sums[slot][:, :], inverse[:, j, :], ALU.mult
                                ).then_inc(divided, 1)
                if not (isinstance(i, int) and i < 1):
                    elu(i - 1, (j - 1) % turn)
                dve.wait_ge(divided, i + 1)
                v.tensor_scalar(below[:, slot, :], mean[:, slot, :], keep["b1"][:, 0:1], 0.0, ALU.add, ALU.min
                                ).then_inc(below_ready, 1)

            each_turn(dve, step)
            elu(CHUNKS - 1, turn - 1)

        @block.scalar
        def _(act):
            def copy_rows(i, k, j):
                slot = slot_of[j]
                act.wait_ge(rows_ready, i + 1)
                wait_past(act, stored[slot], 16 * chunks_in_slot_before(k, j))
                nc.scalar.copy(rows[:, slot, :, 0:D], ps_rows[slot][:, :, 0:D])
                nc.scalar.copy(rows[:, slot, :, LOADS:ROW2], ps_rows[slot][:, :, LOADS:ROW2]
                               ).then_inc(rows_copied, 1)

            def step(i, k, j):
                slot = slot_of[j]
                act.wait_ge(below_ready, i + 1)
                nc.scalar.activation(above[:, slot, :], mean[:, slot, :], ACT.Relu, bias=keep["b1"][:, 0:1])
                nc.scalar.activation(below[:, slot, :], below[:, slot, :], ACT.Exp).then_inc(parts_ready, 1)
                if not (isinstance(i, int) and i < 2):
                    copy_rows(i - 2, k - 1 if j < 2 else k, (j - 2) % turn)

            act.wait_ge(ones_set, 1)
            each_turn(act, step)
            copy_rows(CHUNKS - 2, turns - 1, turn - 2)
            copy_rows(CHUNKS - 1, turns - 1, turn - 1)

        @block.sync
        def _(sp):
            weights_row = acc[D:D + 1, :, :].rearrange("o h n -> o (h n)").rearrange("o (p c) -> o p c", p=P)
            sp.dma_start(spread[:, :], weights_row).then_inc(spread_in, 16)
            sp.wait_ge(inverted, 1)
            sp.dma_start(dram["inverses"].rearrange("h n -> (h n)").rearrange("(p c) -> p c", p=P), spread[:, :]
                         ).then_inc(spread_out, 16)
            table = dram["table2"].rearrange("(n b p) c -> p n b c", b=CHUNK, p=P)

            def step(i, k, j):
                sp.wait_ge(rows_copied, i + 1)
                sp.dma_start(table[:, bass.ds(i, 1)].rearrange("p o b c -> p (o b) c"), rows[:, slot_of[j], :, :]
                             ).then_inc(stored[slot_of[j]], 16)

            each_turn(sp, step)
            for s in range(slots):
                sp.wait_ge(stored[s], 16 * turns * slot_of.count(s))


def finish_nodes(nc, dram, keep, acc):
    with ExitStack() as stack:
        m = Mem(nc, stack, "finish")
        slots = max(SLOT_OF) + 1
        part = m.sbuf("part", [LOADS, slots, CHUNK * P])
        weights = m.sbuf("weights", [P, slots, CHUNK])
        mean = m.sbuf("mean", [P, slots, CHUNK, D])
        rows = m.sbuf("rows", [P, slots, CHUNK, D])
        turned = [m.psum(f"turned{s}", [P, CHUNK, P]) for s in range(slots)]

        part_ready = m.sem("part_ready")
        part_turned = m.sem("part_turned")
        eps_added = m.sem("eps_added")
        inverted = m.sem("inverted")
        divided = m.sem("divided")
        rows_ready = m.sem("rows_ready")
        pe_passed = m.sem("pe_passed")
        pool_passed = m.sem("pool_passed")
        stored = [m.sem(f"stored{s}") for s in range(slots)]
        block = stack.enter_context(nc.Block())

        @block.gpsimd
        def _(pool):
            def step(i, k, j):
                if not isinstance(i, int):
                    wait_alone(pool, part_turned, i - 1, pool_passed)
                elif i >= 2:
                    pool.wait_ge(part_turned, i - 1)
                cols = bass.ds(i * (CHUNK * P), CHUNK * P)
                nc.gpsimd.tensor_tensor(part[:, SLOT_OF[j], :], acc[:, 0, cols], acc[:, 1, cols], ALU.add
                                        ).then_inc(part_ready, 1)

            each_turn(pool, step)

        @block.tensor
        def _(pe):
            def step(i, k, j):
                if isinstance(i, int):
                    wait_past(pe, divided, i - 1)
                    pe.wait_ge(part_ready, i + 1)
                else:
                    wait_alone(pe, divided, i - 1, pe_passed)
                    wait_alone(pe, part_ready, i + 1, pe_passed)
                slot = SLOT_OF[j]
                for b in range(CHUNK):
                    t = nc.tensor.transpose(turned[slot][:, b, 0:LOADS], part[:, slot, b * P:(b + 1) * P],
                                            keep["ident"][0:LOADS, 0:LOADS])
                t.then_inc(part_turned, 1)

            each_turn(pe, step)

        @block.vector
        def _(dve):
            v = nc.vector

            def biased(i, k, j):
                slot = SLOT_OF[j]
                dve.wait_ge(divided, i + 1)
                wait_past(dve, stored[slot], 16 * chunks_in_slot_before(k, j))
                v.tensor_tensor(rows[:, slot], mean[:, slot],
                                keep["b2"][:, :].unsqueeze(1).to_broadcast([P, CHUNK, D]), ALU.add
                                ).then_inc(rows_ready, 1)

            def step(i, k, j):
                slot = SLOT_OF[j]
                dve.wait_ge(part_turned, i + 1)
                v.tensor_scalar(weights[:, slot, :], turned[slot][:, :, D], EPS, None, ALU.add).then_inc(eps_added, 1)
                if not (isinstance(i, int) and i < 1):
                    biased(i - 1, k - 1 if j < 1 else k, (j - 1) % TURN)
                dve.wait_ge(eps_added, i + 1)
                v.reciprocal(weights[:, slot, :], weights[:, slot, :]).then_inc(inverted, 1)
                dve.wait_ge(inverted, i + 1)
                v.tensor_tensor(mean[:, slot], turned[slot][:, :, 0:D],
                                weights[:, slot, :].unsqueeze(2).to_broadcast([P, CHUNK, D]), ALU.mult
                                ).then_inc(divided, 1)

            each_turn(dve, step)
            biased(CHUNKS - 1, CHUNKS // TURN - 1, TURN - 1)

        @block.sync
        def _(sp):
            nodes = dram["nodes"].rearrange("(n b p) c -> p n b c", b=CHUNK, p=P)

            def step(i, k, j):
                sp.wait_ge(rows_ready, i + 1)
                sp.dma_start(nodes[:, bass.ds(i, 1)].rearrange("p o b c -> p (o b) c"), rows[:, SLOT_OF[j]]
                             ).then_inc(stored[SLOT_OF[j]], 16)

            each_turn(sp, step)
            for s in range(slots):
                sp.wait_ge(stored[s], 16 * SLOT_OF.count(s) * (CHUNKS // TURN))


def dense_layer(nc, dram, keep, out):
    with ExitStack() as stack:
        m = Mem(nc, stack, "dense")
        tiles = BATCH // P
        parts = CTX + 1
        deep = parts * D // P
        cols = 500
        pieces = 5
        span = cols * pieces
        spans = NODES // span
        per_span = tiles * pieces
        ring = 4
        raw = m.sbuf("raw", [P, deep, span])
        w_high = m.sbuf("w_high", [P, 2, deep, span], F32R)
        w_low = m.sbuf("w_low", [P, 2, deep, span], F32R)
        fc_b = m.sbuf("fc_b", [P, 2, span])
        x_high = m.sbuf("x_high", [P, deep, BATCH], F32R)
        x_low = m.sbuf("x_low", [P, deep, BATCH], F32R)
        results = m.sbuf("results", [P, ring, span])
        idx = m.sbuf("idx", [P, tiles * parts], I32)
        place = m.sbuf("place", [P, tiles * parts])
        below = m.sbuf("below", [P, tiles * parts])
        gathered = m.sbuf("gathered", [P, 2, parts * D])
        turned = [m.psum(f"turned{s}", [P, 2 * deep, P]) for s in range(2)]
        ps = [m.psum(f"ps{s}", [P, 512]) for s in range(pieces)]

        piece_in = [m.sem(f"piece_in{s}") for s in range(pieces)]
        span_in = m.sem("span_in")
        bias_in = [m.sem("bias_in_even"), m.sem("bias_in_odd")]
        idx_in = m.sem("idx_in")
        step = m.sem("step")
        idx_ready = m.sem("idx_ready")
        landed = [m.sem("landed_even"), m.sem("landed_odd")]
        x_turned = m.sem("x_turned")
        x_high_ready = m.sem("x_high_ready")
        x_split = m.sem("x_split")
        w_high_ready = m.sem("w_high_ready")
        w_split = m.sem("w_split")
        product = m.sem("product")
        biased = m.sem("biased")
        stored = [m.sem(f"stored{s}") for s in range(ring)]
        block = stack.enter_context(nc.Block())
        out_v = out.rearrange("(p t) c -> p t c", t=tiles)
        w_v = dram["fc_w"].rearrange("(k p) n -> p k n", p=P)

        def piece(s):
            return slice(s * cols, (s + 1) * cols)

        @block.sync
        def _(sp):
            sp.dma_start(idx[:, 0:tiles], dram["user_idx"].rearrange("(p t) -> p t", p=P)).then_inc(idx_in, 16)
            sp.dma_start(idx[:, tiles:], dram["ctx_idx"].rearrange("(p t) c -> p (t c)", p=P)).then_inc(idx_in, 16)
            for s in range(pieces):
                sp.dma_start(raw[:, :, piece(s)], w_v[:, :, piece(s)]).then_inc(piece_in[s], 16)
            with sp.Fori(0, spans) as c:
                for t in range(tiles):
                    sp.wait_ge(biased, c * per_span + (t + 1) * pieces)
                    sp.dma_start(out_v[:, t, bass.ds(c * span, span)], results[:, t % ring, :]
                                 ).then_inc(stored[t % ring], 16)
            for s in range(ring):
                sp.wait_ge(stored[s], 16 * spans * tiles // ring)

        @block.scalar
        def _(act):
            def load_bias(c, slot):
                act.dma_start(fc_b[:, slot, :], dram["fc_b"].rearrange("(o n) -> o n", o=1)[:, bass.ds(c * span, span)]
                              .to_broadcast([P, span])).then_inc(bias_in[slot], 16)

            def load_span(c):
                act.wait_ge(w_split, c * pieces)
                act.dma_start(raw[:, :, :], w_v[:, :, bass.ds(c * span, span)]).then_inc(span_in, 16)

            def high_parts(slot, pieces_now=range(pieces)):
                for s in pieces_now:
                    nc.scalar.copy(w_high[:, slot, :, piece(s)], raw[:, :, piece(s)]).then_inc(w_high_ready, 1)

            def next_span(c, slot, last=False):
                act.wait_ge(biased, (c - 1) * per_span)
                load_bias(c, slot)
                act.wait_ge(span_in, 16 * c)
                high_parts(slot)
                if not last:
                    load_span(c + 1)

            load_bias(0, 0)
            for s in range(pieces):
                act.wait_ge(piece_in[s], 16)
                high_parts(0, [s])
            load_span(1)
            load_bias(1, 1)
            for t in range(tiles):
                if t == tiles // 2:
                    act.wait_ge(span_in, 16)
                    high_parts(1)
                act.wait_ge(x_turned, t + 1)
                nc.scalar.copy(x_high[:, :, t * P:(t + 1) * P], turned[t % 2][:, 0:deep]).then_inc(x_high_ready, 1)
            load_span(2)
            with act.Fori(0, (spans - 3) // 2) as i:
                next_span(2 * i + 2, 0)
                next_span(2 * i + 3, 1)
            next_span(spans - 1, 0, last=True)

        @block.vector
        def _(dve):
            v = nc.vector
            mine = Steps(dve, step)
            dve.wait_ge(idx_in, 32)
            clamp_indices(v, mine, idx, place, below)
            v.tensor_copy(idx[:, :], place[:, :]).then_inc(idx_ready, 1)

            def low_part(c, slot, s):
                dve.wait_ge(w_high_ready, c * pieces + (s + 1))
                v.tensor_tensor(w_low[:, slot, :, piece(s)], raw[:, :, piece(s)],
                                w_high[:, slot, :, piece(s)].bitcast(F32), ALU.subtract).then_inc(w_split, 1)

            def split_x(t):
                dve.wait_ge(x_high_ready, t + 1)
                v.tensor_tensor(x_low[:, :, t * P:(t + 1) * P], turned[t % 2][:, 0:deep],
                                x_high[:, :, t * P:(t + 1) * P].bitcast(F32), ALU.subtract).then_inc(x_split, 1)

            def add_bias(c, slot, first=False, last=False):
                dve.wait_ge(bias_in[slot], 8 * (c - slot) + 16)
                for t in range(tiles):
                    if first and t + 1 < tiles:
                        split_x(t + 1)
                    for s in range(pieces):
                        dve.wait_ge(product, c * per_span + (t * pieces + s + 1))
                        if s == 0 and not (first and t < ring):
                            dve.wait_ge(stored[t % ring], 16 * (c * (tiles // ring) + t // ring))
                        v.tensor_tensor(results[:, t % ring, piece(s)], ps[s][:, 0:cols], fc_b[:, slot, piece(s)],
                                        ALU.add).then_inc(biased, 1)
                    if not last and t >= tiles - pieces - 1 and t < tiles - 1:
                        low_part(c + 1, 1 - slot, t - (tiles - pieces - 1))

            for s in range(pieces):
                low_part(0, 0, s)
            split_x(0)
            add_bias(0, 0, first=True)
            with dve.Fori(0, (spans - 3) // 2) as i:
                add_bias(2 * i + 1, 1)
                add_bias(2 * i + 2, 0)
            add_bias(spans - 2, 1)
            add_bias(spans - 1, 0, last=True)

        @block.gpsimd
        def _(pool):
            pool.wait_ge(idx_ready, 1)
            for t in range(tiles):
                if t >= 2:
                    pool.wait_ge(x_turned, t - 1)
                for c in range(parts):
                    col = tiles + t * CTX + c - 1 if c else t
                    nc.gpsimd.indirect_dma_start(
                        gathered[:, t % 2, c * D:(c + 1) * D], None, dram["user"] if c == 0 else dram["nodes"],
                        bass.IndirectOffsetOnAxis(ap=idx[:, col:col + 1], axis=0)).then_inc(landed[t % 2], 16)

        @block.tensor
        def _(pe):
            def turn_x(t):
                pe.wait_ge(landed[t % 2], 16 * parts * (t // 2 + 1))
                if t >= 2:
                    pe.wait_ge(x_split, t - 1)
                for k in range(deep):
                    q = nc.tensor.transpose(turned[t % 2][:, k, :], gathered[:, t % 2, k * P:(k + 1) * P],
                                            keep["ident"][:, :])
                q.then_inc(x_turned, 1)

            def products(c, slot, first=False):
                if not first:
                    pe.wait_ge(w_split, (c + 1) * pieces)
                for t in range(tiles):
                    if first:
                        if t + 1 < tiles:
                            turn_x(t + 1)
                        pe.wait_ge(x_split, t + 1)
                    for s in range(pieces):
                        if first and t == 0:
                            pe.wait_ge(w_split, s + 1)
                        if not (first and t == 0):
                            pe.wait_ge(biased, c * per_span + ((t - 1) * pieces + s + 1))
                        own = slice(t * P, (t + 1) * P)
                        terms = [(a, b, k) for k in range(deep)
                                 for a, b in ((x_low, w_high), (x_high, w_low), (x_high, w_high))]
                        for n, (a, b, k) in enumerate(terms):
                            q = nc.tensor.matmul(ps[s][:, 0:cols], a[:, k, own], b[:, slot, k, piece(s)],
                                                 start=(n == 0), stop=(n == len(terms) - 1))
                        q.then_inc(product, 1)

            turn_x(0)
            products(0, 0, first=True)
            with pe.Fori(0, (spans - 3) // 2) as i:
                products(2 * i + 1, 1)
                products(2 * i + 2, 0)
            products(spans - 2, 1)
            products(spans - 1, 0)


INPUTS = ["r_user_idx", "r_context_idx", "L0_rec_edge_index", "L0_rec_user_emb", "L0_rec_service_emb",
          "L0_rec_W1", "L0_rec_att_src1", "L0_rec_att_dst1", "L0_rec_b1", "L0_rec_W2", "L0_rec_att_src2",
          "L0_rec_att_dst2", "L0_rec_b2", "L0_rec_fc_w", "L0_rec_fc_b"]
SHAPES = {"r_user_idx": ([BATCH], I32), "r_context_idx": ([BATCH, CTX], I32), "L0_rec_edge_index": ([2, EDGES], I32),
          "L0_rec_user_emb": ([NODES, D], F32), "L0_rec_service_emb": ([NODES, D], F32),
          "L0_rec_W1": ([D, 2 * D], F32), "L0_rec_att_src1": ([2, D], F32), "L0_rec_att_dst1": ([2, D], F32),
          "L0_rec_b1": ([2 * D], F32), "L0_rec_W2": ([2 * D, D], F32), "L0_rec_att_src2": ([1, D], F32),
          "L0_rec_att_dst2": ([1, D], F32), "L0_rec_b2": ([D], F32), "L0_rec_fc_w": ([4 * D, NODES], F32),
          "L0_rec_fc_b": ([NODES], F32)}


def declare(nc):
    def inp(n):
        return nc.dram_tensor(f"in_{n}", SHAPES[n][0], SHAPES[n][1], kind="ExternalInput").ap()
    a = {n: inp(n) for n in INPUTS}
    d = {"edges": a["L0_rec_edge_index"], "W1": a["L0_rec_W1"], "W2": a["L0_rec_W2"], "b1": a["L0_rec_b1"],
         "b2": a["L0_rec_b2"], "att_src1": a["L0_rec_att_src1"], "att_dst1": a["L0_rec_att_dst1"],
         "att_src2": a["L0_rec_att_src2"], "att_dst2": a["L0_rec_att_dst2"], "service": a["L0_rec_service_emb"],
         "user": a["L0_rec_user_emb"], "fc_w": a["L0_rec_fc_w"], "fc_b": a["L0_rec_fc_b"],
         "user_idx": a["r_user_idx"], "ctx_idx": a["r_context_idx"]}
    d["out"] = nc.dram_tensor("out", [BATCH, NODES], F32, kind="ExternalOutput").ap()
    for name, shape, dt in (("keys", [1 + P * COLS], I32), ("window", [1, QUARTERS], I32),
                            ("quarter_keys", [QUARTERS + 1, QUARTER + 2], I32), ("needed", [NEED_HIGH * P, 2], F32),
                            ("table1", [NODES, ROW1], F32),
                            ("inverses", [HEADS1, WIDTH], F32), ("table2", [WIDTH, ROW2], F32), ("nodes", [WIDTH, D], F32)):
        d[name] = nc.dram_tensor(name, shape, dt, kind="Internal").ap()
    return d


def program(nc, dram):
    with ExitStack() as stack:
        m = Mem(nc, stack, "all")
        keep = {
            "ident": m.sbuf("ident", [P, P]), "lane": m.sbuf("lane", [P, P]), "ones": m.sbuf("ones", [P, P]),
            "before": m.sbuf("before", [P, P]),
            "w1z": m.sbuf("w1z", [LOADS, HEADS1, P]),
            "w2ext": m.sbuf("w2ext", [P, ROW2]), "b1": m.sbuf("b1", [P, 1]), "b2": m.sbuf("b2", [P, D]),
        }
        with ExitStack() as graph:
            m = Mem(nc, graph, "graph")
            keep |= {
                "rows": m.sbuf("rows", [P, TILES], I32),
                "places": m.sbuf("places", [P, TILES]),
                "chosen": m.sbuf("chosen", [ROWS, GROUPS * SUBS], I32),
                "chosen_groups": m.sbuf("chosen_groups", [1, 1], I32),
                "starts": m.sbuf("starts", [ROWS, GROUPS, P], BF16),
                "ends": m.sbuf("ends", [ROWS, GROUPS, P], BF16),
                "others": m.sbuf("others", [ROWS, GROUPS, P], BF16),
            }
            keep["first_keys"] = keep["rows"][0:ROWS, 0:FIRST_GROUPS * SUBS * (QUARTER + 2)].rearrange(
                "r (g s e) -> r g s e", g=FIRST_GROUPS, s=SUBS)
            weights_and_sort(nc, dram, keep)
            with ExitStack() as one:
                m = Mem(nc, one, "graph1")
                keep["window"] = m.sbuf("window", [1, TILES], I32)
                keep["found"] = m.sbuf("found", [P, QUARTERS // P + 1, 2])
                index_tiles(nc, dram, keep, "index1")
                acc = m.sbuf("acc", [LOADS, HEADS1, WIDTH])
                sum_messages(nc, dram["table1"], keep, acc, HEADS1, "layer1", meanwhile=choose_tiles)
                update_nodes(nc, dram, keep, acc)
            m = Mem(nc, graph, "graph2")
            keep["window"] = m.sbuf("window", [1, QUARTERS], I32)
            index_tiles(nc, dram, keep, "index2", keep["chosen"], keep["chosen_groups"][0:1, 0:1])
            acc = m.sbuf("acc", [LOADS, 2 * HEADS2, WIDTH])
            sum_messages(nc, dram["table2"], keep, acc, HEADS2, "layer2", SUBS, keep["chosen_groups"][0:1, 0:1])
            finish_nodes(nc, dram, keep, acc)
        dense_layer(nc, dram, keep, dram["out"])


def kernel(**inputs):
    import concourse.bacc as bacc
    from concourse.bass_utils import run_bass_kernel_spmd

    nc = bacc.Bacc("TRN2", target_bir_lowering=False, num_devices=1)
    program(nc, declare(nc))
    arrays = {f"in_{name}": np.ascontiguousarray(inputs[name]) for name in INPUTS}
    return run_bass_kernel_spmd(nc, [arrays], core_ids=[0]).results[0]["out"]
```
